# Optimizing a Trainium2 kernel written in Bass

```python
import numpy as np
import jax
import jax.numpy as jnp

def _softmax(x, axis=-1):
    return jax.nn.softmax(x, axis=axis)

def _gelu(x):
    return jax.nn.gelu(x, approximate=True)

def _silu(x):
    return jax.nn.silu(x)

def _sigmoid(x):
    return jax.nn.sigmoid(x)

def _layernorm(x, axis=-1, eps=1e-05):
    m = jnp.mean(x, axis=axis, keepdims=True)
    v = jnp.var(x, axis=axis, keepdims=True)
    return (x - m) / jnp.sqrt(v + eps)

def _scatter_add(tgt, idx, src, axis=0):
    return tgt.at[idx].add(src)

def _segment_sum(src, seg, n):
    return jax.ops.segment_sum(src, seg, n)
kernel_name = 'mk_cond_seq_d1_seqx_r2_ddeab8'

def setup_inputs(seed: int=0):
    np.random.seed(seed)
    _w = jnp.asarray

    def _rec_inputs():
        import jax
        import jax.numpy as jnp
        _rk = jax.random.key(seed)
        x = 1.648e-05 + 1 * jax.random.normal(jax.random.fold_in(_rk, 1), (32, 128, 576), jnp.float32)
        _lenS = 128 - jax.random.randint(jax.random.fold_in(_rk, 7), (32,), 0, max(1, 128 // 4) + 1, jnp.int32)
        _lenS2 = 128 - jax.random.randint(jax.random.fold_in(_rk, 8), (32,), 0, max(1, 128 // 4) + 1, jnp.int32)
        cond_1152 = 0.00914911 + 1.00357 * jax.random.normal(jax.random.fold_in(_rk, 11), (32, 576), jnp.float32)
        return (x, cond_1152)
    x, cond_1152 = _rec_inputs()

    def _L0_cond_setup():
        import jax, jax.numpy as jnp
        import numpy as np
        DIM = 576
        HEADS = 16
        HEAD_DIM = DIM // HEADS
        HIDDEN = int(DIM * 4.0)
        EPS = 1e-12

        def rmsnorm(x, g, d):
            n = jnp.linalg.norm(x, axis=-1, keepdims=True)
            return x / jnp.maximum(n, EPS) * d ** 0.5 * g

        def modulate(x, scale, shift):
            return x * (1.0 + scale[:, None, :]) + shift[:, None, :]
        key = jax.random.key(seed)
        ks = jax.random.split(key, 12)
        B, N = (8, 512)
        s = 0.02
        return {'x': jax.random.normal(ks[0], (B, N, DIM), jnp.float32), 'c': jax.random.normal(ks[1], (B, DIM), jnp.float32), 'g1': jnp.ones((1,), jnp.float32), 'g2': jnp.ones((1,), jnp.float32), 'qkv_w': jax.random.normal(ks[2], (3 * DIM, DIM), jnp.float32) * s, 'qkv_b': jnp.zeros((3 * DIM,), jnp.float32), 'qg': jnp.ones((1,), jnp.float32), 'kg': jnp.ones((1,), jnp.float32), 'proj_w': jax.random.normal(ks[3], (DIM, DIM), jnp.float32) * s, 'proj_b': jnp.zeros((DIM,), jnp.float32), 'fc1_w': jax.random.normal(ks[4], (HIDDEN, DIM), jnp.float32) * s, 'fc1_b': jnp.zeros((HIDDEN,), jnp.float32), 'fc2_w': jax.random.normal(ks[5], (DIM, HIDDEN), jnp.float32) * s, 'fc2_b': jnp.zeros((DIM,), jnp.float32), 'ada_w': jax.random.normal(ks[6], (6 * DIM, DIM), jnp.float32) * s, 'ada_b': jnp.zeros((6 * DIM,), jnp.float32)}
    _L0_cond_all = _L0_cond_setup()
    _L0_cond_in = {k: v for k, v in _L0_cond_all.items() if k in ('g1', 'g2', 'qkv_w', 'qkv_b', 'qg', 'kg', 'proj_w', 'proj_b', 'fc1_w', 'fc1_b', 'fc2_w', 'fc2_b', 'ada_w', 'ada_b')}
    del _L0_cond_all
    return {'x': x, 'cond_1152': cond_1152, 'L0_cond_g1': _L0_cond_in['g1'], 'L0_cond_g2': _L0_cond_in['g2'], 'L0_cond_qkv_w': _L0_cond_in['qkv_w'], 'L0_cond_qkv_b': _L0_cond_in['qkv_b'], 'L0_cond_qg': _L0_cond_in['qg'], 'L0_cond_kg': _L0_cond_in['kg'], 'L0_cond_proj_w': _L0_cond_in['proj_w'], 'L0_cond_proj_b': _L0_cond_in['proj_b'], 'L0_cond_fc1_w': _L0_cond_in['fc1_w'], 'L0_cond_fc1_b': _L0_cond_in['fc1_b'], 'L0_cond_fc2_w': _L0_cond_in['fc2_w'], 'L0_cond_fc2_b': _L0_cond_in['fc2_b'], 'L0_cond_ada_w': _L0_cond_in['ada_w'], 'L0_cond_ada_b': _L0_cond_in['ada_b']}

def reference(x, cond_1152, L0_cond_g1, L0_cond_g2, L0_cond_qkv_w, L0_cond_qkv_b, L0_cond_qg, L0_cond_kg, L0_cond_proj_w, L0_cond_proj_b, L0_cond_fc1_w, L0_cond_fc1_b, L0_cond_fc2_w, L0_cond_fc2_b, L0_cond_ada_w, L0_cond_ada_b):
    import jax
    import jax.numpy as jnp

    def _L0_cond_ref(x, c, g1, g2, qkv_w, qkv_b, qg, kg, proj_w, proj_b, fc1_w, fc1_b, fc2_w, fc2_b, ada_w, ada_b):
        import jax, jax.numpy as jnp
        import numpy as np
        DIM = 576
        HEADS = 16
        HEAD_DIM = DIM // HEADS
        HIDDEN = int(DIM * 4.0)
        EPS = 1e-12

        def rmsnorm(x, g, d):
            n = jnp.linalg.norm(x, axis=-1, keepdims=True)
            return x / jnp.maximum(n, EPS) * d ** 0.5 * g

        def modulate(x, scale, shift):
            return x * (1.0 + scale[:, None, :]) + shift[:, None, :]
        B, N, D = x.shape
        mod = jax.nn.silu(c) @ ada_w.T + ada_b
        shift_msa, scale_msa, gate_msa, shift_mlp, scale_mlp, gate_mlp = jnp.split(mod, 6, axis=-1)
        gate_msa = jnp.tanh(gate_msa)
        gate_mlp = jnp.tanh(gate_mlp)
        h = modulate(rmsnorm(x, g1, D), scale_msa, shift_msa)
        qkv = h @ qkv_w.T + qkv_b
        qkv = qkv.reshape(B, N, 3, HEADS, HEAD_DIM).transpose(2, 0, 3, 1, 4)
        q, k, v = (qkv[0], qkv[1], qkv[2])
        q = rmsnorm(q, qg, HEAD_DIM)
        k = rmsnorm(k, kg, HEAD_DIM)
        q = q * HEAD_DIM ** (-0.5)
        attn = jax.nn.softmax(jnp.einsum('bhqd,bhkd->bhqk', q, k), axis=-1)
        o = jnp.einsum('bhqk,bhkd->bhqd', attn, v)
        o = o.transpose(0, 2, 1, 3).reshape(B, N, D)
        o = o @ proj_w.T + proj_b
        x = x + gate_msa[:, None, :] * o
        h2 = modulate(rmsnorm(x, g2, D), scale_mlp, shift_mlp)
        m = jax.nn.gelu(h2 @ fc1_w.T + fc1_b, approximate=True) @ fc2_w.T + fc2_b
        x = x + gate_mlp[:, None, :] * m
        return x
    x = _L0_cond_ref(x, cond_1152, L0_cond_g1, L0_cond_g2, L0_cond_qkv_w, L0_cond_qkv_b, L0_cond_qg, L0_cond_kg, L0_cond_proj_w, L0_cond_proj_b, L0_cond_fc1_w, L0_cond_fc1_b, L0_cond_fc2_w, L0_cond_fc2_b, L0_cond_ada_w, L0_cond_ada_b)
    return x

_drawn_inputs = setup_inputs


def setup_inputs(seed=0):
    import zlib

    import numpy as np

    out = dict(_drawn_inputs(seed))
    spreads = {'L0_cond_qkv_b': (0.0, 0.574),
     'L0_cond_proj_b': (0.0, 0.285),
     'L0_cond_fc1_b': (0.0, 0.504),
     'L0_cond_fc2_b': (0.0, 0.286),
     'L0_cond_ada_b': (0.0, 0.1)}
    factors = {'L0_cond_qkv_w': 2.758}
    for name, (base, spread) in spreads.items():
        noise = np.random.default_rng([zlib.crc32(name.encode()), seed]).standard_normal(out[name].shape)
        drawn = base * np.exp(spread * noise) if base else spread * noise
        out[name] = jnp.asarray(drawn.astype(out[name].dtype))
    for name, factor in factors.items():
        out[name] = (out[name] * factor).astype(out[name].dtype)
    return out
```

```python
from contextlib import ExitStack

import concourse.bass as bass
from concourse import mybir

F32 = mybir.dt.float32
F32R = mybir.dt.float32r
ALU = mybir.AluOpType
ACT = mybir.ActivationFunctionType
AX_X = mybir.AxisListType.X

P = 128
B = 32
T = 128
D = 576
H = 16
HD = D // H
F = 4 * D
KF = D // P
TAIL = D - KF * P
KT = KF + 1
DX = KT * P
HG = 4
G = H // HG
GC = 3 * HG * HD
QK = 2 * HG * HD
NH = D // 2
ST = 3 * HD
VW = 2 * HD + 2
MT = F // P
PAIRS = B // 2
BANK = 512
EPS2 = 1e-24


def build(nc, x, cond_t, g1, g2, qkv_wt, qkv_b, qg, kg, proj_wt, proj_b,
          fc1_wt, fc1_bt, fc2_wt, fc2_b, ada_wt, ada_b, out):
    gate1_d = nc.dram_tensor("gate_msa_rows", [B, D], F32, kind="Internal").ap()
    gate2_d = nc.dram_tensor("gate_mlp_rows", [B, D], F32, kind="Internal").ap()
    gb2_d = nc.dram_tensor("gated_fc2_bias_rows", [B, D], F32, kind="Internal").ap()
    x1_d = nc.dram_tensor("x_after_attention", [B, T, D], F32, kind="Internal").ap()
    x1g_d = nc.dram_tensor("x_after_attention_biased", [B, T, D], F32, kind="Internal").ap()

    with ExitStack() as whole:
        def keep_sb(name, shape, dt):
            return whole.enter_context(nc.sbuf_tensor(name, shape, dt))

        coef = keep_sb("coef", [P, 4, KT, B], F32)
        ident = keep_sb("ident", [P, P], F32)
        minus_half = keep_sb("minus_half", [P, 2 * HG], F32)
        attention_stage(nc, x, cond_t, g1, g2, qkv_wt, qkv_b, qg, kg, proj_wt, proj_b, fc2_b, ada_wt, ada_b,
                        gate1_d, gate2_d, gb2_d, x1_d, x1g_d, coef, ident, minus_half)
        mlp_stage(nc, fc1_wt, fc1_bt, fc2_wt, gate2_d, x1_d, x1g_d, out, coef, ident, minus_half)


def attention_stage(nc, x, cond_t, g1, g2, qkv_wt, qkv_b, qg, kg, proj_wt, proj_b, fc2_b, ada_wt, ada_b,
                    gate1_d, gate2_d, gb2_d, x1_d, x1g_d, coef, ident, minus_half):
    with ExitStack() as ctx:
        def sb(name, shape, dt):
            return ctx.enter_context(nc.sbuf_tensor(name, shape, dt))

        def ps(name, shape):
            return ctx.enter_context(nc.psum_tensor(name, shape, F32))

        def sem(name):
            return ctx.enter_context(nc.semaphore(name))

        wq_hi = sb("wq_hi", [P, KF, 3 * D], F32R)
        wq_lo = sb("wq_lo", [P, KF, 3 * D], F32R)
        wq_x = sb("wq_x", [P, 3 * D], F32R)
        wq_y = sb("wq_y", [P, 3 * D], F32R)
        wp_hi = sb("wp_hi", [P, KF, D], F32R)
        wp_lo = sb("wp_lo", [P, KF, D], F32R)
        wp_x = sb("wp_x", [P, D], F32R)
        wp_y = sb("wp_y", [P, D], F32R)
        stage = sb("stage", [P, 2, 3 * D], F32)
        bias_stage = sb("bias_stage", [P, 3 * D], F32)
        ada = sb("ada", [P, 2, KT, D], F32)
        condt = sb("condt", [P, KT, B], F32)
        sigm = sb("sigm", [P, 2, KT, B], F32)
        silut = sb("silut", [P, KT, B], F32)
        modrow = sb("modrow", [B, 2, DX], F32)
        gains = sb("gains", [P, 4], F32)
        gscale = sb("gscale", [P, 2], F32)
        qk_gain = sb("qk_gain", [P, 2, HG], F32)
        ident_r = sb("ident_r", [P, P], F32R)

        xin = sb("xin", [P, D], F32)
        xsq = sb("xsq", [P, D], F32)
        xss = sb("xss", [P, 1], F32)
        xr = sb("xr", [P, 2], F32)
        xn = sb("xn", [P, DX], F32)
        h = sb("h", [P, DX], F32)
        h_hi = sb("h_hi", [P, DX], F32R)
        h_lo = sb("h_lo", [P, DX], F32R)
        o = sb("o", [P, DX], F32)
        ot_hi = sb("ot_hi", [P, DX], F32R)
        ot_lo = sb("ot_lo", [P, DX], F32R)
        xres = sb("xres", [P, D], F32)
        gate1 = sb("gate1", [P, D], F32)
        gb2_all = sb("gb2_all", [P, D], F32)
        gated = sb("gated", [P, D], F32)
        x1 = sb("x1", [P, D], F32)
        x1g = sb("x1g", [P, D], F32)
        gate_rows = (gated[0:B, :], x1[0:B, :])
        gb2_rows = x1g[0:B, :]
        fc2_b_rows = xres[0:B, :]

        sq = sb("sq", [P, QK], F32)
        ss = sb("ss", [P, 2 * HG], F32)
        ssg = sb("ssg", [P, 2 * HG], F32)
        rpow = sb("rpow", [P, 2 * HG], F32)
        rqk = sb("rqk", [P, 2 * HG], F32)
        qk = sb("qk", [P, 2, HG, HD], F32)
        stack = sb("stack", [P, 2 * HG * ST], F32R)
        v = sb("v", [P, G, HG, VW], F32R)
        qs = sb("qs", [P, HG * T], F32R)
        ks = sb("ks", [P, HG * T], F32R)
        mx = sb("mx", [P, HG], F32)
        pr = sb("pr", [P, HG * T], F32)
        pt_hi = sb("pt_hi", [P, HG * T], F32R)
        pt_lo = sb("pt_lo", [P, HG * T], F32R)
        olo = sb("olo", [P, HG, HD], F32)
        osum = sb("osum", [P, HG, HD], F32)
        rden = sb("rden", [P, HG], F32)

        q_ps = ps("q_ps", [P, 2, BANK])
        ts_ps = ps("ts_ps", [P, BANK])
        tk_ps = ps("tk_ps", [P, BANK])
        pt_ps = ps("pt_ps", [P, BANK])
        o_ps = ps("o_ps", [P, BANK])
        y_ps = ps("y_ps", [P, 2, BANK])
        y_flat = y_ps[:, :, :].rearrange("p a b -> p (a b)")
        y_half = y_ps[:, :, 0:NH]

        half = HG * ST

        def stacked(first):
            base = stack[:, first * HD:first * HD + HD]
            step = half + (HD if first == 1 else -HD if first == 2 else 0)
            return bass.AP(tensor=base.tensor, offset=base.offset,
                           ap=[base.ap[0], [step, 2], [ST, HG], [1, HD]])

        cond_in = sem("cond_in")
        gains_in = sem("gains_in")
        fc2_b_in = sem("fc2_b_in")
        ada_in = [sem(f"ada_in{i}") for i in range(2)]
        stage_in = [sem(f"stage_in{i}") for i in range(2)]
        x_in = sem("x_in")
        res_in = sem("res_in")
        gate_in = sem("gate_in")
        gates_out = sem("gates_out")
        x1_out = sem("x1_out")
        x1g_out = sem("x1g_out")
        bias_in = sem("bias_in")
        cond_padded = sem("cond_padded")
        bias_zeroed = sem("bias_zeroed")
        const_step = sem("const_step")
        constants = sem("constants")
        ident_zeroed = sem("ident_zeroed")
        ident_made = sem("ident_made")
        ident_r_made = sem("ident_r_made")
        gains_made = sem("gains_made")
        silu_step = sem("silu_step")
        silu_exp = sem("silu_exp")
        silu_made = sem("silu_made")
        ada_done = sem("ada_done")
        row_done = sem("row_done")
        coef_t = sem("coef_t")
        coef_made = sem("coef_made")
        tanh_done = sem("tanh_done")
        gb2_done = sem("gb2_done")
        w_hi_done = sem("w_hi_done")
        w_split = sem("w_split")
        x_squared = sem("x_squared")
        x_guarded = sem("x_guarded")
        x_rnorm = sem("x_rnorm")
        x_scaled = sem("x_scaled")
        x_t = sem("x_t")
        h_made = sem("h_made")
        h_hi_made = sem("h_hi_made")
        h_split = sem("h_split")
        qkv_done = sem("qkv_done")
        qk_squared = sem("qk_squared")
        qk_summed = sem("qk_summed")
        qk_guarded = sem("qk_guarded")
        qk_pow = sem("qk_pow")
        qk_rnorm = sem("qk_rnorm")
        qk_scaled = sem("qk_scaled")
        qk_hi = sem("qk_hi")
        qk_lo = sem("qk_lo")
        qk_dup = sem("qk_dup")
        v_hi_made = sem("v_hi_made")
        v_split = sem("v_split")
        stack_t = sem("stack_t")
        stack_read = sem("stack_read")
        scores_done = sem("scores_done")
        max_done = sem("max_done")
        shifted = sem("shifted")
        exp_done = sem("exp_done")
        probs_t = sem("probs_t")
        probs_hi = sem("probs_hi")
        probs_split = sem("probs_split")
        pv_done = sem("pv_done")
        olo_read = sem("olo_read")
        o_summed = sem("o_summed")
        o_normed = sem("o_normed")
        o_dup = sem("o_dup")
        o_t = sem("o_t")
        ot_hi_made = sem("ot_hi_made")
        ot_split = sem("ot_split")
        proj_done = sem("proj_done")
        gated_done = sem("gated_done")
        x1_done = sem("x1_done")
        x1g_done = sem("x1g_done")

        steps = [("block", qkv_wt, 3 * D, wq_hi[:, k, :], wq_lo[:, k, :], k) for k in range(KF)]
        steps += [("tail", qkv_wt, 3 * D, wq_x, wq_y, KF), ("bias", qkv_b, 3 * D, wq_x, wq_y, KF)]
        steps += [("block", proj_wt, D, wp_hi[:, k, :], wp_lo[:, k, :], k) for k in range(KF)]
        steps += [("tail", proj_wt, D, wp_x, wp_y, KF), ("bias", proj_b, D, wp_x, wp_y, KF)]
        QKV_STEPS = KF + 2

        def staged(n):
            kind, cols = steps[n][0], steps[n][2]
            if kind == "bias":
                return bias_stage[:, 0:cols], bias_in, 32 * (1 if n < QKV_STEPS else 2)
            in_ring = [i for i in range(n + 1) if steps[i][0] != "bias"]
            ring = (len(in_ring) - 1) % 2
            loads = sum(1 if steps[i][0] == "block" else 2 for i in in_ring[ring::2])
            return stage[:, ring, 0:cols], stage_in[ring], 16 * loads

        def stage_freed(n):
            if steps[n][0] == "bias":
                return 0 if n < QKV_STEPS else QKV_STEPS
            in_ring = [i for i in range(n) if steps[i][0] != "bias"]
            return in_ring[-2] + 1 if len(in_ring) >= 2 else 0

        def run_batches(eng, body):
            body(0, 0, False)
            body(1, 1, False)
            with eng.Fori(2, B - 1) as b:
                body(b, 2, False)
            body(B - 1, 2, True)

        block = ctx.enter_context(nc.Block())

        @block.sync
        def _(sp):
            def load_stage(n):
                kind, src, cols, _, _, k = steps[n]
                dst, landed, _ = staged(n)
                if stage_freed(n):
                    sp.wait_ge(w_split, stage_freed(n))
                if kind == "block":
                    sp.dma_start(dst, src[k * P:(k + 1) * P, :]).then_inc(landed, 16)
                elif kind == "tail":
                    for half_ in range(2):
                        sp.dma_start(dst[half_ * TAIL:(half_ + 1) * TAIL, :],
                                     src[KF * P:D, :]).then_inc(landed, 16)
                else:
                    for row in (64, 96):
                        sp.dma_start(dst[row:row + 1, :], src).then_inc(landed, 16)

            def load_ada(j):
                if j >= 2:
                    sp.wait_ge(ada_done, j - 1)
                cols = slice(j * D, (j + 1) * D)
                dst = ada[:, j % 2, :, :]
                sp.dma_start(dst[:, 0:KF, :], ada_wt[0:KF * P, cols].rearrange("(k p) n -> p k n", p=P)
                             ).then_inc(ada_in[j % 2], 16)
                sp.dma_start(dst[0:TAIL, KF, :], ada_wt[KF * P:D, cols]).then_inc(ada_in[j % 2], 16)
                sp.dma_start(dst[TAIL:TAIL + 1, KF, :], ada_b[:, cols]).then_inc(ada_in[j % 2], 16)

            sp.dma_start(condt[:, 0:KF, :], cond_t[0:KF * P, :].rearrange("(k p) n -> p k n", p=P)
                         ).then_inc(cond_in, 16)
            sp.dma_start(condt[0:TAIL, KF, :], cond_t[KF * P:D, :]).then_inc(cond_in, 16)
            load_ada(0)
            for i, g in enumerate((g1, g2, qg, kg)):
                sp.dma_start(gains[:, i:i + 1], g.partition_broadcast(P)).then_inc(gains_in, 16)
            sp.dma_start(fc2_b_rows, fc2_b.partition_broadcast(B)).then_inc(fc2_b_in, 16)
            sp.dma_start(xin[:, :], x[0]).then_inc(x_in, 16)
            load_ada(1)
            sp.wait_ge(bias_zeroed, 1)
            for n in range(QKV_STEPS):
                load_stage(n)
            load_ada(2)
            for n in range(QKV_STEPS, len(steps)):
                load_stage(n)
            for j in range(3, 6):
                load_ada(j)

            sp.wait_ge(tanh_done, 2)
            sp.dma_start(gate1_d, gate_rows[0]).then_inc(gates_out, 16)
            sp.dma_start(gate2_d, gate_rows[1]).then_inc(gates_out, 16)
            sp.wait_ge(gb2_done, 1)
            sp.dma_start(gb2_d, gb2_rows).then_inc(gates_out, 16)
            sp.wait_ge(gates_out, 48)

            def batch(b, early, last):
                if not last:
                    sp.wait_ge(x_scaled, b + 1)
                    sp.dma_start(xin[:, :], x[bass.ds(b + 1, 1), :, :].rearrange("a t d -> (a t) d")
                                 ).then_inc(x_in, 16)
                if early == 2:
                    finish(b - 2)
                if early >= 1:
                    load_rows(b - 1)

            def load_rows(b):
                if not isinstance(b, int) or b >= 1:
                    sp.wait_ge(x1_done, b)
                    sp.wait_ge(x1g_done, b)
                sp.dma_start(xres[:, :], x[bass.ds(b, 1), :, :].rearrange("a t d -> (a t) d")).then_inc(res_in, 16)
                sp.dma_start(gate1[:, :], gate1_d[bass.ds(b, 1), :].partition_broadcast(P)).then_inc(gate_in, 16)
                sp.dma_start(gb2_all[:, :], gb2_d[bass.ds(b, 1), :].partition_broadcast(P)).then_inc(gate_in, 16)

            def finish(b):
                sp.wait_ge(x1_done, b + 1)
                sp.dma_start(x1_d[bass.ds(b, 1), :, :].rearrange("a t d -> (a t) d"), x1[:, :]).then_inc(x1_out, 16)
                sp.wait_ge(x1g_done, b + 1)
                sp.dma_start(x1g_d[bass.ds(b, 1), :, :].rearrange("a t d -> (a t) d"), x1g[:, :]).then_inc(x1g_out, 16)

            run_batches(sp, batch)
            finish(B - 2)
            load_rows(B - 1)
            finish(B - 1)
            sp.wait_ge(x1_out, 16 * B)
            sp.wait_ge(x1g_out, 16 * B)

        @block.tensor
        def _(pe):
            def ada_part(j):
                pe.wait_ge(ada_in[j % 2], 48 * (j // 2 + 1))
                dst = q_ps if j % 2 == 0 else y_ps
                for n in range(2):
                    for k in range(KT):
                        rows = P if k < KF else TAIL + 1
                        last = nc.tensor.matmul(dst[0:B, n, 0:NH], silut[0:rows, k, :],
                                                ada[0:rows, j % 2, k, n * NH:(n + 1) * NH],
                                                start=(k == 0), stop=(k == KT - 1))
                last.then_inc(ada_done, 1)

            def coef_part(i):
                pe.wait_ge(row_done, i + 1)
                if i >= 1:
                    pe.wait_ge(coef_made, i)
                for k in range(KT):
                    last = nc.tensor.transpose(pt_ps[:, k * B:(k + 1) * B],
                                               modrow[:, i % 2, k * P:(k + 1) * P], ident[0:B, 0:B])
                last.then_inc(coef_t, 1)

            pe.wait_ge(silu_made, 1)
            pe.wait_ge(ident_made, 1)
            ada_part(0)
            ada_part(1)
            coef_part(0)
            coef_part(1)

            def x_transposed(b):
                pe.wait_ge(x_scaled, b + 1)
                if isinstance(b, int) and b == 0:
                    pe.wait_ge(row_done, 2)
                elif isinstance(b, int) and b == 1:
                    pe.wait_ge(tanh_done, 2)
                elif isinstance(b, int) and b == 2:
                    pe.wait_ge(h_made, 2 * KT)
                else:
                    pe.wait_ge(gated_done, b - 2)
                for k in range(KT):
                    last = nc.tensor.transpose(y_flat[:, k * P:(k + 1) * P], xn[:, k * P:(k + 1) * P], ident[:, :])
                last.then_inc(x_t, 1)

            x_transposed(0)
            ada_part(2)
            pe.wait_ge(h_made, KT)
            ada_part(3)
            coef_part(2)
            pe.wait_ge(tanh_done, 1)
            ada_part(4)
            coef_part(3)
            pe.wait_ge(row_done, 3)
            ada_part(5)
            pe.wait_ge(row_done, 4)
            pe.wait_ge(coef_made, 4)
            pe.wait_ge(ident_r_made, 1)
            pe.wait_ge(constants, 1)

            passes = [(h_hi, wq_hi, k) for k in range(KF)] + [(h_hi, wq_lo, k) for k in range(KF)]
            passes += [(h_hi, wq_x, KF)] + [(h_lo, wq_hi, k) for k in range(KF)] + [(h_lo, wq_y, KF)]

            def qkv(b, g, first, last_):
                for n in range(first, last_):
                    a, w, k = passes[n]
                    mov = w[:, g * GC:(g + 1) * GC] if k == KF else w[:, k, g * GC:(g + 1) * GC]
                    ins = nc.tensor.matmul(q_ps[:, g % 2, 0:GC], a[:, k * P:(k + 1) * P], mov,
                                           start=(n == 0), stop=(n == 13))
                if last_ == 14:
                    ins.then_inc(qkv_done, 1)

            def stacks_transposed(u):
                for w, dst in ((0, ts_ps), (1, tk_ps)):
                    for i in range(HG):
                        c = w * half + i * ST
                        ins = nc.tensor.transpose(dst[0:ST, i * T:(i + 1) * T].bitcast(F32R),
                                                  stack[:, c:c + ST], ident_r[:, :])
                ins.then_inc(stack_t, 1)

            def scores():
                for i in range(HG):
                    ins = nc.tensor.matmul(ts_ps[:, i * T:(i + 1) * T], qs[0:ST, i * T:(i + 1) * T],
                                           ks[0:ST, i * T:(i + 1) * T], start=True, stop=True)
                ins.then_inc(scores_done, 1)

            def probs_transposed():
                for i in range(HG):
                    ins = nc.tensor.transpose(pt_ps[:, i * T:(i + 1) * T], pr[:, i * T:(i + 1) * T], ident[:, :])
                ins.then_inc(probs_t, 1)

            def values(g):
                for i in range(HG):
                    c = i * VW
                    nc.tensor.matmul(o_ps[:, c:c + VW], pt_hi[:, i * T:(i + 1) * T], v[:, g, i, :],
                                     start=True, stop=False)
                    ins = nc.tensor.matmul(o_ps[:, c:c + HD + 2], pt_lo[:, i * T:(i + 1) * T],
                                           v[:, g, i, 0:HD + 2], start=False, stop=True)
                ins.then_inc(pv_done, 1)

            def o_transposed(b):
                pe.wait_ge(o_dup, b + 1)
                if not isinstance(b, int) or b >= 1:
                    pe.wait_ge(gated_done, b)
                pe.wait_ge(h_made, KT * B if isinstance(b, int) and b + 3 > B else (b + 3) * KT)
                for k in range(KT):
                    last = nc.tensor.transpose(y_flat[:, k * P:(k + 1) * P], o[:, k * P:(k + 1) * P], ident[:, :])
                last.then_inc(o_t, 1)

            proj_passes = [(ot_hi, wp_hi, k) for k in range(KF)] + [(ot_hi, wp_lo, k) for k in range(KF)]
            proj_passes += [(ot_hi, wp_x, KF)] + [(ot_lo, wp_hi, k) for k in range(KF)] + [(ot_lo, wp_y, KF)]

            def project(b, first, last_):
                if first == 0:
                    pe.wait_ge(ot_split, b + 1)
                for n in range(first, last_):
                    a, w, k = proj_passes[n]
                    for c in range(2):
                        mov = w[:, c * NH:(c + 1) * NH] if k == KF else w[:, k, c * NH:(c + 1) * NH]
                        ins = nc.tensor.matmul(y_ps[:, c, 0:NH], a[:, k * P:(k + 1) * P], mov,
                                               start=(n == 0), stop=(n == 13))
                if last_ == 14:
                    ins.then_inc(proj_done, 1)

            def slot(b, g, early, run=True, last=False):
                u = 4 * b + g
                one = early > 0 or g >= 1
                two = early > 0 or g >= 2
                three = early > 0 or g >= 3
                if run:
                    if g == 0:
                        pe.wait_ge(h_hi_made, b + 1)
                    if two:
                        pe.wait_ge(qk_scaled, u - 1)
                    qkv(b, g, 0, 9)
                if two:
                    pe.wait_ge(exp_done, u - 1)
                    if three:
                        pe.wait_ge(probs_split, u - 2)
                    probs_transposed()
                if one and (run or g == 0):
                    pe.wait_ge(qk_lo, u)
                    pe.wait_ge(qk_dup, u)
                    if two:
                        pe.wait_ge(shifted, u - 1)
                    stacks_transposed(u)
                if run:
                    if g == 0:
                        pe.wait_ge(h_split, b + 1)
                    qkv(b, g, 9, 14)
                if g == 2 and early >= 1:
                    o_transposed(b - 1)
                if two:
                    pe.wait_ge(probs_split, u - 1)
                    if three:
                        pe.wait_ge(o_normed, u - 2)
                    values((g + 2) % 4)
                if one and (run or g == 0):
                    pe.wait_ge(stack_read, 2 * u)
                    scores()
                if g == 0 and early >= 2:
                    project(b - 2, 7, 14)
                if g == 1 and run and not last:
                    x_transposed(b + 1)
                if g == 3 and early >= 1:
                    project(b - 1, 0, 7)

            def batch(b, early, last):
                if isinstance(b, int) and b == 0:
                    pe.wait_ge(w_split, QKV_STEPS)
                if isinstance(b, int) and b == 1:
                    pe.wait_ge(w_split, len(steps))
                for g in range(G):
                    slot(b, g, early, last=last)

            run_batches(pe, batch)
            slot(B, 0, 2, run=False)
            slot(B, 1, 2, run=False)
            o_transposed(B - 1)
            project(B - 1, 0, 14)

        @block.scalar
        def _(act):
            act.wait_ge(cond_in, 32)
            act.wait_ge(cond_padded, 1)
            nc.scalar.activation(sigm[:, 0, :, :], condt[:, :, :], ACT.Exp, scale=-1.0).then_inc(silu_exp, 1)

            def w_hi(n):
                kind, _, cols, hi, lo, _ = steps[n]
                src, landed, filled = staged(n)
                act.wait_ge(landed, filled)
                if kind == "block":
                    nc.scalar.activation(hi, src, ACT.Copy).then_inc(w_hi_done, 1)
                elif kind == "tail":
                    nc.scalar.activation(lo[0:64, :], src[0:64, :], ACT.Copy)
                    nc.scalar.activation(hi[:, :], src, ACT.Copy).then_inc(w_hi_done, 1)
                else:
                    nc.scalar.activation(lo[64:96, :], src[64:96, :], ACT.Copy)
                    nc.scalar.activation(lo[96:128, :], src[96:128, :], ACT.Copy).then_inc(w_hi_done, 1)

            def square_x(b):
                act.wait_ge(x_in, 16 * b + 16)
                if not isinstance(b, int) or b >= 1:
                    act.wait_ge(x_guarded, b)
                nc.scalar.activation(xsq[:, :], xin[:, :], ACT.Square, accum_out=xss[:, :]).then_inc(x_squared, 1)

            def modulate(b, k):
                nc.scalar.activation(h[:, k * P:(k + 1) * P], y_flat[:, k * P:(k + 1) * P], ACT.Identity,
                                     bias=coef[:, 0, k, bass.ds(b, 1)], scale=coef[:, 1, k, bass.ds(b, 1)]
                                     ).then_inc(h_made, 1)

            def h_hi_of(b):
                act.wait_ge(h_made, (b + 1) * KT)
                if not isinstance(b, int) or b >= 1:
                    act.wait_ge(qkv_done, 4 * b)
                nc.scalar.activation(h_hi[:, :], h[:, :], ACT.Copy).then_inc(h_hi_made, 1)

            square_x(0)
            for n in range(3):
                w_hi(n)
            act.wait_ge(x_t, 1)
            act.wait_ge(coef_made, 2)
            for k in range(KT):
                modulate(0, k)
            h_hi_of(0)
            for n in range(3, QKV_STEPS):
                w_hi(n)
            for n in range(QKV_STEPS, len(steps)):
                w_hi(n)
            for j, i in ((2, 0), (5, 1)):
                act.wait_ge(ada_done, j + 1)
                src = q_ps if j % 2 == 0 else y_ps
                nc.scalar.activation(gate_rows[i].rearrange("p (a b) -> p a b", a=2), src[0:B, :, 0:NH],
                                     ACT.Tanh).then_inc(tanh_done, 1)

            def slot(b, g, early, run=True, last=False):
                u = 4 * b + g
                one = early > 0 or g >= 1
                two = early > 0 or g >= 2
                three = early > 0 or g >= 3
                if two:
                    act.wait_ge(shifted, u - 1)
                    nc.scalar.activation(pr[:, :], pr[:, :], ACT.Exp).then_inc(exp_done, 1)
                if one and (run or g == 0):
                    act.wait_ge(qk_hi, u)
                    nc.scalar.activation(dup_of(stacked), stacked(0), ACT.Copy).then_inc(qk_dup, 1)
                if g == 2 and run and not last:
                    for k in range(2, KT):
                        modulate(b + 1, k)
                if g == 3 and early >= 1:
                    ot_hi_of(b - 1)
                if two:
                    act.wait_ge(probs_t, u - 1)
                    if three:
                        act.wait_ge(pv_done, u - 2)
                    nc.scalar.activation(pt_hi[:, :], pt_ps[:, :], ACT.Copy).then_inc(probs_hi, 1)
                if one and (run or g == 0):
                    act.wait_ge(stack_t, u)
                    if two:
                        act.wait_ge(scores_done, u - 1)
                    nc.scalar.activation(qs[0:ST, :], ts_ps[0:ST, :], ACT.Copy).then_inc(stack_read, 1)
                    nc.scalar.activation(ks[0:ST, :], tk_ps[0:ST, :], ACT.Copy).then_inc(stack_read, 1)
                if run:
                    act.wait_ge(qkv_done, u + 1)
                    if one:
                        act.wait_ge(qk_summed, u)
                    nc.scalar.activation(sq[:, :], q_ps[:, g % 2, 0:QK], ACT.Square).then_inc(qk_squared, 1)
                    if early > 0:
                        act.wait_ge(pv_done, u - 3)
                    nc.scalar.activation(v[:, g, :, 0:HD], q_ps[:, g % 2, QK:GC].rearrange("p (a b) -> p a b", b=HD),
                                         ACT.Copy).then_inc(v_hi_made, 1)
                if g == 3 and run and not last:
                    h_hi_of(b + 1)
                if two:
                    act.wait_ge(pv_done, u - 1)
                    nc.scalar.activation(olo[:, :, :], o_heads()[:, :, HD + 2:VW], ACT.Copy).then_inc(olo_read, 1)
                if g == 0 and run and not last:
                    square_x(b + 1)
                if g == 1 and run and not last:
                    act.wait_ge(x_t, b + 2)
                    act.wait_ge(h_split, b + 1)
                    for k in range(2):
                        modulate(b + 1, k)

            def dup_of(view):
                return view(2)

            def ot_hi_of(b):
                act.wait_ge(o_t, b + 1)
                if not isinstance(b, int) or b >= 1:
                    act.wait_ge(proj_done, b)
                nc.scalar.activation(ot_hi[:, :], y_flat[:, 0:DX], ACT.Copy).then_inc(ot_hi_made, 1)

            def o_heads():
                return o_ps[:, 0:HG * VW].rearrange("p (a b) -> p a b", b=VW)

            def batch(b, early, last):
                for g in range(G):
                    slot(b, g, early, last=last)

            run_batches(act, batch)
            slot(B, 0, 2, run=False)
            slot(B, 1, 2, run=False)
            ot_hi_of(B - 1)

        @block.vector
        def _(dve):
            nc.vector.memset(condt[TAIL:P, KF, :], 0.0).then_inc(cond_padded, 1)
            nc.vector.memset(silut[:, :, :], 1.0).then_inc(const_step, 1)
            nc.vector.memset(bias_stage[:, :], 0.0).then_inc(bias_zeroed, 1)
            for t in (h_lo, ot_lo):
                nc.vector.memset(t[64:128, KF * P:DX].bitcast(F32), 0.0).then_inc(const_step, 1)
            dve.wait_ge(const_step, 3)
            for t in (h_lo, ot_lo):
                for row in (64, 96):
                    nc.vector.memset(t[row:row + 1, KF * P:DX].bitcast(F32), 1.0)
            nc.vector.memset(minus_half[:, :], -0.5)
            nc.vector.memset(v[:, :, :, HD:HD + 1].bitcast(F32), 1.0)
            nc.vector.memset(v[:, :, :, HD + 1:HD + 2].bitcast(F32), 0.0).then_inc(constants, 1)
            dve.wait_ge(silu_exp, 1)
            nc.vector.tensor_scalar(sigm[:, 1, :, :], sigm[:, 0, :, :], 1.0, None, ALU.add).then_inc(silu_step, 1)
            dve.wait_ge(silu_step, 1)
            nc.vector.reciprocal(sigm[:, 0, :, :], sigm[:, 1, :, :]).then_inc(silu_step, 1)
            dve.wait_ge(silu_step, 2)
            nc.vector.tensor_tensor(silut[:, 0:KF, :], condt[:, 0:KF, :], sigm[:, 0, 0:KF, :], ALU.mult)
            nc.vector.tensor_tensor(silut[0:TAIL, KF, :], condt[0:TAIL, KF, :], sigm[0:TAIL, 0, KF, :],
                                    ALU.mult).then_inc(silu_made, 1)
            dve.wait_ge(ident_made, 1)
            nc.vector.tensor_copy(ident_r[:, :], ident[:, :]).then_inc(ident_r_made, 1)
            dve.wait_ge(gains_in, 64)
            nc.vector.tensor_scalar(gscale[:, :], gains[:, 0:2], float(D) ** 0.5, None, ALU.mult).then_inc(gains_made, 1)
            nc.vector.tensor_copy(qk_gain[:, 0, :], gains[:, 2:3].to_broadcast([P, HG]))
            nc.vector.tensor_scalar(qk_gain[:, 1, :], gains[:, 3:4].to_broadcast([P, HG]), float(HD) ** 0.5, None,
                                    ALU.mult).then_inc(gains_made, 1)
            dve.wait_ge(gains_made, 2)

            def w_lo(n):
                kind, _, cols, hi, lo, _ = steps[n]
                dve.wait_ge(w_hi_done, n + 1)
                src = staged(n)[0]
                if kind == "block":
                    ins = nc.vector.tensor_tensor(lo, src, hi.bitcast(F32), ALU.subtract)
                elif kind == "tail":
                    ins = nc.vector.tensor_tensor(hi[64:128, :], src[64:128, :], hi[64:128, :].bitcast(F32), ALU.subtract)
                else:
                    ins = nc.vector.tensor_tensor(lo[96:128, :], src[96:128, :], lo[96:128, :].bitcast(F32), ALU.subtract)
                ins.then_inc(w_split, 1)

            def guard_x(b):
                dve.wait_ge(x_squared, b + 1)
                nc.vector.tensor_scalar(xr[:, 0:1], xss[:, :], EPS2, None, ALU.max).then_inc(x_guarded, 1)

            def scale_x(b):
                dve.wait_ge(x_rnorm, b + 1)
                if not isinstance(b, int) or b >= 1:
                    dve.wait_ge(x_t, b)
                nc.vector.tensor_scalar(xn[:, 0:D], xin[:, :], xr[:, 1:2], None, ALU.mult)
                nc.vector.tensor_scalar(xn[:, D:DX], xin[:, KF * P:D], xr[:, 1:2], None, ALU.mult).then_inc(x_scaled, 1)

            def ada_row(j):
                i = {0: 0, 1: 1, 3: 2, 4: 3}[j]
                dve.wait_ge(ada_done, j + 1)
                if i >= 2:
                    dve.wait_ge(coef_t, i - 1)
                src = (q_ps if j % 2 == 0 else y_ps)[0:B, :, :]
                dst = modrow[:, i % 2, :]
                pieces = ((dst[:, 0:D].rearrange("p (a b) -> p a b", a=2), src[:, :, 0:NH]),
                          (dst[:, D:DX], src[:, 1, NH - TAIL:NH]))
                for to, of in pieces:
                    if i % 2 == 0:
                        ins = nc.vector.tensor_copy(to, of)
                    else:
                        ins = nc.vector.tensor_scalar(to, of, 1.0, gscale[0:B, i // 2:i // 2 + 1], ALU.add, ALU.mult)
                ins.then_inc(row_done, 1)

            def coef_out(i):
                dve.wait_ge(coef_t, i + 1)
                nc.vector.tensor_copy(coef[:, i, :, :], pt_ps[:, 0:KT * B].rearrange("p (k b) -> p k b", k=KT)
                                      ).then_inc(coef_made, 1)

            def h_lo_of(b):
                dve.wait_ge(h_hi_made, b + 1)
                nc.vector.tensor_tensor(h_lo[:, 0:KF * P], h[:, 0:KF * P], h_hi[:, 0:KF * P].bitcast(F32), ALU.subtract)
                nc.vector.tensor_tensor(h_lo[0:64, KF * P:DX], h[0:64, KF * P:DX], h_hi[0:64, KF * P:DX].bitcast(F32),
                                        ALU.subtract).then_inc(h_split, 1)

            guard_x(0)
            scale_x(0)
            ada_row(0)
            ada_row(1)
            for i in range(2):
                coef_out(i)
            for n in range(3):
                w_lo(n)
            h_lo_of(0)
            for n in range(3, len(steps)):
                w_lo(n)
            for i, j in ((2, 3), (3, 4)):
                ada_row(j)
                coef_out(i)
            dve.wait_ge(tanh_done, 2)
            dve.wait_ge(fc2_b_in, 16)
            nc.vector.tensor_tensor(gb2_rows, gate_rows[1], fc2_b_rows, ALU.mult).then_inc(gb2_done, 1)

            def slot(b, g, early, run=True, last=False):
                u = 4 * b + g
                one = early > 0 or g >= 1
                two = early > 0 or g >= 2
                if one and (run or g == 0):
                    dve.wait_ge(qk_rnorm, u)
                    nc.vector.tensor_tensor(qk[:, :, :, :].rearrange("p a b c -> p (a b) c"),
                                            q_ps[:, (g + 1) % 2, 0:QK].rearrange("p (a c) -> p a c", c=HD),
                                            rqk[:, :].unsqueeze(2).to_broadcast([P, 2 * HG, HD]),
                                            ALU.mult).then_inc(qk_scaled, 1)
                    dve.wait_ge(qk_scaled, u)
                    if two:
                        dve.wait_ge(stack_t, u - 1)
                    nc.vector.tensor_copy(stacked(0), qk[:, :, :, :]).then_inc(qk_hi, 1)
                    dve.wait_ge(qk_hi, u)
                    nc.vector.tensor_tensor(stacked(1), qk[:, :, :, :], stacked(0).bitcast(F32), ALU.subtract
                                            ).then_inc(qk_lo, 1)
                if g == 1 and run and not last:
                    guard_x(b + 1)
                if g == 1 and early >= 2:
                    x1_of(b - 2)
                if g == 1 and run and not last:
                    scale_x(b + 1)
                if g == 3 and early >= 1:
                    ot_lo_of(b - 1)
                if two:
                    dve.wait_ge(probs_hi, u - 1)
                    nc.vector.tensor_tensor(pt_lo[:, :], pt_ps[:, :], pt_hi[:, :].bitcast(F32), ALU.subtract
                                            ).then_inc(probs_split, 1)
                if run:
                    dve.wait_ge(qk_squared, u + 1)
                    if one:
                        dve.wait_ge(qk_pow, u)
                    nc.vector.tensor_reduce(ss[:, :], sq[:, :].rearrange("p (a c) -> p a c", c=HD), AX_X, ALU.add
                                            ).then_inc(qk_summed, 1)
                    dve.wait_ge(qk_summed, u + 1)
                    nc.vector.tensor_scalar(ssg[:, :], ss[:, :], EPS2, None, ALU.max).then_inc(qk_guarded, 1)
                    dve.wait_ge(v_hi_made, u + 1)
                    nc.vector.tensor_tensor(v[:, g, :, HD + 2:VW],
                                            q_ps[:, g % 2, QK:GC].rearrange("p (a b) -> p a b", b=HD),
                                            v[:, g, :, 0:HD].bitcast(F32), ALU.subtract).then_inc(v_split, 1)
                if g == 3 and run and not last:
                    h_lo_of(b + 1)
                if two:
                    gg = (g + 2) % 4
                    dve.wait_ge(olo_read, u - 1)
                    oh = o_ps[:, 0:HG * VW].rearrange("p (a b) -> p a b", b=VW)
                    nc.vector.reciprocal(rden[:, :].unsqueeze(2), oh[:, :, HD:HD + 1])
                    nc.vector.tensor_tensor(osum[:, :, :], oh[:, :, 0:HD], olo[:, :, :], ALU.add).then_inc(o_summed, 1)
                    dve.wait_ge(o_summed, u - 1)
                    if gg == 0 and not (isinstance(b, int) and b == 0):
                        dve.wait_ge(o_t, b)
                    nc.vector.tensor_tensor(o[:, gg * HG * HD:(gg + 1) * HG * HD].rearrange("p (a b) -> p a b", b=HD),
                                            osum[:, :, :], rden[:, :].unsqueeze(2).to_broadcast([P, HG, HD]),
                                            ALU.mult).then_inc(o_normed, 1)
                    if gg == 3:
                        dve.wait_ge(o_normed, u - 1)
                        nc.vector.tensor_copy(o[:, D:DX], o[:, KF * P:D]).then_inc(o_dup, 1)
                if one and (run or g == 0):
                    dve.wait_ge(scores_done, u)
                    s_heads = ts_ps[:, :].rearrange("p (a b) -> p a b", b=T)
                    nc.vector.tensor_reduce(mx[:, :], s_heads, AX_X, ALU.max).then_inc(max_done, 1)
                    dve.wait_ge(max_done, u)
                    if two:
                        dve.wait_ge(probs_t, u - 1)
                    nc.vector.tensor_tensor(pr[:, :].rearrange("p (a b) -> p a b", b=T), s_heads,
                                            mx[:, :].unsqueeze(2).to_broadcast([P, HG, T]),
                                            ALU.subtract).then_inc(shifted, 1)

            def ot_lo_of(b):
                dve.wait_ge(ot_hi_made, b + 1)
                if not isinstance(b, int) or b >= 1:
                    dve.wait_ge(proj_done, b)
                nc.vector.tensor_tensor(ot_lo[:, 0:KF * P], y_flat[:, 0:KF * P], ot_hi[:, 0:KF * P].bitcast(F32),
                                        ALU.subtract)
                nc.vector.tensor_tensor(ot_lo[0:64, KF * P:DX], y_flat[0:64, KF * P:DX],
                                        ot_hi[0:64, KF * P:DX].bitcast(F32), ALU.subtract).then_inc(ot_split, 1)

            def x1_of(b):
                dve.wait_ge(proj_done, b + 1)
                dve.wait_ge(gate_in, 32 * b + 32)
                nc.vector.tensor_tensor(gated[:, :].rearrange("p (a b) -> p a b", a=2), y_half,
                                        gate1[:, :].rearrange("p (a b) -> p a b", a=2), ALU.mult
                                        ).then_inc(gated_done, 1)
                dve.wait_ge(gated_done, b + 1)
                dve.wait_ge(res_in, 16 * b + 16)
                if not isinstance(b, int) or b >= 1:
                    dve.wait_ge(x1_out, 16 * b)
                    dve.wait_ge(x1g_done, b)
                nc.vector.tensor_tensor(x1[:, :], gated[:, :], xres[:, :], ALU.add).then_inc(x1_done, 1)

            def batch(b, early, last):
                for g in range(G):
                    slot(b, g, early, last=last)

            run_batches(dve, batch)
            slot(B, 0, 2, run=False)
            slot(B, 1, 2, run=False)
            ot_lo_of(B - 1)
            x1_of(B - 1)

        @block.gpsimd
        def _(pool):
            nc.gpsimd.memset(ident[:, :], 0.0).then_inc(ident_zeroed, 1)
            pool.wait_ge(ident_zeroed, 1)
            nc.gpsimd.affine_select(out=ident[:, :], in_=ident[:, :], compare_op=ALU.not_equal, fill=1.0, base=0,
                                    pattern=[[-1, P]], channel_multiplier=1).then_inc(ident_made, 1)

            def x_rnorm_of(b):
                pool.wait_ge(x_guarded, b + 1)
                nc.gpsimd.tensor_tensor(xr[:, 1:2], xr[:, 0:1], minus_half[:, 0:1], ALU.pow).then_inc(x_rnorm, 1)

            def qk_rnorm_of(u):
                pool.wait_ge(qk_guarded, u + 1)
                nc.gpsimd.tensor_tensor(rpow[:, :], ssg[:, :], minus_half[:, :], ALU.pow).then_inc(qk_pow, 1)
                pool.wait_ge(qk_pow, u + 1)
                if not isinstance(u, int) or u >= 1:
                    pool.wait_ge(qk_scaled, u)
                nc.gpsimd.tensor_tensor(rqk[:, :], rpow[:, :], qk_gain[:, :, :].rearrange("p a b -> p (a b)"),
                                        ALU.mult).then_inc(qk_rnorm, 1)

            def x1g_of(b):
                pool.wait_ge(x1_done, b + 1)
                pool.wait_ge(gate_in, 32 * b + 32)
                if not isinstance(b, int) or b >= 1:
                    pool.wait_ge(x1g_out, 16 * b)
                nc.gpsimd.tensor_tensor(x1g[:, :], x1[:, :], gb2_all[:, :], ALU.add).then_inc(x1g_done, 1)

            pool.wait_ge(gains_made, 2)
            pool.wait_ge(constants, 1)
            x_rnorm_of(0)

            def batch(b, early, last):
                for g in range(G):
                    if g == 1 and not last:
                        x_rnorm_of(b + 1)
                    if g == 2 and early >= 2:
                        x1g_of(b - 2)
                    qk_rnorm_of(4 * b + g)

            run_batches(pool, batch)
            x1g_of(B - 2)
            x1g_of(B - 1)


def mlp_stage(nc, fc1_wt, fc1_bt, fc2_wt, gate2_d, x1_d, x1g_d, out, coef, ident, minus_half):
    with ExitStack() as ctx:
        def sb(name, shape, dt):
            return ctx.enter_context(nc.sbuf_tensor(name, shape, dt))

        def ps(name, shape):
            return ctx.enter_context(nc.psum_tensor(name, shape, F32))

        def sem(name):
            return ctx.enter_context(nc.semaphore(name))

        w1_hi = sb("w1_hi", [P, KF, F], F32R)
        w1_lo = sb("w1_lo", [P, KF, F], F32R)
        w1_x = sb("w1_x", [P, F], F32R)
        w2_hi = sb("w2_hi", [P, MT, D], F32R)
        w2_lo = sb("w2_lo", [P, MT, D], F32R)
        stage1 = sb("stage1", [P, 2, KT, P], F32)
        stage2 = sb("stage2", [P, 2, D], F32)
        fc1_b = sb("fc1_b", [P, MT], F32)
        xin = sb("x1_in", [P, DX], F32)
        xss = sb("x1_ss", [P, 1], F32)
        xr = sb("x1_r", [P, 2], F32)
        h = sb("h2", [P, KT, 2, T], F32)
        h_hi = sb("h2_hi", [P, KT, 2, T], F32R)
        h_lo = sb("h2_lo", [P, KT, 2, T], F32R)
        act_f = sb("act_f", [P, 2 * T], F32)
        act_hi = sb("act_hi", [P, 2, 2 * T], F32R)
        act_lo = sb("act_lo", [P, 2, 2 * T], F32R)
        res = sb("res", [P, 2, D], F32)
        gate = sb("gate", [P, 2, D], F32)

        z_ps = ps("z_ps", [P, 2, 2, BANK])
        f_ps = ps("f_ps", [P, 2, BANK])
        x_ps = ps("x_ps", [P, 2, BANK])
        x_flat = x_ps[:, :, :].rearrange("p a b -> p (a b)")

        w1_in = [sem(f"w1_in{i}") for i in range(2)]
        w2_in = [sem(f"w2_in{i}") for i in range(2)]
        b1_in = sem("b1_in")
        x_in = sem("x1_landed")
        res_in = sem("res_landed")
        gate_in = sem("gate_landed")
        out_done = sem("out_done")
        w_hi_made = sem("w12_hi_made")
        w_split = sem("w12_split")
        x_squared = sem("x1_squared")
        x_guarded = sem("x1_guarded")
        x_rnorm = sem("x1_rnorm")
        x_dup = sem("x1_dup")
        x_scaled = sem("x1_scaled")
        x_t = sem("x1_t")
        h_made = sem("h2_made")
        h_hi_made = sem("h2_hi_made")
        h_split = sem("h2_split")
        f_done = sem("f_done")
        gelu_done = sem("gelu_done")
        act_hi_made = sem("act_hi_made")
        act_split = sem("act_split")
        z_step = sem("z_step")
        gated = sem("mlp_gated")
        summed = sem("mlp_summed")

        def run_pairs(eng, pair):
            pair(0, True, False)
            with eng.Fori(1, PAIRS - 1) as p:
                pair(p, False, False)
            pair(PAIRS - 1, False, True)

        SQUARE_AT, TRANSPOSE_AT, MODULATE_AT = (1, 9), (4, 12), (5, 13)

        block = ctx.enter_context(nc.Block())

        @block.sync
        def _(sp):
            def load_x(b):
                sp.dma_start(xin[:, 0:D], x1_d[bass.ds(b, 1), :, :].rearrange("a t d -> (a t) d")).then_inc(x_in, 16)

            def load_rows(p):
                if not isinstance(p, int) or p >= 1:
                    sp.wait_ge(out_done, 32 * p)
                for i in range(2):
                    sp.dma_start(res[:, i, :], x1g_d[bass.ds(2 * p + i, 1), :, :].rearrange("a t d -> (a t) d")
                                 ).then_inc(res_in, 16)
                    sp.dma_start(gate[:, i, :], gate2_d[bass.ds(2 * p + i, 1), :].partition_broadcast(P)
                                 ).then_inc(gate_in, 16)

            def load_w(m):
                if m >= 2:
                    sp.wait_ge(w_split, m - 1)
                cols = slice(m * P, (m + 1) * P)
                dst = stage1[:, m % 2, :, :]
                sp.dma_start(dst[:, 0:KF, :], fc1_wt[0:KF * P, cols].rearrange("(k p) n -> p k n", p=P)
                             ).then_inc(w1_in[m % 2], 16)
                for i in range(2):
                    sp.dma_start(dst[i * TAIL:(i + 1) * TAIL, KF, :], fc1_wt[KF * P:D, cols]).then_inc(w1_in[m % 2], 16)
                sp.dma_start(stage2[:, m % 2, :], fc2_wt[m * P:(m + 1) * P, :]).then_inc(w2_in[m % 2], 16)

            load_x(0)
            sp.dma_start(fc1_b[:, :], fc1_bt).then_inc(b1_in, 16)
            load_w(0)
            load_w(1)
            sp.wait_ge(x_t, 1)
            load_x(1)
            load_w(2)
            load_rows(0)
            for m in range(3, MT):
                load_w(m)
                for i in range(2):
                    if m == 3 + 5 * i:
                        sp.wait_ge(x_t, 2 + i)
                        load_x(2 + i)

            def pair(p, first, last):
                if not last and not first:
                    for i in range(2):
                        sp.wait_ge(x_t, 2 * p + 2 + i)
                        load_x(2 * p + 2 + i)
                for i in range(2):
                    sp.wait_ge(summed, 2 * p + 1 + i)
                    sp.dma_start(out[bass.ds(2 * p + i, 1), :, :].rearrange("a t d -> (a t) d"), res[:, i, :]
                                 ).then_inc(out_done, 16)
                if not last:
                    load_rows(p + 1)

            run_pairs(sp, pair)
            sp.wait_ge(out_done, 32 * PAIRS)

        @block.tensor
        def _(pe):
            def x_transposed(b):
                pe.wait_ge(x_scaled, b + 1)
                if not isinstance(b, int) or b >= 1:
                    pe.wait_ge(h_made, KT * b)
                for k in range(KT):
                    last = nc.tensor.transpose(x_flat[:, k * P:(k + 1) * P], xin[:, k * P:(k + 1) * P], ident[:, :])
                last.then_inc(x_t, 1)

            hi_passes = [(w1_hi, h_hi, k) for k in range(KF)] + [(w1_lo, h_hi, k) for k in range(KF)] + [(w1_x, h_hi, KF)]
            lo_passes = [(w1_hi, h_lo, k) for k in range(KF)] + [(w1_x, h_lo, KF)]
            passes = hi_passes + lo_passes

            def fc1(p, m):
                for n, (w, a, k) in enumerate(passes):
                    if m == 0 and n == len(hi_passes):
                        pe.wait_ge(h_split, p + 1)
                    cols = slice(m * P, (m + 1) * P)
                    ins = nc.tensor.matmul(f_ps[:, m % 2, 0:2 * T], w[:, cols] if k == KF else w[:, k, cols],
                                           a[:, k, :, :], start=(n == 0), stop=(n == len(passes) - 1))
                ins.then_inc(f_done, 1)

            def fc2(m):
                for i in range(2):
                    tok = slice(i * T, (i + 1) * T)
                    for n, (a, w) in enumerate(((act_hi, w2_hi), (act_hi, w2_lo), (act_lo, w2_hi))):
                        for c in range(2):
                            ins = nc.tensor.matmul(z_ps[:, i, c, 0:NH], a[:, m % 2, tok], w[:, m, c * NH:(c + 1) * NH],
                                                   start=(m == 0 and n == 0), stop=(m == MT - 1 and n == 2))
                ins.then_inc(z_step, 1)

            def pair(p, first, last):
                pe.wait_ge(h_hi_made, p + 1)
                for m in range(MT + 1):
                    if m < MT:
                        if first:
                            pe.wait_ge(w_split, m + 1)
                        if not (first and m < 2):
                            pe.wait_ge(gelu_done, p * MT + m - 1)
                        fc1(p, m)
                    if m >= 1:
                        if m == 1 and not first:
                            pe.wait_ge(gated, 2 * p)
                        pe.wait_ge(act_split, p * MT + m)
                        fc2(m - 1)
                    if not last:
                        for i in range(2):
                            if m == TRANSPOSE_AT[i]:
                                x_transposed(2 * p + 2 + i)

            x_transposed(0)
            x_transposed(1)
            run_pairs(pe, pair)

        @block.scalar
        def _(act):
            def square_x(b):
                act.wait_ge(x_in, 16 * b + 16)
                if not isinstance(b, int) or b >= 1:
                    act.wait_ge(x_guarded, b)
                    act.wait_ge(h_made, KT * b)
                nc.scalar.activation(x_flat[:, 0:D], xin[:, 0:D], ACT.Square, accum_out=xss[:, :]).then_inc(x_squared, 1)

            def modulate(b, i):
                act.wait_ge(x_t, b + 1)
                for k in range(KT):
                    nc.scalar.activation(h[:, k, i, :], x_flat[:, k * P:(k + 1) * P], ACT.Identity,
                                         bias=coef[:, 2, k, bass.ds(b, 1)], scale=coef[:, 3, k, bass.ds(b, 1)]
                                         ).then_inc(h_made, 1)

            def h_hi_of(p):
                act.wait_ge(h_made, (p + 1) * (2 * KT))
                if not isinstance(p, int) or p >= 1:
                    act.wait_ge(f_done, p * MT)
                nc.scalar.activation(h_hi[:, :, :, :], h[:, :, :, :], ACT.Copy).then_inc(h_hi_made, 1)

            def w_hi(m):
                act.wait_ge(w1_in[m % 2], 48 * (m // 2 + 1))
                act.wait_ge(w2_in[m % 2], 16 * (m // 2 + 1))
                cols = slice(m * P, (m + 1) * P)
                nc.scalar.activation(w1_hi[:, :, cols], stage1[:, m % 2, 0:KF, :], ACT.Copy)
                nc.scalar.activation(w1_x[:, cols], stage1[:, m % 2, KF, :], ACT.Copy)
                nc.scalar.activation(w2_hi[:, m, :], stage2[:, m % 2, :], ACT.Copy).then_inc(w_hi_made, 1)

            square_x(0)
            w_hi(0)
            modulate(0, 0)
            square_x(1)
            w_hi(1)
            modulate(1, 1)
            h_hi_of(0)
            act.wait_ge(b1_in, 16)

            def pair(p, first, last):
                for m in range(MT):
                    if first and m + 2 < MT:
                        w_hi(m + 2)
                    act.wait_ge(f_done, p * MT + m + 1)
                    if not (first and m == 0):
                        act.wait_ge(act_split, p * MT + m)
                    nc.scalar.activation(act_f[:, :], f_ps[:, m % 2, 0:2 * T], ACT.Gelu_apprx_tanh,
                                         bias=fc1_b[:, m:m + 1]).then_inc(gelu_done, 1)
                    if not last:
                        for i in range(2):
                            if m == SQUARE_AT[i]:
                                square_x(2 * p + 2 + i)
                            if m == MODULATE_AT[i]:
                                act.wait_ge(x_t, 2 * p + 3 + i)
                                for k in range(KT):
                                    nc.scalar.activation(
                                        h[:, k, i, :], x_flat[:, k * P:(k + 1) * P], ACT.Identity,
                                        bias=coef[:, 2, k, bass.ds(2 * p + 2 + i, 1)],
                                        scale=coef[:, 3, k, bass.ds(2 * p + 2 + i, 1)]).then_inc(h_made, 1)
                if not last:
                    h_hi_of(p + 1)

            run_pairs(act, pair)

        @block.vector
        def _(dve):
            def guard_x(b):
                dve.wait_ge(x_squared, b + 1)
                nc.vector.tensor_scalar(xr[:, 0:1], xss[:, :], EPS2, None, ALU.max).then_inc(x_guarded, 1)

            def scale_x(b):
                dve.wait_ge(x_rnorm, b + 1)
                nc.vector.tensor_scalar(xin[:, D:DX], xin[:, KF * P:D], xr[:, 1:2], None, ALU.mult).then_inc(x_dup, 1)
                dve.wait_ge(x_dup, b + 1)
                nc.vector.tensor_scalar(xin[:, 0:D], xin[:, 0:D], xr[:, 1:2], None, ALU.mult).then_inc(x_scaled, 1)

            def h_lo_of(p):
                dve.wait_ge(h_hi_made, p + 1)
                nc.vector.tensor_tensor(h_lo[:, :, :, :], h[:, :, :, :], h_hi[:, :, :, :].bitcast(F32), ALU.subtract
                                        ).then_inc(h_split, 1)

            def w_lo(m):
                dve.wait_ge(w_hi_made, m + 1)
                cols = slice(m * P, (m + 1) * P)
                s = m % 2
                nc.vector.tensor_tensor(w1_lo[:, :, cols], stage1[:, s, 0:KF, :], w1_hi[:, :, cols].bitcast(F32), ALU.subtract)
                nc.vector.tensor_tensor(w1_x[64:128, cols], stage1[64:128, s, KF, :], w1_x[64:128, cols].bitcast(F32),
                                        ALU.subtract)
                nc.vector.tensor_tensor(w2_lo[:, m, :], stage2[:, s, :], w2_hi[:, m, :].bitcast(F32), ALU.subtract
                                        ).then_inc(w_split, 1)

            guard_x(0)
            scale_x(0)
            w_lo(0)
            guard_x(1)
            scale_x(1)
            w_lo(1)
            h_lo_of(0)

            def pair(p, first, last):
                for m in range(MT):
                    if first and m + 2 < MT:
                        w_lo(m + 2)
                    if not (first and m < 2):
                        dve.wait_ge(z_step, p * MT + m - 1)
                    dve.wait_ge(gelu_done, p * MT + m + 1)
                    nc.vector.tensor_copy(act_hi[:, m % 2, :], act_f[:, :]).then_inc(act_hi_made, 1)
                    dve.wait_ge(act_hi_made, p * MT + m + 1)
                    nc.vector.tensor_tensor(act_lo[:, m % 2, :], act_f[:, :], act_hi[:, m % 2, :].bitcast(F32),
                                            ALU.subtract).then_inc(act_split, 1)
                    if not last:
                        for i in range(2):
                            if m == SQUARE_AT[i]:
                                guard_x(2 * p + 2 + i)
                            if m == SQUARE_AT[i] + 1:
                                scale_x(2 * p + 2 + i)
                if not last:
                    h_lo_of(p + 1)
                dve.wait_ge(z_step, p * MT + MT)
                for i in range(2):
                    dve.wait_ge(gate_in, 32 * p + 32)
                    nc.vector.tensor_tensor(gate[:, i, :].rearrange("p (a b) -> p a b", a=2), z_ps[:, i, :, 0:NH],
                                            gate[:, i, :].rearrange("p (a b) -> p a b", a=2), ALU.mult
                                            ).then_inc(gated, 1)

            run_pairs(dve, pair)

        @block.gpsimd
        def _(pool):
            def x_rnorm_of(b):
                pool.wait_ge(x_guarded, b + 1)
                nc.gpsimd.tensor_tensor(xr[:, 1:2], xr[:, 0:1], minus_half[:, 0:1], ALU.pow).then_inc(x_rnorm, 1)

            x_rnorm_of(0)
            x_rnorm_of(1)

            def pair(p, first, last):
                if not last:
                    x_rnorm_of(2 * p + 2)
                    x_rnorm_of(2 * p + 3)
                for i in range(2):
                    pool.wait_ge(gated, 2 * p + 1 + i)
                    pool.wait_ge(res_in, 32 * p + 32)
                    nc.gpsimd.tensor_tensor(res[:, i, :], res[:, i, :], gate[:, i, :], ALU.add).then_inc(summed, 1)

            run_pairs(pool, pair)


def kernel(**inputs):
    import numpy as np
    import concourse.bacc as bacc
    from concourse import mybir as mb
    from concourse.bass_utils import run_bass_kernel_spmd

    def rows(name):
        return np.asarray(inputs[name]).reshape(1, -1)

    by_unit = lambda a: np.asarray(a).reshape(3, G, HG * HD, -1).transpose(1, 0, 2, 3).reshape(3 * D, -1)
    arrays = {
        "x": np.asarray(inputs["x"]),
        "cond_t": np.asarray(inputs["cond_1152"]).T,
        "g1": rows("L0_cond_g1"), "g2": rows("L0_cond_g2"),
        "qkv_wt": by_unit(inputs["L0_cond_qkv_w"]).T,
        "qkv_b": by_unit(inputs["L0_cond_qkv_b"]).T,
        "qg": rows("L0_cond_qg"), "kg": rows("L0_cond_kg"),
        "proj_wt": np.asarray(inputs["L0_cond_proj_w"]).T, "proj_b": rows("L0_cond_proj_b"),
        "fc1_wt": np.asarray(inputs["L0_cond_fc1_w"]).T,
        "fc1_bt": np.asarray(inputs["L0_cond_fc1_b"]).reshape(MT, P).T,
        "fc2_wt": np.asarray(inputs["L0_cond_fc2_w"]).T, "fc2_b": rows("L0_cond_fc2_b"),
        "ada_wt": np.asarray(inputs["L0_cond_ada_w"]).T, "ada_b": rows("L0_cond_ada_b"),
    }
    arrays = {name: np.ascontiguousarray(a) for name, a in arrays.items()}
    nc = bacc.Bacc("TRN2", target_bir_lowering=False, num_devices=1)
    args = {name: nc.dram_tensor(name + "_dram", a.shape, mb.dt.from_np(a.dtype), kind="ExternalInput").ap()
            for name, a in arrays.items()}
    out = nc.dram_tensor("out_dram", (B, T, D), mb.dt.float32, kind="ExternalOutput").ap()
    build(nc, out=out, **args)
    ran = run_bass_kernel_spmd(nc, [{name + "_dram": a for name, a in arrays.items()}], core_ids=[0])
    return ran.results[0]["out_dram"]
```

```python
from contextlib import ExitStack

import concourse.bass as bass
from concourse import mybir

F32 = mybir.dt.float32
F32R = mybir.dt.float32r
F16 = mybir.dt.float16
BF16 = mybir.dt.bfloat16
ALU = mybir.AluOpType
ACT = mybir.ActivationFunctionType
AX_X = mybir.AxisListType.X

P = 128
B = 32
T = 128
D = 576
H = 16
HD = D // H
F = 4 * D
KF = D // P
TAIL = D - KF * P
KT = KF + 1
DX = KT * P
HG = 4
G = H // HG
GC = 3 * HG * HD
QK = 2 * HG * HD
NH = D // 2
ST = 3 * HD
VW = HD + 1
P_SCALE = 2.0 ** 15
MT = F // P
PAIRS = B // 2
BANK = 512
EPS2 = 1e-24


def build(nc, x, cond_t, g1, g2, qkv_wt, qkv_b, qg, kg, proj_wt, proj_b,
          fc1_wt, fc1_bt, fc2_wt, fc2_b, ada_wt, ada_b, out):
    gate1_d = nc.dram_tensor("gate_msa_rows", [B, D], F32, kind="Internal").ap()
    gate2_d = nc.dram_tensor("gate_mlp_rows", [B, D], F32, kind="Internal").ap()
    gb2_d = nc.dram_tensor("gated_fc2_bias_rows", [B, D], F32, kind="Internal").ap()
    x1_d = nc.dram_tensor("x_after_attention", [B, T, D], F32, kind="Internal").ap()
    x1g_d = nc.dram_tensor("x_after_attention_biased", [B, T, D], F32, kind="Internal").ap()

    with ExitStack() as whole:
        def keep_sb(name, shape, dt):
            return whole.enter_context(nc.sbuf_tensor(name, shape, dt))

        coef = keep_sb("coef", [P, 4, KT, B], F32)
        ident = keep_sb("ident", [P, P], F32)
        minus_half = keep_sb("minus_half", [P, 2 * HG], F32)
        attention_stage(nc, x, cond_t, g1, g2, qkv_wt, qkv_b, qg, kg, proj_wt, proj_b, fc2_b, ada_wt, ada_b,
                        gate1_d, gate2_d, gb2_d, x1_d, x1g_d, coef, ident, minus_half)
        mlp_stage(nc, fc1_wt, fc1_bt, fc2_wt, gate2_d, x1_d, x1g_d, out, coef, ident, minus_half)


def attention_stage(nc, x, cond_t, g1, g2, qkv_wt, qkv_b, qg, kg, proj_wt, proj_b, fc2_b, ada_wt, ada_b,
                    gate1_d, gate2_d, gb2_d, x1_d, x1g_d, coef, ident, minus_half):
    with ExitStack() as ctx:
        def sb(name, shape, dt):
            return ctx.enter_context(nc.sbuf_tensor(name, shape, dt))

        def ps(name, shape):
            return ctx.enter_context(nc.psum_tensor(name, shape, F32))

        def sem(name):
            return ctx.enter_context(nc.semaphore(name))

        wq_hi = sb("wq_hi", [P, KF, 3 * D], F32R)
        wq_lo = sb("wq_lo", [P, KF, 3 * D], F32R)
        wq_x = sb("wq_x", [P, 3 * D], F32R)
        wq_y = sb("wq_y", [P, 3 * D], F32R)
        wp_hi = sb("wp_hi", [P, KF, D], F32R)
        wp_lo = sb("wp_lo", [P, KF, D], F32R)
        wp_x = sb("wp_x", [P, D], F32R)
        wp_y = sb("wp_y", [P, D], F32R)
        stage = sb("stage", [P, 2, KT, GC], F32)
        bias_stage = sb("bias_stage", [P, 3 * D], F32)
        ada = sb("ada", [P, 2, KT, D], F32)
        condt = sb("condt", [P, KT, B], F32)
        sigm = sb("sigm", [P, 2, KT, B], F32)
        silut = sb("silut", [P, KT, B], F32)
        modrow = sb("modrow", [B, 2, DX], F32)
        gains = sb("gains", [P, 4], F32)
        gscale = sb("gscale", [P, 2], F32)
        qk_gain = sb("qk_gain", [P, 2, HG], F32)
        ident_r = sb("ident_r", [P, P], F32R)

        xin = sb("xin", [P, D], F32)
        xsq = sb("xsq", [P, D], F32)
        xss = sb("xss", [P, 1], F32)
        xr = sb("xr", [P, 2], F32)
        xn = sb("xn", [P, DX], F32)
        h = sb("h", [P, DX], F32)
        h_hi = sb("h_hi", [P, DX], F32R)
        h_lo = sb("h_lo", [P, DX], F32R)
        o = sb("o", [P, DX], F32)
        ot_hi = sb("ot_hi", [P, DX], F32R)
        ot_lo = sb("ot_lo", [P, DX], F32R)
        xres = sb("xres", [P, D], F32)
        gate1 = sb("gate1", [P, D], F32)
        gb2_all = sb("gb2_all", [P, D], F32)
        gated = sb("gated", [P, D], F32)
        x1 = sb("x1", [P, D], F32)
        x1g = sb("x1g", [P, D], F32)
        gate_rows = (gated[0:B, :], x1[0:B, :])
        gb2_rows = x1g[0:B, :]
        fc2_b_rows = xres[0:B, :]

        sq = sb("sq", [P, QK], F32)
        ss = sb("ss", [P, 2 * HG], F32)
        ssg = sb("ssg", [P, 2 * HG], F32)
        rpow = sb("rpow", [P, 2 * HG], F32)
        rqk = sb("rqk", [P, 2 * HG], F32)
        qk = sb("qk", [P, 2, HG, HD], F32)
        stack = sb("stack", [P, 2 * HG * ST], F32R)
        v = sb("v", [P, G, 3, HG, VW], BF16)
        v_rest = sb("v_rest", [P, HG, HD], F32)
        qs = sb("qs", [P, HG * T], F32R)
        ks = sb("ks", [P, HG * T], F32R)
        neg_max = sb("neg_max", [P, HG], F32)
        pr = sb("pr", [P, HG * T], F32)
        pt_hi = sb("pt_hi", [P, HG * T], F16)
        pt_lo = sb("pt_lo", [P, HG * T], F16)
        rden = sb("rden", [P, HG], F32)
        zero = sb("zero", [P, HG], F32)

        q_ps = ps("q_ps", [P, 2, BANK])
        ts_ps = ps("ts_ps", [P, BANK])
        tk_ps = ps("tk_ps", [P, BANK])
        pt_ps = ps("pt_ps", [P, BANK])
        o_ps = ps("o_ps", [P, BANK])
        y_ps = ps("y_ps", [P, 2, BANK])
        y_flat = y_ps[:, :, :].rearrange("p a b -> p (a b)")
        y_half = y_ps[:, :, 0:NH]

        half = HG * ST

        def stacked(first):
            base = stack[:, first * HD:first * HD + HD]
            step = half + (HD if first == 1 else -HD if first == 2 else 0)
            return bass.AP(tensor=base.tensor, offset=base.offset,
                           ap=[base.ap[0], [step, 2], [ST, HG], [1, HD]])

        cond_in = sem("cond_in")
        gains_in = sem("gains_in")
        fc2_b_in = sem("fc2_b_in")
        ada_in = [sem(f"ada_in{i}") for i in range(2)]
        stage_in = [sem(f"stage_in{i}") for i in range(2)]
        x_in = sem("x_in")
        res_in = sem("res_in")
        gate_in = sem("gate_in")
        gates_out = sem("gates_out")
        x1_out = sem("x1_out")
        x1g_out = sem("x1g_out")
        bias_in = sem("bias_in")
        cond_padded = sem("cond_padded")
        bias_zeroed = sem("bias_zeroed")
        const_step = sem("const_step")
        constants = sem("constants")
        ident_zeroed = sem("ident_zeroed")
        ident_made = sem("ident_made")
        ident_r_made = sem("ident_r_made")
        gains_made = sem("gains_made")
        silu_step = sem("silu_step")
        silu_exp = sem("silu_exp")
        silu_made = sem("silu_made")
        ada_done = sem("ada_done")
        row_done = sem("row_done")
        coef_t = sem("coef_t")
        coef_made = sem("coef_made")
        tanh_done = sem("tanh_done")
        gb2_done = sem("gb2_done")
        w_hi_done = sem("w_hi_done")
        w_split = sem("w_split")
        bias_hi_done = sem("bias_hi_done")
        bias_split = sem("bias_split")
        x_squared = sem("x_squared")
        x_guarded = sem("x_guarded")
        x_rnorm = sem("x_rnorm")
        x_scaled = sem("x_scaled")
        x_t = sem("x_t")
        h_made = sem("h_made")
        h_hi_made = sem("h_hi_made")
        h_split = sem("h_split")
        qkv_done = sem("qkv_done")
        qk_squared = sem("qk_squared")
        qk_summed = sem("qk_summed")
        qk_guarded = sem("qk_guarded")
        qk_pow = sem("qk_pow")
        qk_rnorm = sem("qk_rnorm")
        qk_scaled = sem("qk_scaled")
        qk_hi = sem("qk_hi")
        qk_lo = sem("qk_lo")
        qk_dup = sem("qk_dup")
        stack_t = sem("stack_t")
        stack_read = sem("stack_read")
        scores_done = sem("scores_done")
        v_first = sem("v_first")
        v_left = sem("v_left")
        v_second = sem("v_second")
        v_parts = sem("v_parts")
        max_done = sem("max_done")
        exp_done = sem("exp_done")
        o_rden = sem("o_rden")
        probs_t = sem("probs_t")
        probs_hi = sem("probs_hi")
        probs_split = sem("probs_split")
        pv_done = sem("pv_done")
        o_normed = sem("o_normed")
        o_dup = sem("o_dup")
        o_t = sem("o_t")
        ot_hi_made = sem("ot_hi_made")
        ot_split = sem("ot_split")
        proj_done = sem("proj_done")
        gated_done = sem("gated_done")
        x1_done = sem("x1_done")
        x1g_done = sem("x1g_done")

        steps = [(qkv_wt, g * GC, GC, wq_hi, wq_lo, wq_x, wq_y) for g in range(G)]
        steps += [(proj_wt, c * NH, NH, wp_hi, wp_lo, wp_x, wp_y) for c in range(2)]
        biases = ((qkv_b, 3 * D, wq_y), (proj_b, D, wp_y))

        PARTS = (0, 1, 2, 5, 3, 4)

        def run_batches(eng, body):
            body(0, 0, False)
            body(1, 1, False)
            with eng.Fori(2, B - 1) as b:
                body(b, 2, False)
            body(B - 1, 2, True)

        block = ctx.enter_context(nc.Block())

        @block.sync
        def _(sp):
            def load_bias(i):
                src, cols, _ = biases[i]
                if i == 1:
                    sp.wait_ge(bias_split, 1)
                for row in (64, 96):
                    sp.dma_start(bias_stage[row:row + 1, 0:cols], src).then_inc(bias_in, 16)

            def load_stage(n):
                src, c0, cols = steps[n][:3]
                if n >= 2:
                    sp.wait_ge(w_split, n - 1)
                dst, landed = stage[:, n % 2, :, 0:cols], stage_in[n % 2]
                sp.dma_start(dst[:, 0:KF, :], src[0:KF * P, c0:c0 + cols].rearrange("(k p) n -> p k n", p=P)
                             ).then_inc(landed, 16)
                for i in range(2):
                    sp.dma_start(dst[i * TAIL:(i + 1) * TAIL, KF, :], src[KF * P:D, c0:c0 + cols]).then_inc(landed, 16)

            def load_ada(i):
                if i >= 2:
                    sp.wait_ge(ada_done, i - 1)
                cols = slice(PARTS[i] * D, (PARTS[i] + 1) * D)
                dst = ada[:, i % 2, :, :]
                sp.dma_start(dst[:, 0:KF, :], ada_wt[0:KF * P, cols].rearrange("(k p) n -> p k n", p=P)
                             ).then_inc(ada_in[i % 2], 16)
                sp.dma_start(dst[0:TAIL, KF, :], ada_wt[KF * P:D, cols]).then_inc(ada_in[i % 2], 16)
                sp.dma_start(dst[TAIL:TAIL + 1, KF, :], ada_b[:, cols]).then_inc(ada_in[i % 2], 16)

            sp.dma_start(condt[:, 0:KF, :], cond_t[0:KF * P, :].rearrange("(k p) n -> p k n", p=P)
                         ).then_inc(cond_in, 16)
            sp.dma_start(condt[0:TAIL, KF, :], cond_t[KF * P:D, :]).then_inc(cond_in, 16)
            load_ada(0)
            for i, g in enumerate((g1, g2, qg, kg)):
                sp.dma_start(gains[:, i:i + 1], g.partition_broadcast(P)).then_inc(gains_in, 16)
            sp.dma_start(fc2_b_rows, fc2_b.partition_broadcast(B)).then_inc(fc2_b_in, 16)
            sp.dma_start(xin[:, :], x[0]).then_inc(x_in, 16)
            load_ada(1)
            sp.wait_ge(bias_zeroed, 1)
            load_bias(0)
            load_stage(0)
            load_stage(1)
            load_ada(2)
            load_stage(2)
            load_ada(3)
            sp.wait_ge(x_scaled, 1)
            sp.dma_start(xin[:, :], x[1]).then_inc(x_in, 16)
            load_stage(3)
            load_bias(1)
            for n in range(G, len(steps)):
                load_stage(n)
            load_ada(4)
            load_ada(5)

            sp.wait_ge(tanh_done, 2)
            sp.dma_start(gate1_d, gate_rows[0]).then_inc(gates_out, 16)
            sp.dma_start(gate2_d, gate_rows[1]).then_inc(gates_out, 16)
            sp.wait_ge(gb2_done, 1)
            sp.dma_start(gb2_d, gb2_rows).then_inc(gates_out, 16)
            sp.wait_ge(gates_out, 48)

            def batch(b, early, last):
                if not last and early > 0:
                    sp.wait_ge(x_scaled, b + 1)
                    sp.dma_start(xin[:, :], x[bass.ds(b + 1, 1), :, :].rearrange("a t d -> (a t) d")
                                 ).then_inc(x_in, 16)
                if early == 2:
                    finish(b - 2)
                if early >= 1:
                    load_rows(b - 1)

            def load_rows(b):
                if not isinstance(b, int) or b >= 1:
                    sp.wait_ge(x1_done, b)
                    sp.wait_ge(x1g_done, b)
                sp.dma_start(xres[:, :], x[bass.ds(b, 1), :, :].rearrange("a t d -> (a t) d")).then_inc(res_in, 16)
                sp.dma_start(gate1[:, :], gate1_d[bass.ds(b, 1), :].partition_broadcast(P)).then_inc(gate_in, 16)
                sp.dma_start(gb2_all[:, :], gb2_d[bass.ds(b, 1), :].partition_broadcast(P)).then_inc(gate_in, 16)

            def finish(b):
                sp.wait_ge(x1_done, b + 1)
                sp.dma_start(x1_d[bass.ds(b, 1), :, :].rearrange("a t d -> (a t) d"), x1[:, :]).then_inc(x1_out, 16)
                sp.wait_ge(x1g_done, b + 1)
                sp.dma_start(x1g_d[bass.ds(b, 1), :, :].rearrange("a t d -> (a t) d"), x1g[:, :]).then_inc(x1g_out, 16)

            run_batches(sp, batch)
            finish(B - 2)
            load_rows(B - 1)
            finish(B - 1)
            sp.wait_ge(x1_out, 16 * B)
            sp.wait_ge(x1g_out, 16 * B)

        @block.tensor
        def _(pe):
            def ada_part(i, dst):
                pe.wait_ge(ada_in[i % 2], 48 * (i // 2 + 1))
                for n in range(2):
                    for k in range(KT):
                        rows = P if k < KF else TAIL + 1
                        last = nc.tensor.matmul(dst[0:B, n, 0:NH], silut[0:rows, k, :],
                                                ada[0:rows, i % 2, k, n * NH:(n + 1) * NH],
                                                start=(k == 0), stop=(k == KT - 1))
                last.then_inc(ada_done, 1)

            def coef_part(i):
                pe.wait_ge(row_done, i + 1)
                if i >= 1:
                    pe.wait_ge(coef_made, i)
                if i == 2:
                    pe.wait_ge(probs_split, G * B)
                for k in range(KT):
                    last = nc.tensor.transpose(pt_ps[:, k * B:(k + 1) * B],
                                               modrow[:, i % 2, k * P:(k + 1) * P], ident[0:B, 0:B])
                last.then_inc(coef_t, 1)

            pe.wait_ge(silu_made, 1)
            pe.wait_ge(ident_made, 1)
            ada_part(0, q_ps)
            ada_part(1, y_ps)
            coef_part(0)
            coef_part(1)

            def x_transposed(b):
                pe.wait_ge(x_scaled, b + 1)
                if isinstance(b, int) and b == 0:
                    pe.wait_ge(row_done, 2)
                elif isinstance(b, int) and b == 1:
                    pe.wait_ge(tanh_done, 1)
                elif isinstance(b, int) and b == 2:
                    pe.wait_ge(h_made, 2 * KT)
                else:
                    pe.wait_ge(gated_done, b - 2)
                for k in range(KT):
                    last = nc.tensor.transpose(y_flat[:, k * P:(k + 1) * P], xn[:, k * P:(k + 1) * P], ident[:, :])
                last.then_inc(x_t, 1)

            x_transposed(0)
            pe.wait_ge(coef_made, 2)
            pe.wait_ge(ident_r_made, 1)
            pe.wait_ge(constants, 1)
            pe.wait_ge(bias_split, 1)

            passes = [(h_hi, wq_hi, k) for k in range(KF)] + [(h_hi, wq_lo, k) for k in range(KF)]
            passes += [(h_hi, wq_x, KF)] + [(h_lo, wq_hi, k) for k in range(KF)] + [(h_lo, wq_y, KF)]

            def qkv(b, g, first, last_):
                for n in range(first, last_):
                    a, w, k = passes[n]
                    mov = w[:, g * GC:(g + 1) * GC] if k == KF else w[:, k, g * GC:(g + 1) * GC]
                    ins = nc.tensor.matmul(q_ps[:, g % 2, 0:GC], a[:, k * P:(k + 1) * P], mov,
                                           start=(n == 0), stop=(n == 13))
                if last_ == 14:
                    ins.then_inc(qkv_done, 1)

            def stacks_transposed(u):
                for w, dst in ((0, ts_ps), (1, tk_ps)):
                    for i in range(HG):
                        c = w * half + i * ST
                        ins = nc.tensor.transpose(dst[0:ST, i * T:(i + 1) * T].bitcast(F32R),
                                                  stack[:, c:c + ST], ident_r[:, :])
                ins.then_inc(stack_t, 1)

            def scores():
                for i in range(HG):
                    ins = nc.tensor.matmul(ts_ps[:, i * T:(i + 1) * T], qs[0:ST, i * T:(i + 1) * T],
                                           ks[0:ST, i * T:(i + 1) * T], start=True, stop=True)
                ins.then_inc(scores_done, 1)

            def probs_transposed(u):
                for i in range(HG):
                    pe.wait_ge(exp_done, (u - 2) * HG + i + 1)
                    ins = nc.tensor.transpose(pt_ps[:, i * T:(i + 1) * T], pr[:, i * T:(i + 1) * T], ident[:, :])
                ins.then_inc(probs_t, 1)

            def values(g):
                for i in range(HG):
                    out_ = o_ps[:, i * VW:(i + 1) * VW]
                    hi, lo = pt_hi[:, i * T:(i + 1) * T], pt_lo[:, i * T:(i + 1) * T]
                    nc.tensor.matmul(out_, hi, v[:, g, 0, i, :], start=True, stop=False)
                    nc.tensor.matmul(out_[:, 0:HD], hi, v[:, g, 1, i, 0:HD], start=False, stop=False)
                    nc.tensor.matmul(out_[:, 0:HD], hi, v[:, g, 2, i, 0:HD], start=False, stop=False)
                    nc.tensor.matmul(out_, lo, v[:, g, 0, i, :], start=False, stop=False)
                    ins = nc.tensor.matmul(out_[:, 0:HD], lo, v[:, g, 1, i, 0:HD], start=False, stop=True)
                ins.then_inc(pv_done, 1)

            def o_transposed(b):
                pe.wait_ge(o_dup, b + 1)
                if not isinstance(b, int) or b >= 1:
                    pe.wait_ge(gated_done, b)
                pe.wait_ge(h_made, KT * B if isinstance(b, int) and b + 3 > B else (b + 3) * KT)
                for k in range(KT):
                    last = nc.tensor.transpose(y_flat[:, k * P:(k + 1) * P], o[:, k * P:(k + 1) * P], ident[:, :])
                last.then_inc(o_t, 1)

            proj_passes = [(ot_hi, wp_hi, k) for k in range(KF)] + [(ot_hi, wp_lo, k) for k in range(KF)]
            proj_passes += [(ot_hi, wp_x, KF)] + [(ot_lo, wp_hi, k) for k in range(KF)] + [(ot_lo, wp_y, KF)]

            def project(b, first, last_):
                if first == 0:
                    pe.wait_ge(ot_split, b + 1)
                for n in range(first, last_):
                    a, w, k = proj_passes[n]
                    for c in range(2):
                        mov = w[:, c * NH:(c + 1) * NH] if k == KF else w[:, k, c * NH:(c + 1) * NH]
                        ins = nc.tensor.matmul(y_ps[:, c, 0:NH], a[:, k * P:(k + 1) * P], mov,
                                               start=(n == 0), stop=(n == 13))
                if last_ == 14:
                    ins.then_inc(proj_done, 1)

            def slot(b, g, early, run=True, last=False):
                u = 4 * b + g
                one = early > 0 or g >= 1
                two = early > 0 or g >= 2
                three = early > 0 or g >= 3
                if run:
                    if g == 0:
                        pe.wait_ge(h_hi_made, b + 1)
                    if two:
                        pe.wait_ge(qk_scaled, u - 1)
                        pe.wait_ge(v_left, u - 1)
                    qkv(b, g, 0, 9)
                    if g == 0:
                        pe.wait_ge(h_split, b + 1)
                    qkv(b, g, 9, 11)
                if two:
                    if three:
                        pe.wait_ge(probs_split, u - 2)
                    probs_transposed(u)
                if run:
                    qkv(b, g, 11, 14)
                if one and (run or g == 0):
                    pe.wait_ge(qk_lo, u)
                    pe.wait_ge(qk_dup, u)
                    stacks_transposed(u)
                if g == 0 and early == 0:
                    ada_part(2, y_ps)
                if g == 2 and early == 0:
                    pe.wait_ge(h_made, 2 * KT)
                    ada_part(3, y_ps)
                if g == 0 and early >= 2:
                    project(b - 2, 7, 14)
                if g == 1 and run and not last:
                    x_transposed(b + 1)
                if g == 2 and early >= 1:
                    o_transposed(b - 1)
                if g == 3 and early >= 1:
                    project(b - 1, 0, 7)
                if two:
                    pe.wait_ge(probs_split, u - 1)
                    pe.wait_ge(v_parts, u - 1)
                    if three:
                        pe.wait_ge(o_normed, u - 2)
                    values((g + 2) % 4)
                if one and (run or g == 0):
                    pe.wait_ge(stack_read, 2 * u)
                    scores()

            def batch(b, early, last):
                for g in range(G):
                    if early == 0:
                        pe.wait_ge(w_split, g + 1)
                    if early == 1 and g == 3:
                        pe.wait_ge(w_split, len(steps))
                        pe.wait_ge(bias_split, 2)
                    slot(b, g, early, last=last)

            run_batches(pe, batch)
            slot(B, 0, 2, run=False)
            ada_part(4, q_ps)
            slot(B, 1, 2, run=False)
            o_transposed(B - 1)
            pe.wait_ge(row_done, 3)
            ada_part(5, q_ps)
            coef_part(2)
            project(B - 1, 0, 14)
            coef_part(3)

        @block.scalar
        def _(act):
            act.wait_ge(cond_in, 32)
            act.wait_ge(cond_padded, 1)
            nc.scalar.activation(sigm[:, 0, :, :], condt[:, :, :], ACT.Exp, scale=-1.0).then_inc(silu_exp, 1)

            def w_hi(n):
                _, c0, cols, hi, _, x_, y_ = steps[n]
                act.wait_ge(stage_in[n % 2], 48 * (n // 2 + 1))
                src = stage[:, n % 2, :, 0:cols]
                c = slice(c0, c0 + cols)
                nc.scalar.activation(hi[:, :, c], src[:, 0:KF, :], ACT.Copy)
                nc.scalar.activation(x_[:, c], src[:, KF, :], ACT.Copy)
                nc.scalar.activation(y_[0:64, c], src[0:64, KF, :], ACT.Copy).then_inc(w_hi_done, 1)

            def bias_hi(i):
                _, cols, y_ = biases[i]
                act.wait_ge(bias_in, 32 * (i + 1))
                nc.scalar.activation(y_[64:128, :], bias_stage[64:128, 0:cols], ACT.Copy).then_inc(bias_hi_done, 1)

            def tanh_of(n, i):
                act.wait_ge(ada_done, n + 1)
                nc.scalar.activation(gate_rows[i].rearrange("p (a b) -> p a b", a=2), y_ps[0:B, :, 0:NH],
                                     ACT.Tanh).then_inc(tanh_done, 1)

            def square_x(b):
                act.wait_ge(x_in, 16 * b + 16)
                if not isinstance(b, int) or b >= 1:
                    act.wait_ge(x_guarded, b)
                nc.scalar.activation(xsq[:, :], xin[:, :], ACT.Square, accum_out=xss[:, :]).then_inc(x_squared, 1)

            def modulate(b, k):
                nc.scalar.activation(h[:, k * P:(k + 1) * P], y_flat[:, k * P:(k + 1) * P], ACT.Identity,
                                     bias=coef[:, 0, k, bass.ds(b, 1)], scale=coef[:, 1, k, bass.ds(b, 1)]
                                     ).then_inc(h_made, 1)

            def h_hi_of(b):
                act.wait_ge(h_made, (b + 1) * KT)
                if not isinstance(b, int) or b >= 1:
                    act.wait_ge(qkv_done, 4 * b)
                nc.scalar.activation(h_hi[:, :], h[:, :], ACT.Copy).then_inc(h_hi_made, 1)

            square_x(0)
            bias_hi(0)
            w_hi(0)
            act.wait_ge(x_t, 1)
            act.wait_ge(coef_made, 2)
            for k in range(KT):
                modulate(0, k)
            h_hi_of(0)
            w_hi(1)

            def slot(b, g, early, run=True, last=False):
                u = 4 * b + g
                one = early > 0 or g >= 1
                two = early > 0 or g >= 2
                three = early > 0 or g >= 3
                if two:
                    if three:
                        act.wait_ge(probs_t, u - 2)
                    act.wait_ge(max_done, u - 1)
                    for i in range(HG):
                        nc.scalar.activation(pr[:, i * T:(i + 1) * T], ts_ps[:, i * T:(i + 1) * T], ACT.Exp,
                                             bias=neg_max[:, i:i + 1]).then_inc(exp_done, 1)
                if one and (run or g == 0):
                    act.wait_ge(qk_hi, u)
                    nc.scalar.activation(stacked(2), stacked(0), ACT.Copy).then_inc(qk_dup, 1)
                if g == 2 and run and not last:
                    for k in range(3, KT):
                        modulate(b + 1, k)
                if two:
                    act.wait_ge(probs_t, u - 1)
                    if three:
                        act.wait_ge(pv_done, u - 2)
                    nc.scalar.activation(pt_hi[:, :], pt_ps[:, :], ACT.Copy, scale=P_SCALE).then_inc(probs_hi, 1)
                if run:
                    act.wait_ge(qkv_done, u + 1)
                    if one:
                        act.wait_ge(qk_summed, u)
                    nc.scalar.activation(sq[:, :], q_ps[:, g % 2, 0:QK], ACT.Square).then_inc(qk_squared, 1)
                    if early > 0:
                        act.wait_ge(pv_done, u - 3)
                    nc.scalar.activation(v[:, g, 0, :, 0:HD], q_ps[:, g % 2, QK:GC].rearrange("p (a b) -> p a b", b=HD),
                                         ACT.Copy).then_inc(v_first, 1)
                if one and (run or g == 0):
                    act.wait_ge(stack_t, u)
                    if two:
                        act.wait_ge(scores_done, u - 1)
                    nc.scalar.activation(qs[0:ST, :], ts_ps[0:ST, :], ACT.Copy).then_inc(stack_read, 1)
                    nc.scalar.activation(ks[0:ST, :], tk_ps[0:ST, :], ACT.Copy).then_inc(stack_read, 1)
                if early == 0:
                    if g == 0:
                        tanh_of(2, 0)
                    if g == 2:
                        tanh_of(3, 1)
                    if g < 2:
                        w_hi(g + 2)
                    if g == 3:
                        bias_hi(1)
                        w_hi(4)
                        w_hi(5)
                if g == 3 and run and not last:
                    h_hi_of(b + 1)
                if g == 2 and early >= 1:
                    ot_hi_of(b - 1)
                if g == 0 and run and not last:
                    square_x(b + 1)
                if g == 1 and run and not last:
                    act.wait_ge(x_t, b + 2)
                    act.wait_ge(h_split, b + 1)
                    for k in range(3):
                        modulate(b + 1, k)

            def ot_hi_of(b):
                act.wait_ge(o_t, b + 1)
                if not isinstance(b, int) or b >= 1:
                    act.wait_ge(proj_done, b)
                nc.scalar.activation(ot_hi[:, :], y_flat[:, 0:DX], ACT.Copy).then_inc(ot_hi_made, 1)

            def batch(b, early, last):
                for g in range(G):
                    slot(b, g, early, last=last)

            run_batches(act, batch)
            slot(B, 0, 2, run=False)
            slot(B, 1, 2, run=False)
            ot_hi_of(B - 1)

        @block.vector
        def _(dve):
            nc.vector.memset(condt[TAIL:P, KF, :], 0.0).then_inc(cond_padded, 1)
            nc.vector.memset(silut[:, :, :], 1.0).then_inc(const_step, 1)
            nc.vector.memset(bias_stage[:, :], 0.0).then_inc(bias_zeroed, 1)
            for t in (h_lo, ot_lo):
                nc.vector.memset(t[64:128, KF * P:DX].bitcast(F32), 0.0).then_inc(const_step, 1)
            dve.wait_ge(const_step, 3)
            for t in (h_lo, ot_lo):
                for row in (64, 96):
                    nc.vector.memset(t[row:row + 1, KF * P:DX].bitcast(F32), 1.0)
            nc.vector.memset(minus_half[:, :], -0.5)
            nc.vector.memset(zero[:, :], 0.0)
            nc.vector.memset(v[:, :, 0, :, HD:HD + 1], 1.0).then_inc(constants, 1)
            dve.wait_ge(silu_exp, 1)
            nc.vector.tensor_scalar(sigm[:, 1, :, :], sigm[:, 0, :, :], 1.0, None, ALU.add).then_inc(silu_step, 1)
            dve.wait_ge(silu_step, 1)
            nc.vector.reciprocal(sigm[:, 0, :, :], sigm[:, 1, :, :]).then_inc(silu_step, 1)
            dve.wait_ge(silu_step, 2)
            nc.vector.tensor_tensor(silut[:, 0:KF, :], condt[:, 0:KF, :], sigm[:, 0, 0:KF, :], ALU.mult)
            nc.vector.tensor_tensor(silut[0:TAIL, KF, :], condt[0:TAIL, KF, :], sigm[0:TAIL, 0, KF, :],
                                    ALU.mult).then_inc(silu_made, 1)
            dve.wait_ge(ident_made, 1)
            nc.vector.tensor_copy(ident_r[:, :], ident[:, :]).then_inc(ident_r_made, 1)
            dve.wait_ge(gains_in, 64)
            nc.vector.tensor_scalar(gscale[:, :], gains[:, 0:2], float(D) ** 0.5, None, ALU.mult).then_inc(gains_made, 1)
            nc.vector.tensor_copy(qk_gain[:, 0, :], gains[:, 2:3].to_broadcast([P, HG]))
            nc.vector.tensor_scalar(qk_gain[:, 1, :], gains[:, 3:4].to_broadcast([P, HG]), float(HD) ** 0.5, None,
                                    ALU.mult).then_inc(gains_made, 1)
            dve.wait_ge(gains_made, 2)

            def w_lo(n):
                _, c0, cols, hi, lo, x_, _ = steps[n]
                dve.wait_ge(w_hi_done, n + 1)
                src = stage[:, n % 2, :, 0:cols]
                c = slice(c0, c0 + cols)
                nc.vector.tensor_tensor(lo[:, :, c], src[:, 0:KF, :], hi[:, :, c].bitcast(F32), ALU.subtract)
                nc.vector.tensor_tensor(x_[64:128, c], src[64:128, KF, :], x_[64:128, c].bitcast(F32), ALU.subtract
                                        ).then_inc(w_split, 1)

            def bias_lo(i):
                _, cols, y_ = biases[i]
                dve.wait_ge(bias_hi_done, i + 1)
                nc.vector.tensor_tensor(y_[96:128, :], bias_stage[96:128, 0:cols], y_[96:128, :].bitcast(F32),
                                        ALU.subtract).then_inc(bias_split, 1)

            def guard_x(b):
                dve.wait_ge(x_squared, b + 1)
                nc.vector.tensor_scalar(xr[:, 0:1], xss[:, :], EPS2, None, ALU.max).then_inc(x_guarded, 1)

            def scale_x(b):
                dve.wait_ge(x_rnorm, b + 1)
                if not isinstance(b, int) or b >= 1:
                    dve.wait_ge(x_t, b)
                nc.vector.tensor_scalar(xn[:, 0:D], xin[:, :], xr[:, 1:2], None, ALU.mult)
                nc.vector.tensor_scalar(xn[:, D:DX], xin[:, KF * P:D], xr[:, 1:2], None, ALU.mult).then_inc(x_scaled, 1)

            def ada_row(i, n, src_ps):
                dve.wait_ge(ada_done, n + 1)
                if i >= 2:
                    dve.wait_ge(coef_t, i - 1)
                src = src_ps[0:B, :, :]
                dst = modrow[:, i % 2, :]
                pieces = ((dst[:, 0:D].rearrange("p (a b) -> p a b", a=2), src[:, :, 0:NH]),
                          (dst[:, D:DX], src[:, 1, NH - TAIL:NH]))
                for to, of in pieces:
                    if i % 2 == 0:
                        ins = nc.vector.tensor_copy(to, of)
                    else:
                        ins = nc.vector.tensor_scalar(to, of, 1.0, gscale[0:B, i // 2:i // 2 + 1], ALU.add, ALU.mult)
                ins.then_inc(row_done, 1)

            def coef_out(i):
                dve.wait_ge(coef_t, i + 1)
                nc.vector.tensor_copy(coef[:, i, :, :], pt_ps[:, 0:KT * B].rearrange("p (k b) -> p k b", k=KT)
                                      ).then_inc(coef_made, 1)

            def h_lo_of(b):
                dve.wait_ge(h_hi_made, b + 1)
                nc.vector.tensor_tensor(h_lo[:, 0:KF * P], h[:, 0:KF * P], h_hi[:, 0:KF * P].bitcast(F32), ALU.subtract)
                nc.vector.tensor_tensor(h_lo[0:64, KF * P:DX], h[0:64, KF * P:DX], h_hi[0:64, KF * P:DX].bitcast(F32),
                                        ALU.subtract).then_inc(h_split, 1)

            guard_x(0)
            scale_x(0)
            ada_row(0, 0, q_ps)
            ada_row(1, 1, y_ps)
            for i in range(2):
                coef_out(i)
            bias_lo(0)
            w_lo(0)
            h_lo_of(0)
            w_lo(1)

            def slot(b, g, early, run=True, last=False):
                u = 4 * b + g
                one = early > 0 or g >= 1
                two = early > 0 or g >= 2
                if one and (run or g == 0):
                    dve.wait_ge(qk_rnorm, u)
                    nc.vector.tensor_tensor(qk[:, :, :, :].rearrange("p a b c -> p (a b) c"),
                                            q_ps[:, (g + 1) % 2, 0:QK].rearrange("p (a c) -> p a c", c=HD),
                                            rqk[:, :].unsqueeze(2).to_broadcast([P, 2 * HG, HD]),
                                            ALU.mult).then_inc(qk_scaled, 1)
                    dve.wait_ge(qk_scaled, u)
                    if two:
                        dve.wait_ge(stack_t, u - 1)
                    nc.vector.tensor_copy(stacked(0), qk[:, :, :, :]).then_inc(qk_hi, 1)
                    dve.wait_ge(qk_hi, u)
                    nc.vector.tensor_tensor(stacked(1), qk[:, :, :, :], stacked(0).bitcast(F32), ALU.subtract
                                            ).then_inc(qk_lo, 1)
                if g == 1 and run and not last:
                    scale_x(b + 1)
                if g == 1 and early >= 2:
                    gate_of(b - 2)
                if g == 3 and early >= 1:
                    ot_lo_of(b - 1)
                if two:
                    dve.wait_ge(probs_hi, u - 1)
                    nc.vector.scalar_tensor_tensor(out=pt_lo[:, :], in0=pt_ps[:, :], scalar=P_SCALE, in1=pt_hi[:, :],
                                                   op0=ALU.mult, op1=ALU.subtract).then_inc(probs_split, 1)
                if run:
                    dve.wait_ge(qk_squared, u + 1)
                    if one:
                        dve.wait_ge(qk_pow, u)
                    nc.vector.tensor_reduce(ss[:, :], sq[:, :].rearrange("p (a c) -> p a c", c=HD), AX_X, ALU.add
                                            ).then_inc(qk_summed, 1)
                    dve.wait_ge(qk_summed, u + 1)
                    nc.vector.tensor_scalar(ssg[:, :], ss[:, :], EPS2, None, ALU.max).then_inc(qk_guarded, 1)
                    dve.wait_ge(v_first, u + 1)
                    if one:
                        dve.wait_ge(v_parts, u)
                    nc.vector.tensor_tensor(v_rest[:, :, :], q_ps[:, g % 2, QK:GC].rearrange("p (a b) -> p a b", b=HD),
                                            v[:, g, 0, :, 0:HD], ALU.subtract).then_inc(v_left, 1)
                if early == 0:
                    if g < 2:
                        w_lo(g + 2)
                    if g == 2:
                        dve.wait_ge(tanh_done, 2)
                        dve.wait_ge(fc2_b_in, 16)
                        nc.vector.tensor_tensor(gb2_rows, gate_rows[1], fc2_b_rows, ALU.mult).then_inc(gb2_done, 1)
                    if g == 3:
                        bias_lo(1)
                        w_lo(4)
                        w_lo(5)
                if g == 3 and run and not last:
                    h_lo_of(b + 1)
                if g == 0 and run and not last:
                    guard_x(b + 1)
                if two:
                    gg = (g + 2) % 4
                    dve.wait_ge(pv_done, u - 1)
                    oh = o_ps[:, 0:HG * VW].rearrange("p (a b) -> p a b", b=VW)
                    nc.vector.reciprocal(rden[:, :].unsqueeze(2), oh[:, :, HD:VW]).then_inc(o_rden, 1)
                    dve.wait_ge(o_rden, u - 1)
                    if gg == 0 and not (isinstance(b, int) and b == 0):
                        dve.wait_ge(o_t, b)
                    nc.vector.tensor_tensor(o[:, gg * HG * HD:(gg + 1) * HG * HD].rearrange("p (a b) -> p a b", b=HD),
                                            oh[:, :, 0:HD], rden[:, :].unsqueeze(2).to_broadcast([P, HG, HD]),
                                            ALU.mult).then_inc(o_normed, 1)
                    if gg == 3:
                        dve.wait_ge(o_normed, u - 1)
                        nc.vector.tensor_copy(o[:, D:DX], o[:, KF * P:D]).then_inc(o_dup, 1)
                if one and (run or g == 0):
                    dve.wait_ge(scores_done, u)
                    if two:
                        dve.wait_ge(exp_done, HG * (u - 1))
                    nc.vector.tensor_reduce(neg_max[:, :], ts_ps[:, :].rearrange("p (a b) -> p a b", b=T), AX_X, ALU.max,
                                            negate=True).then_inc(max_done, 1)

            def ot_lo_of(b):
                dve.wait_ge(ot_hi_made, b + 1)
                if not isinstance(b, int) or b >= 1:
                    dve.wait_ge(proj_done, b)
                nc.vector.tensor_tensor(ot_lo[:, 0:KF * P], y_flat[:, 0:KF * P], ot_hi[:, 0:KF * P].bitcast(F32),
                                        ALU.subtract)
                nc.vector.tensor_tensor(ot_lo[0:64, KF * P:DX], y_flat[0:64, KF * P:DX],
                                        ot_hi[0:64, KF * P:DX].bitcast(F32), ALU.subtract).then_inc(ot_split, 1)

            def gate_of(b):
                dve.wait_ge(proj_done, b + 1)
                dve.wait_ge(gate_in, 32 * b + 32)
                if not isinstance(b, int) or b >= 1:
                    dve.wait_ge(x1_done, b)
                nc.vector.tensor_tensor(gated[:, :].rearrange("p (a b) -> p a b", a=2), y_half,
                                        gate1[:, :].rearrange("p (a b) -> p a b", a=2), ALU.mult
                                        ).then_inc(gated_done, 1)

            def batch(b, early, last):
                for g in range(G):
                    slot(b, g, early, last=last)

            run_batches(dve, batch)
            slot(B, 0, 2, run=False)
            ada_row(2, 4, q_ps)
            slot(B, 1, 2, run=False)
            ada_row(3, 5, q_ps)
            ot_lo_of(B - 1)
            coef_out(2)
            gate_of(B - 1)
            coef_out(3)

        @block.gpsimd
        def _(pool):
            nc.gpsimd.memset(ident[:, :], 0.0).then_inc(ident_zeroed, 1)
            pool.wait_ge(ident_zeroed, 1)
            nc.gpsimd.affine_select(out=ident[:, :], in_=ident[:, :], compare_op=ALU.not_equal, fill=1.0, base=0,
                                    pattern=[[-1, P]], channel_multiplier=1).then_inc(ident_made, 1)

            def x_rnorm_of(b):
                pool.wait_ge(x_guarded, b + 1)
                nc.gpsimd.tensor_tensor(xr[:, 1:2], xr[:, 0:1], minus_half[:, 0:1], ALU.pow).then_inc(x_rnorm, 1)

            def qk_rnorm_of(u):
                pool.wait_ge(qk_guarded, u + 1)
                nc.gpsimd.tensor_tensor(rpow[:, :], ssg[:, :], minus_half[:, :], ALU.pow).then_inc(qk_pow, 1)
                pool.wait_ge(qk_pow, u + 1)
                if not isinstance(u, int) or u >= 1:
                    pool.wait_ge(qk_scaled, u)
                nc.gpsimd.tensor_tensor(rqk[:, :], rpow[:, :], qk_gain[:, :, :].rearrange("p a b -> p (a b)"),
                                        ALU.mult).then_inc(qk_rnorm, 1)

            def v_rest_split(b, g):
                u = 4 * b + g
                pool.wait_ge(v_left, u + 1)
                if not isinstance(b, int) or b >= 1:
                    pool.wait_ge(pv_done, u - 3)
                nc.gpsimd.tensor_tensor(v[:, g, 1, :, 0:HD], v_rest[:, :, :],
                                        zero[:, :].unsqueeze(2).to_broadcast([P, HG, HD]), ALU.add).then_inc(v_second, 1)
                pool.wait_ge(v_second, u + 1)
                nc.gpsimd.tensor_tensor(v[:, g, 2, :, 0:HD], v_rest[:, :, :], v[:, g, 1, :, 0:HD], ALU.subtract
                                        ).then_inc(v_parts, 1)

            def x1_of(b):
                pool.wait_ge(gated_done, b + 1)
                pool.wait_ge(res_in, 16 * b + 16)
                if not isinstance(b, int) or b >= 1:
                    pool.wait_ge(x1_out, 16 * b)
                nc.gpsimd.tensor_tensor(x1[:, :], gated[:, :], xres[:, :], ALU.add).then_inc(x1_done, 1)
                pool.wait_ge(x1_done, b + 1)
                pool.wait_ge(gate_in, 32 * b + 32)
                if not isinstance(b, int) or b >= 1:
                    pool.wait_ge(x1g_out, 16 * b)
                nc.gpsimd.tensor_tensor(x1g[:, :], x1[:, :], gb2_all[:, :], ALU.add).then_inc(x1g_done, 1)

            pool.wait_ge(gains_made, 2)
            pool.wait_ge(constants, 1)
            x_rnorm_of(0)

            def batch(b, early, last):
                for g in range(G):
                    qk_rnorm_of(4 * b + g)
                    if g == 0 and not last:
                        x_rnorm_of(b + 1)
                    v_rest_split(b, g)
                    if g == 1 and early >= 2:
                        x1_of(b - 2)

            run_batches(pool, batch)
            x1_of(B - 2)
            x1_of(B - 1)


def mlp_stage(nc, fc1_wt, fc1_bt, fc2_wt, gate2_d, x1_d, x1g_d, out, coef, ident, minus_half):
    with ExitStack() as ctx:
        def sb(name, shape, dt):
            return ctx.enter_context(nc.sbuf_tensor(name, shape, dt))

        def ps(name, shape):
            return ctx.enter_context(nc.psum_tensor(name, shape, F32))

        def sem(name):
            return ctx.enter_context(nc.semaphore(name))

        w1_hi = sb("w1_hi", [P, KF, F], F32R)
        w1_lo = sb("w1_lo", [P, KF, F], F32R)
        w1_x = sb("w1_x", [P, F], F32R)
        w2_hi = sb("w2_hi", [P, MT, D], F32R)
        w2_lo = sb("w2_lo", [P, MT, D], F32R)
        stage1 = sb("stage1", [P, 2, KT, P], F32)
        stage2 = sb("stage2", [P, 2, D], F32)
        fc1_b = sb("fc1_b", [P, MT], F32)
        xin = sb("x1_in", [P, DX], F32)
        xss = sb("x1_ss", [P, 1], F32)
        xr = sb("x1_r", [P, 2], F32)
        h = sb("h2", [P, KT, 2, T], F32)
        h_hi = sb("h2_hi", [P, KT, 2, T], F32R)
        h_lo = sb("h2_lo", [P, KT, 2, T], F32R)
        act_f = sb("act_f", [P, 2 * T], F32)
        act_hi = sb("act_hi", [P, 2, 2 * T], F32R)
        act_lo = sb("act_lo", [P, 2, 2 * T], F32R)
        res = sb("res", [P, 2, D], F32)
        gate = sb("gate", [P, 2, D], F32)

        z_ps = ps("z_ps", [P, 2, 2, BANK])
        f_ps = ps("f_ps", [P, 2, BANK])
        x_ps = ps("x_ps", [P, 2, BANK])
        x_flat = x_ps[:, :, :].rearrange("p a b -> p (a b)")

        w1_in = [sem(f"w1_in{i}") for i in range(2)]
        w2_in = [sem(f"w2_in{i}") for i in range(2)]
        b1_in = sem("b1_in")
        x_in = sem("x1_landed")
        res_in = sem("res_landed")
        gate_in = sem("gate_landed")
        out_done = sem("out_done")
        w_hi_made = sem("w12_hi_made")
        w_split = sem("w12_split")
        x_squared = sem("x1_squared")
        x_guarded = sem("x1_guarded")
        x_rnorm = sem("x1_rnorm")
        x_dup = sem("x1_dup")
        x_scaled = sem("x1_scaled")
        x_t = sem("x1_t")
        h_made = sem("h2_made")
        h_hi_made = sem("h2_hi_made")
        h_split = sem("h2_split")
        f_done = sem("f_done")
        gelu_done = sem("gelu_done")
        act_hi_made = sem("act_hi_made")
        act_split = sem("act_split")
        z_step = sem("z_step")
        gated = sem("mlp_gated")
        summed = sem("mlp_summed")

        def run_pairs(eng, pair):
            pair(0, True, False)
            with eng.Fori(1, PAIRS - 1) as p:
                pair(p, False, False)
            pair(PAIRS - 1, False, True)

        SQUARE_AT, TRANSPOSE_AT, MODULATE_AT = (2, 9), (5, 12), (6, 13)

        block = ctx.enter_context(nc.Block())

        @block.sync
        def _(sp):
            def load_x(b):
                sp.dma_start(xin[:, 0:D], x1_d[bass.ds(b, 1), :, :].rearrange("a t d -> (a t) d")).then_inc(x_in, 16)

            def load_rows(p):
                if not isinstance(p, int) or p >= 1:
                    sp.wait_ge(out_done, 32 * p)
                for i in range(2):
                    sp.dma_start(res[:, i, :], x1g_d[bass.ds(2 * p + i, 1), :, :].rearrange("a t d -> (a t) d")
                                 ).then_inc(res_in, 16)
                    sp.dma_start(gate[:, i, :], gate2_d[bass.ds(2 * p + i, 1), :].partition_broadcast(P)
                                 ).then_inc(gate_in, 16)

            def load_w(m):
                if m >= 2:
                    sp.wait_ge(w_split, m - 1)
                cols = slice(m * P, (m + 1) * P)
                dst = stage1[:, m % 2, :, :]
                sp.dma_start(dst[:, 0:KF, :], fc1_wt[0:KF * P, cols].rearrange("(k p) n -> p k n", p=P)
                             ).then_inc(w1_in[m % 2], 16)
                for i in range(2):
                    sp.dma_start(dst[i * TAIL:(i + 1) * TAIL, KF, :], fc1_wt[KF * P:D, cols]).then_inc(w1_in[m % 2], 16)
                sp.dma_start(stage2[:, m % 2, :], fc2_wt[m * P:(m + 1) * P, :]).then_inc(w2_in[m % 2], 16)

            load_x(0)
            sp.dma_start(fc1_b[:, :], fc1_bt).then_inc(b1_in, 16)
            load_w(0)
            load_w(1)
            sp.wait_ge(x_t, 1)
            load_x(1)
            load_w(2)
            load_rows(0)
            for m in range(3, MT):
                load_w(m)
                for i in range(2):
                    if m == 3 + 5 * i:
                        sp.wait_ge(x_t, 2 + i)
                        load_x(2 + i)

            def pair(p, ahead):
                for i in ahead:
                    sp.wait_ge(x_t, 2 * p + i)
                    load_x(2 * p + i)
                for i in range(2):
                    sp.wait_ge(summed, 2 * p + 1 + i)
                    sp.dma_start(out[bass.ds(2 * p + i, 1), :, :].rearrange("a t d -> (a t) d"), res[:, i, :]
                                 ).then_inc(out_done, 16)
                if ahead:
                    load_rows(p + 1)

            pair(0, (4,))
            with sp.Fori(1, PAIRS - 2) as p:
                pair(p, (3, 4))
            pair(PAIRS - 2, (3,))
            pair(PAIRS - 1, ())
            sp.wait_ge(out_done, 32 * PAIRS)

        @block.tensor
        def _(pe):
            def x_transposed(b):
                pe.wait_ge(x_scaled, b + 1)
                if not isinstance(b, int) or b >= 1:
                    pe.wait_ge(h_made, KT * b)
                for k in range(KT):
                    last = nc.tensor.transpose(x_flat[:, k * P:(k + 1) * P], xin[:, k * P:(k + 1) * P], ident[:, :])
                last.then_inc(x_t, 1)

            hi_passes = [(w1_hi, h_hi, k) for k in range(KF)] + [(w1_lo, h_hi, k) for k in range(KF)] + [(w1_x, h_hi, KF)]
            lo_passes = [(w1_hi, h_lo, k) for k in range(KF)] + [(w1_x, h_lo, KF)]
            passes = hi_passes + lo_passes

            def fc1(p, m):
                for n, (w, a, k) in enumerate(passes):
                    if m == 0 and n == len(hi_passes):
                        pe.wait_ge(h_split, p + 1)
                    cols = slice(m * P, (m + 1) * P)
                    ins = nc.tensor.matmul(f_ps[:, m % 2, 0:2 * T], w[:, cols] if k == KF else w[:, k, cols],
                                           a[:, k, :, :], start=(n == 0), stop=(n == len(passes) - 1))
                ins.then_inc(f_done, 1)

            def fc2(m):
                for i in range(2):
                    tok = slice(i * T, (i + 1) * T)
                    for n, (a, w) in enumerate(((act_hi, w2_hi), (act_hi, w2_lo), (act_lo, w2_hi))):
                        for c in range(2):
                            ins = nc.tensor.matmul(z_ps[:, i, c, 0:NH], a[:, m % 2, tok], w[:, m, c * NH:(c + 1) * NH],
                                                   start=(m == 0 and n == 0), stop=(m == MT - 1 and n == 2))
                ins.then_inc(z_step, 1)

            def pair(p, first, last):
                pe.wait_ge(h_hi_made, p + 1)
                for m in range(MT + 1):
                    if m < MT:
                        if first:
                            pe.wait_ge(w_split, m + 1)
                        if not (first and m < 2):
                            pe.wait_ge(gelu_done, p * MT + m - 1)
                        fc1(p, m)
                    if m >= 1:
                        if m == 1 and not first:
                            pe.wait_ge(gated, 2 * p)
                        pe.wait_ge(act_split, p * MT + m)
                        fc2(m - 1)
                    if not last:
                        for i in range(2):
                            if m == TRANSPOSE_AT[i]:
                                x_transposed(2 * p + 2 + i)

            x_transposed(0)
            x_transposed(1)
            run_pairs(pe, pair)

        @block.scalar
        def _(act):
            def square_x(b):
                act.wait_ge(x_in, 16 * b + 16)
                if not isinstance(b, int) or b >= 1:
                    act.wait_ge(x_guarded, b)
                    act.wait_ge(h_made, KT * b)
                nc.scalar.activation(x_flat[:, 0:D], xin[:, 0:D], ACT.Square, accum_out=xss[:, :]).then_inc(x_squared, 1)

            def modulate(b, i):
                act.wait_ge(x_t, b + 1)
                for k in range(KT):
                    nc.scalar.activation(h[:, k, i, :], x_flat[:, k * P:(k + 1) * P], ACT.Identity,
                                         bias=coef[:, 2, k, bass.ds(b, 1)], scale=coef[:, 3, k, bass.ds(b, 1)]
                                         ).then_inc(h_made, 1)

            def h_hi_of(p):
                act.wait_ge(h_made, (p + 1) * (2 * KT))
                if not isinstance(p, int) or p >= 1:
                    act.wait_ge(f_done, p * MT)
                nc.scalar.activation(h_hi[:, :, :, :], h[:, :, :, :], ACT.Copy).then_inc(h_hi_made, 1)

            def w_hi(m):
                act.wait_ge(w1_in[m % 2], 48 * (m // 2 + 1))
                act.wait_ge(w2_in[m % 2], 16 * (m // 2 + 1))
                cols = slice(m * P, (m + 1) * P)
                nc.scalar.activation(w1_hi[:, :, cols], stage1[:, m % 2, 0:KF, :], ACT.Copy)
                nc.scalar.activation(w1_x[:, cols], stage1[:, m % 2, KF, :], ACT.Copy)
                nc.scalar.activation(w2_hi[:, m, :], stage2[:, m % 2, :], ACT.Copy).then_inc(w_hi_made, 1)

            square_x(0)
            w_hi(0)
            modulate(0, 0)
            square_x(1)
            w_hi(1)
            modulate(1, 1)
            h_hi_of(0)
            act.wait_ge(b1_in, 16)

            def pair(p, first, last):
                for m in range(MT):
                    if first and m + 2 < MT:
                        w_hi(m + 2)
                    act.wait_ge(f_done, p * MT + m + 1)
                    if not (first and m == 0):
                        act.wait_ge(act_split, p * MT + m)
                    nc.scalar.activation(act_f[:, :], f_ps[:, m % 2, 0:2 * T], ACT.Gelu_apprx_tanh,
                                         bias=fc1_b[:, m:m + 1]).then_inc(gelu_done, 1)
                    if not last:
                        for i in range(2):
                            if m == SQUARE_AT[i]:
                                square_x(2 * p + 2 + i)
                            if m == MODULATE_AT[i]:
                                act.wait_ge(x_t, 2 * p + 3 + i)
                                for k in range(KT):
                                    nc.scalar.activation(
                                        h[:, k, i, :], x_flat[:, k * P:(k + 1) * P], ACT.Identity,
                                        bias=coef[:, 2, k, bass.ds(2 * p + 2 + i, 1)],
                                        scale=coef[:, 3, k, bass.ds(2 * p + 2 + i, 1)]).then_inc(h_made, 1)
                if not last:
                    h_hi_of(p + 1)

            run_pairs(act, pair)

        @block.vector
        def _(dve):
            def guard_x(b):
                dve.wait_ge(x_squared, b + 1)
                nc.vector.tensor_scalar(xr[:, 0:1], xss[:, :], EPS2, None, ALU.max).then_inc(x_guarded, 1)

            def scale_x(b):
                dve.wait_ge(x_rnorm, b + 1)
                nc.vector.tensor_scalar(xin[:, D:DX], xin[:, KF * P:D], xr[:, 1:2], None, ALU.mult).then_inc(x_dup, 1)
                dve.wait_ge(x_dup, b + 1)
                nc.vector.tensor_scalar(xin[:, 0:D], xin[:, 0:D], xr[:, 1:2], None, ALU.mult).then_inc(x_scaled, 1)

            def h_lo_of(p):
                dve.wait_ge(h_hi_made, p + 1)
                nc.vector.tensor_tensor(h_lo[:, :, :, :], h[:, :, :, :], h_hi[:, :, :, :].bitcast(F32), ALU.subtract
                                        ).then_inc(h_split, 1)

            def w_lo(m):
                dve.wait_ge(w_hi_made, m + 1)
                cols = slice(m * P, (m + 1) * P)
                s = m % 2
                nc.vector.tensor_tensor(w1_lo[:, :, cols], stage1[:, s, 0:KF, :], w1_hi[:, :, cols].bitcast(F32), ALU.subtract)
                nc.vector.tensor_tensor(w1_x[64:128, cols], stage1[64:128, s, KF, :], w1_x[64:128, cols].bitcast(F32),
                                        ALU.subtract)
                nc.vector.tensor_tensor(w2_lo[:, m, :], stage2[:, s, :], w2_hi[:, m, :].bitcast(F32), ALU.subtract
                                        ).then_inc(w_split, 1)

            guard_x(0)
            scale_x(0)
            w_lo(0)
            guard_x(1)
            scale_x(1)
            w_lo(1)
            h_lo_of(0)

            def pair(p, first, last):
                for m in range(MT):
                    if first and m + 2 < MT:
                        w_lo(m + 2)
                    if not (first and m < 2):
                        dve.wait_ge(z_step, p * MT + m - 1)
                    dve.wait_ge(gelu_done, p * MT + m + 1)
                    nc.vector.tensor_copy(act_hi[:, m % 2, :], act_f[:, :]).then_inc(act_hi_made, 1)
                    dve.wait_ge(act_hi_made, p * MT + m + 1)
                    nc.vector.tensor_tensor(act_lo[:, m % 2, :], act_f[:, :], act_hi[:, m % 2, :].bitcast(F32),
                                            ALU.subtract).then_inc(act_split, 1)
                    if not last:
                        for i in range(2):
                            if m == SQUARE_AT[i]:
                                guard_x(2 * p + 2 + i)
                            if m == SQUARE_AT[i] + 1:
                                scale_x(2 * p + 2 + i)
                if not last:
                    h_lo_of(p + 1)
                dve.wait_ge(z_step, p * MT + MT)
                for i in range(2):
                    dve.wait_ge(gate_in, 32 * p + 32)
                    nc.vector.tensor_tensor(gate[:, i, :].rearrange("p (a b) -> p a b", a=2), z_ps[:, i, :, 0:NH],
                                            gate[:, i, :].rearrange("p (a b) -> p a b", a=2), ALU.mult
                                            ).then_inc(gated, 1)

            run_pairs(dve, pair)

        @block.gpsimd
        def _(pool):
            def x_rnorm_of(b):
                pool.wait_ge(x_guarded, b + 1)
                nc.gpsimd.tensor_tensor(xr[:, 1:2], xr[:, 0:1], minus_half[:, 0:1], ALU.pow).then_inc(x_rnorm, 1)

            x_rnorm_of(0)
            x_rnorm_of(1)

            def pair(p, first, last):
                if not last:
                    x_rnorm_of(2 * p + 2)
                    x_rnorm_of(2 * p + 3)
                for i in range(2):
                    pool.wait_ge(gated, 2 * p + 1 + i)
                    pool.wait_ge(res_in, 32 * p + 32)
                    nc.gpsimd.tensor_tensor(res[:, i, :], res[:, i, :], gate[:, i, :], ALU.add).then_inc(summed, 1)

            run_pairs(pool, pair)


def kernel(**inputs):
    import numpy as np
    import concourse.bacc as bacc
    from concourse import mybir as mb
    from concourse.bass_utils import run_bass_kernel_spmd

    def rows(name):
        return np.asarray(inputs[name]).reshape(1, -1)

    by_unit = lambda a: np.asarray(a).reshape(3, G, HG * HD, -1).transpose(1, 0, 2, 3).reshape(3 * D, -1)
    arrays = {
        "x": np.asarray(inputs["x"]),
        "cond_t": np.asarray(inputs["cond_1152"]).T,
        "g1": rows("L0_cond_g1"), "g2": rows("L0_cond_g2"),
        "qkv_wt": by_unit(inputs["L0_cond_qkv_w"]).T,
        "qkv_b": by_unit(inputs["L0_cond_qkv_b"]).T,
        "qg": rows("L0_cond_qg"), "kg": rows("L0_cond_kg"),
        "proj_wt": np.asarray(inputs["L0_cond_proj_w"]).T, "proj_b": rows("L0_cond_proj_b"),
        "fc1_wt": np.asarray(inputs["L0_cond_fc1_w"]).T,
        "fc1_bt": np.asarray(inputs["L0_cond_fc1_b"]).reshape(MT, P).T,
        "fc2_wt": np.asarray(inputs["L0_cond_fc2_w"]).T, "fc2_b": rows("L0_cond_fc2_b"),
        "ada_wt": np.asarray(inputs["L0_cond_ada_w"]).T, "ada_b": rows("L0_cond_ada_b"),
    }
    arrays = {name: np.ascontiguousarray(a) for name, a in arrays.items()}
    nc = bacc.Bacc("TRN2", target_bir_lowering=False, num_devices=1)
    args = {name: nc.dram_tensor(name + "_dram", a.shape, mb.dt.from_np(a.dtype), kind="ExternalInput").ap()
            for name, a in arrays.items()}
    out = nc.dram_tensor("out_dram", (B, T, D), mb.dt.float32, kind="ExternalOutput").ap()
    build(nc, out=out, **args)
    ran = run_bass_kernel_spmd(nc, [{name + "_dram": a for name, a in arrays.items()}], core_ids=[0])
    return ran.results[0]["out_dram"]
```

```python
from contextlib import ExitStack

import concourse.bass as bass
from concourse import mybir

F32 = mybir.dt.float32
F32R = mybir.dt.float32r
F16 = mybir.dt.float16
BF16 = mybir.dt.bfloat16
ALU = mybir.AluOpType
ACT = mybir.ActivationFunctionType
AX_X = mybir.AxisListType.X

P = 128
B = 32
T = 128
D = 576
H = 16
HD = D // H
F = 4 * D
KF = D // P
TAIL = D - KF * P
KT = KF + 1
DX = KT * P
HG = 4
G = H // HG
GC = 3 * HG * HD
QK = 2 * HG * HD
NH = D // 2
ST = 3 * HD
VW = 3 * HD + 2
P_SCALE = 2.0 ** 15
MT = F // P
PAIRS = B // 2
BANK = 512
EARLY_TILES = 2
EPS2 = 1e-24


def build(nc, x, cond_t, g1, g2, qkv_wt, qkv_b, qg, kg, proj_wt, proj_b,
          fc1_wt, fc1_bt, fc2_wt, fc2_b, ada_wt, ada_b, out):
    gate1_d = nc.dram_tensor("gate_msa_rows", [B, D], F32, kind="Internal").ap()
    gate2_d = nc.dram_tensor("gate_mlp_rows", [B, D], F32, kind="Internal").ap()
    gb2_d = nc.dram_tensor("gated_fc2_bias_rows", [B, D], F32, kind="Internal").ap()
    x1_d = nc.dram_tensor("x_after_attention", [B, T, D], F32, kind="Internal").ap()
    x1g_d = nc.dram_tensor("x_after_attention_biased", [B, T, D], F32, kind="Internal").ap()

    with ExitStack() as whole:
        def keep_sb(name, shape, dt):
            return whole.enter_context(nc.sbuf_tensor(name, shape, dt))

        coef = keep_sb("coef", [P, 4, KT, B], F32)
        ident = keep_sb("ident", [P, P], F32)
        minus_half = keep_sb("minus_half", [P, 2 * HG], F32)
        h2_hi = keep_sb("h2_hi", [P, KT, 2, T], F32R)
        h2_lo = keep_sb("h2_lo", [P, KT, 2, T], F32R)
        first_tiles = mlp_weights(nc, keep_sb, "first", EARLY_TILES)
        attention_stage(nc, x, cond_t, g1, g2, qkv_wt, qkv_b, qg, kg, proj_wt, proj_b, fc2_b, ada_wt, ada_b,
                        fc1_wt, fc2_wt, gate1_d, gate2_d, gb2_d, x1_d, x1g_d, coef, ident, minus_half,
                        h2_hi, h2_lo, first_tiles)
        mlp_stage(nc, fc1_wt, fc1_bt, fc2_wt, gate2_d, x1_d, x1g_d, out, coef, ident, minus_half,
                  h2_hi, h2_lo, first_tiles)


def landing(nc, sb, name, shape):
    with nc.sbuf_tensor(name + "_raw", shape, F32) as raw:
        pass
    return raw, sb(name, shape, F32R)


def mlp_weights(nc, sb, name, tiles):
    w1_raw, w1_lo = landing(nc, sb, f"w1_lo_{name}", [P, tiles, KF, P])
    w1_x_raw, w1_x = landing(nc, sb, f"w1_x_{name}", [P, tiles, P])
    w2_raw, w2_lo = landing(nc, sb, f"w2_lo_{name}", [P, tiles, D])
    return (sb("w1_hi_" + name, [P, tiles, KF, P], F32R), w1_lo, w1_x,
            sb("w2_hi_" + name, [P, tiles, D], F32R), w2_lo, w1_raw, w1_x_raw, w2_raw)


def load_mlp_tiles(sp, weights, at, first, tiles, fc1_wt, fc2_wt, landed):
    _, _, _, _, _, w1_raw, w1_x_raw, w2_raw = weights
    for i in range(tiles):
        cols = slice((first + i) * P, (first + i + 1) * P)
        sp.dma_start(w1_raw[:, at + i, :, :], fc1_wt[0:KF * P, cols].rearrange("(k p) n -> p k n", p=P)
                     ).then_inc(landed, 16)
    cols = slice(first * P, (first + tiles) * P)
    for i in range(2):
        sp.dma_start(w1_x_raw[i * TAIL:(i + 1) * TAIL, at:at + tiles, :],
                     fc1_wt[KF * P:D, cols].rearrange("p (m n) -> p m n", n=P)).then_inc(landed, 16)
    sp.dma_start(w2_raw[:, at:at + tiles, :], fc2_wt[cols, :].rearrange("(m p) n -> p m n", p=P)
                 ).then_inc(landed, 16)


def mlp_tile_hi(nc, weights, at, tail_hi, done):
    w1_hi, w1_lo, w1_x, w2_hi, w2_lo, w1_raw, w1_x_raw, w2_raw = weights
    nc.scalar.activation(w1_hi[:, at, :, :], w1_raw[:, at, :, :], ACT.Copy)
    nc.scalar.activation(tail_hi[64:128, :], w1_x_raw[64:128, at, :], ACT.Copy)
    nc.scalar.activation(w1_x[0:64, at, :], w1_x_raw[0:64, at, :], ACT.Copy)
    nc.scalar.activation(w2_hi[:, at, :], w2_raw[:, at, :], ACT.Copy).then_inc(done, 1)


def mlp_tile_lo(nc, weights, at, tail_hi, done):
    w1_hi, w1_lo, w1_x, w2_hi, w2_lo, w1_raw, w1_x_raw, w2_raw = weights
    nc.vector.tensor_tensor(w1_lo[:, at, :, :], w1_raw[:, at, :, :], w1_hi[:, at, :, :].bitcast(F32), ALU.subtract)
    nc.vector.tensor_tensor(w1_x[64:128, at, :], w1_x_raw[64:128, at, :], tail_hi[64:128, :].bitcast(F32),
                            ALU.subtract)
    nc.vector.tensor_tensor(w2_lo[:, at, :], w2_raw[:, at, :], w2_hi[:, at, :].bitcast(F32), ALU.subtract
                            ).then_inc(done, 1)


def attention_stage(nc, x, cond_t, g1, g2, qkv_wt, qkv_b, qg, kg, proj_wt, proj_b, fc2_b, ada_wt, ada_b,
                    fc1_wt, fc2_wt, gate1_d, gate2_d, gb2_d, x1_d, x1g_d, coef, ident, minus_half,
                    h2_hi, h2_lo, first_tiles):
    ADA_BUFS = 3
    with ExitStack() as ctx:
        def sb(name, shape, dt):
            return ctx.enter_context(nc.sbuf_tensor(name, shape, dt))

        def ps(name, shape):
            return ctx.enter_context(nc.psum_tensor(name, shape, F32))

        def sem(name):
            return ctx.enter_context(nc.semaphore(name))

        wq_hi = sb("wq_hi", [P, KF, 3 * D], F32R)
        wq_raw, wq_lo = landing(nc, sb, "wq_lo", [P, KF, 3 * D])
        wq_x_raw, wq_x = landing(nc, sb, "wq_x", [P, 3 * D])
        wq_y_raw, wq_y = landing(nc, sb, "wq_y", [P, 3 * D])
        wp_hi = sb("wp_hi", [P, KF, D], F32R)
        wp_raw, wp_lo = landing(nc, sb, "wp_lo", [P, KF, D])
        wp_x_raw, wp_x = landing(nc, sb, "wp_x", [P, D])
        wp_y_raw, wp_y = landing(nc, sb, "wp_y", [P, D])
        aside = sb("aside", [P, 3 * D], F32R)
        ada = sb("ada", [P, ADA_BUFS, KT, NH], F32)
        condt = sb("condt", [P, KT, B], F32)
        sigm = sb("sigm", [P, 2, KT, B], F32)
        silut = sb("silut", [P, KT, B], F32)
        modrow = sb("modrow", [B, 2, DX], F32)
        gains = sb("gains", [P, 4], F32)
        gscale = sb("gscale", [P, 2], F32)
        qk_gain = sb("qk_gain", [P, 2, HG], F32)
        ident_r = sb("ident_r", [P, P], F32R)

        xin = sb("xin", [P, D], F32)
        xss = sb("xss", [P, 1], F32)
        xr = sb("xr", [P, 2], F32)
        xn = sb("xn", [P, DX], F32)
        h = sb("h", [P, DX], F32)
        h_hi = sb("h_hi", [P, 2, DX], F32R)
        h_lo = sb("h_lo", [P, DX], F32R)
        o = sb("o", [P, DX], F32)
        ot_hi = sb("ot_hi", [P, DX], F32R)
        ot_lo = sb("ot_lo", [P, DX], F32R)
        xres = sb("xres", [P, D], F32)
        gate1 = sb("gate1", [P, D], F32)
        gb2_all = sb("gb2_all", [P, D], F32)
        gated = sb("gated", [P, D], F32)
        x1 = sb("x1", [P, D], F32)
        x1g = sb("x1g", [P, D], F32)
        gate_rows = (gated[0:B, :], x1[0:B, :])
        gb2_rows = x1g[0:B, :]
        fc2_b_rows = xres[0:B, :]

        sq = sb("sq", [P, QK], F32)
        ss = sb("ss", [P, 2 * HG], F32)
        ssg = sb("ssg", [P, 2 * HG], F32)
        rpow = sb("rpow", [P, 2 * HG], F32)
        rqk = sb("rqk", [P, 2 * HG], F32)
        qk = sb("qk", [P, 2, HG, HD], F32)
        stack = sb("stack", [P, 2 * HG * ST], F32R)
        v = sb("v", [P, G, HG, VW], BF16)
        v_rest = sb("v_rest", [P, HG, HD], F32)
        qs = sb("qs", [P, HG * T], F32R)
        ks = sb("ks", [P, HG * T], F32R)
        neg_max = sb("neg_max", [P, HG], F32)
        pr = sb("pr", [P, HG * T], F32)
        pt_hi = sb("pt_hi", [P, HG * T], F16)
        pt_lo = sb("pt_lo", [P, HG * T], F16)
        rden = sb("rden", [P, HG], F32)
        o_sum = sb("o_sum", [P, HG, HD], F32)
        zero = sb("zero", [P, HG], F32)

        q_ps = ps("q_ps", [P, 2, BANK])
        ts_ps = ps("ts_ps", [P, BANK])
        tk_ps = ps("tk_ps", [P, BANK])
        pt_ps = ps("pt_ps", [P, BANK])
        o_ps = ps("o_ps", [P, BANK])
        y_ps = ps("y_ps", [P, 2, BANK])
        y_flat = y_ps[:, :, :].rearrange("p a b -> p (a b)")
        y_half = y_ps[:, :, 0:NH]

        ACT_BLOCKS = 3

        def x_block(k):
            bank, at = (0, k) if k < ACT_BLOCKS else (1, k - ACT_BLOCKS)
            return y_ps[:, bank, at * P:(at + 1) * P]

        coef_ps = [t[:, 0:KT * B] for t in (pt_ps, pt_ps, y_flat, y_flat)]

        half = HG * ST

        def v_part(g, part):
            return v[:, g, :, 1 + part * HD:1 + (part + 1) * HD]

        def stacked(first):
            base = stack[:, first * HD:first * HD + HD]
            step = half + (HD if first == 1 else -HD if first == 2 else 0)
            return bass.AP(tensor=base.tensor, offset=base.offset,
                           ap=[base.ap[0], [step, 2], [ST, HG], [1, HD]])

        cond_in = sem("cond_in")
        gains_in = sem("gains_in")
        fc2_b_in = sem("fc2_b_in")
        ada_in = [sem(f"ada_in{i}") for i in range(ADA_BUFS)]
        w_in = [sem(f"w_in{n}") for n in range(6)]
        tiles_in = sem("tiles_in")
        tile_hi_done = sem("tile_hi_done")
        tile_split = sem("tile_split")
        x_in = sem("x_in")
        res_in = sem("res_in")
        gate_in = sem("gate_in")
        gates_out = sem("gates_out")
        x1_out = sem("x1_out")
        x1g_out = sem("x1g_out")
        bias_in = [sem(f"bias_in{i}") for i in range(2)]
        cond_padded = sem("cond_padded")
        bias_zeroed = sem("bias_zeroed")
        const_step = sem("const_step")
        constants = sem("constants")
        ident_zeroed = sem("ident_zeroed")
        ident_made = sem("ident_made")
        ident_r_made = sem("ident_r_made")
        gains_made = sem("gains_made")
        silu_step = sem("silu_step")
        silu_exp = sem("silu_exp")
        silu_made = sem("silu_made")
        ada_done = sem("ada_done")
        row_done = sem("row_done")
        coef_t = sem("coef_t")
        coef_made = sem("coef_made")
        tanh_done = sem("tanh_done")
        gb2_done = sem("gb2_done")
        w_hi_done = sem("w_hi_done")
        w_split = sem("w_split")
        bias_hi_done = sem("bias_hi_done")
        bias_split = sem("bias_split")
        x_squared = sem("x_squared")
        x_guarded = sem("x_guarded")
        x_rnorm = sem("x_rnorm")
        x_scaled = sem("x_scaled")
        x_t = sem("x_t")
        h_made = sem("h_made")
        h_hi_made = sem("h_hi_made")
        h_split = sem("h_split")
        qkv_done = sem("qkv_done")
        qk_squared = sem("qk_squared")
        qk_summed = sem("qk_summed")
        qk_guarded = sem("qk_guarded")
        qk_pow = sem("qk_pow")
        qk_rnorm = sem("qk_rnorm")
        qk_scaled = sem("qk_scaled")
        qk_hi = sem("qk_hi")
        qk_lo = sem("qk_lo")
        qk_dup = sem("qk_dup")
        stack_t = sem("stack_t")
        stack_read = sem("stack_read")
        scores_done = sem("scores_done")
        v_first = sem("v_first")
        v_left = sem("v_left")
        v_second = sem("v_second")
        v_parts = sem("v_parts")
        max_done = sem("max_done")
        exp_done = sem("exp_done")
        o_summed = sem("o_summed")
        probs_t = sem("probs_t")
        probs_hi = sem("probs_hi")
        probs_split = sem("probs_split")
        pv_done = sem("pv_done")
        o_normed = sem("o_normed")
        o_dup = sem("o_dup")
        o_t = sem("o_t")
        ot_hi_made = sem("ot_hi_made")
        ot_split = sem("ot_split")
        proj_done = sem("proj_done")
        gated_done = sem("gated_done")
        x1_done = sem("x1_done")
        x1g_done = sem("x1g_done")

        steps = [(qkv_wt, g * GC, GC, (wq_raw, wq_x_raw, wq_y_raw), (wq_hi, wq_lo, wq_x, wq_y)) for g in range(G)]
        steps += [(proj_wt, c * NH, NH, (wp_raw, wp_x_raw, wp_y_raw), (wp_hi, wp_lo, wp_x, wp_y)) for c in range(2)]
        biases = ((qkv_b, 3 * D, wq_y_raw, wq_y), (proj_b, D, wp_y_raw, wp_y))

        PARTS = (0, 1, 2, 5, 3, 4)

        PROBS_FIRST = (2, 3)

        def run_batches(eng, body):
            body(0, 0, 0)
            body(1, 1, 1)
            with eng.Fori(1, B // 2 - 1) as pair:
                body(2 * pair, 2, 0)
                body(2 * pair + 1, 2, 1)
            body(B - 2, 2, 0)
            body(B - 1, 2, 1)

        block = ctx.enter_context(nc.Block())

        @block.sync
        def _(sp):
            def load_bias(i):
                src, _, y_raw, _ = biases[i]
                for row in (64, 96):
                    sp.dma_start(y_raw[row:row + 1, :], src).then_inc(bias_in[i], 16)

            def load_w(n):
                src, c0, cols, (raw, x_raw, y_raw), _ = steps[n]
                c = slice(c0, c0 + cols)
                sp.dma_start(raw[:, :, c], src[0:KF * P, c].rearrange("(k p) n -> p k n", p=P)
                             ).then_inc(w_in[n], 16)
                for dst in (x_raw[0:TAIL, c], x_raw[TAIL:P, c], y_raw[0:TAIL, c]):
                    sp.dma_start(dst, src[KF * P:D, c]).then_inc(w_in[n], 16)

            def load_ada(*halves):
                for j in halves:
                    i = j // 2
                    if j >= ADA_BUFS:
                        sp.wait_ge(ada_done, j - ADA_BUFS + 1)
                    c0 = PARTS[i] * D + (j % 2) * NH
                    cols, landed = slice(c0, c0 + NH), ada_in[j % ADA_BUFS]
                    dst = ada[:, j % ADA_BUFS, :, :]
                    sp.dma_start(dst[:, 0:KF, :], ada_wt[0:KF * P, cols].rearrange("(k p) n -> p k n", p=P)
                                 ).then_inc(landed, 16)
                    sp.dma_start(dst[0:TAIL, KF, :], ada_wt[KF * P:D, cols]).then_inc(landed, 16)
                    sp.dma_start(dst[TAIL:TAIL + 1, KF, :], ada_b[:, cols]).then_inc(landed, 16)

            sp.dma_start(condt[:, 0:KF, :], cond_t[0:KF * P, :].rearrange("(k p) n -> p k n", p=P)
                         ).then_inc(cond_in, 16)
            sp.dma_start(condt[0:TAIL, KF, :], cond_t[KF * P:D, :]).then_inc(cond_in, 16)
            load_ada(0, 1)
            sp.dma_start(xin[:, :], x[0]).then_inc(x_in, 16)
            load_ada(2)
            for i, g in enumerate((g1, g2, qg, kg)):
                sp.dma_start(gains[:, i:i + 1], g.partition_broadcast(P)).then_inc(gains_in, 16)
            sp.dma_start(fc2_b_rows, fc2_b.partition_broadcast(B)).then_inc(fc2_b_in, 16)
            sp.wait_ge(bias_zeroed, 2)
            load_bias(0)
            load_ada(3)
            load_w(0)
            sp.wait_ge(x_scaled, 1)
            sp.dma_start(xin[:, :], x[1]).then_inc(x_in, 16)
            load_w(1)
            load_ada(4, 5)
            load_w(2)
            load_w(3)
            load_ada(6, 7)
            load_w(4)
            load_ada(8, 9)
            load_bias(1)
            load_w(5)

            sp.wait_ge(tanh_done, 2)
            sp.dma_start(gate1_d, gate_rows[0]).then_inc(gates_out, 16)
            sp.dma_start(gate2_d, gate_rows[1]).then_inc(gates_out, 16)
            sp.wait_ge(gb2_done, 1)
            sp.dma_start(gb2_d, gb2_rows).then_inc(gates_out, 16)
            sp.wait_ge(gates_out, 48)
            load_ada(10, 11)
            load_mlp_tiles(sp, first_tiles, 0, 0, EARLY_TILES, fc1_wt, fc2_wt, tiles_in)

            def batch(b, early):
                if early == 2:
                    x1_out_of(b - 2)
                sp.wait_ge(x_scaled, b + 2)
                if isinstance(b, int) and b + 2 >= B:
                    sp.wait_ge(x1_out, 32)
                    sp.dma_start(xin[:, :], x1_d[b + 2 - B]).then_inc(x_in, 16)
                else:
                    sp.dma_start(xin[:, :], x[bass.ds(b + 2, 1), :, :].rearrange("a t d -> (a t) d")
                                 ).then_inc(x_in, 16)
                if early == 2:
                    x1g_out_of(b - 2)
                if early >= 1:
                    load_rows(b - 1)

            def load_rows(b):
                if not isinstance(b, int) or b >= 1:
                    sp.wait_ge(x1_done, b)
                    sp.wait_ge(x1g_done, b)
                sp.dma_start(xres[:, :], x[bass.ds(b, 1), :, :].rearrange("a t d -> (a t) d")).then_inc(res_in, 16)
                sp.dma_start(gate1[:, :], gate1_d[bass.ds(b, 1), :].partition_broadcast(P)).then_inc(gate_in, 16)
                sp.dma_start(gb2_all[:, :], gb2_d[bass.ds(b, 1), :].partition_broadcast(P)).then_inc(gate_in, 16)

            def x1_out_of(b):
                sp.wait_ge(x1_done, b + 1)
                sp.dma_start(x1_d[bass.ds(b, 1), :, :].rearrange("a t d -> (a t) d"), x1[:, :]).then_inc(x1_out, 16)

            def x1g_out_of(b):
                sp.wait_ge(x1g_done, b + 1)
                sp.dma_start(x1g_d[bass.ds(b, 1), :, :].rearrange("a t d -> (a t) d"), x1g[:, :]).then_inc(x1g_out, 16)

            batch(0, 0)
            batch(1, 1)
            with sp.Fori(2, B - 2) as b:
                batch(b, 2)
            batch(B - 2, 2)
            batch(B - 1, 2)
            x1_out_of(B - 2)
            x1g_out_of(B - 2)
            load_rows(B - 1)
            x1_out_of(B - 1)
            x1g_out_of(B - 1)
            sp.wait_ge(x1_out, 16 * B)
            sp.wait_ge(x1g_out, 16 * B)

        @block.tensor
        def _(pe):
            def ada_part(i, dst):
                for n in range(2):
                    j = 2 * i + n
                    pe.wait_ge(ada_in[j % ADA_BUFS], 48 * (j // ADA_BUFS + 1))
                    for k in range(KT):
                        rows = P if k < KF else TAIL + 1
                        last = nc.tensor.matmul(dst[0:B, n, 0:NH], silut[0:rows, k, :],
                                                ada[0:rows, j % ADA_BUFS, k, :],
                                                start=(k == 0), stop=(k == KT - 1))
                    last.then_inc(ada_done, 1)

            def coef_part(i):
                pe.wait_ge(row_done, i + 1)
                if i == 1:
                    pe.wait_ge(coef_made, i)
                for k in range(KT):
                    last = nc.tensor.transpose(coef_ps[i][:, k * B:(k + 1) * B],
                                               modrow[:, i % 2, k * P:(k + 1) * P], ident[0:B, 0:B])
                last.then_inc(coef_t, 1)

            pe.wait_ge(silu_made, 1)
            pe.wait_ge(ident_made, 1)
            ada_part(0, q_ps)
            ada_part(1, y_ps)
            coef_part(0)
            coef_part(1)

            def x_transposed(b):
                pe.wait_ge(x_scaled, b + 1)
                if isinstance(b, int) and b == 0:
                    pe.wait_ge(row_done, 2)
                elif isinstance(b, int) and b == 1:
                    pe.wait_ge(tanh_done, 2)
                elif isinstance(b, int) and b == 2:
                    pe.wait_ge(coef_made, 4)
                else:
                    pe.wait_ge(gated_done, b - 2)
                for k in range(KT):
                    last = nc.tensor.transpose(x_block(k), xn[:, k * P:(k + 1) * P], ident[:, :])
                last.then_inc(x_t, 1)

            x_transposed(0)
            pe.wait_ge(ident_r_made, 1)
            pe.wait_ge(constants, 1)
            pe.wait_ge(bias_split, 1)

            BEFORE_SCORES = (7, 6, 6, 7)

            passes = [(True, wq_hi, k) for k in range(KF)] + [(True, wq_lo, k) for k in range(KF)]
            passes += [(True, wq_x, KF)] + [(False, wq_hi, k) for k in range(KF)] + [(False, wq_y, KF)]

            def qkv(g, parity, first, last_):
                for n in range(first, last_):
                    hi, w, k = passes[n]
                    a = h_hi[:, parity, :] if hi else h_lo
                    mov = w[:, g * GC:(g + 1) * GC] if k == KF else w[:, k, g * GC:(g + 1) * GC]
                    ins = nc.tensor.matmul(q_ps[:, g % 2, 0:GC], a[:, k * P:(k + 1) * P], mov,
                                           start=(n == 0), stop=(n == 13))
                if last_ == 14:
                    ins.then_inc(qkv_done, 1)

            def stacks_transposed(u, before):
                for w, dst in ((1, tk_ps), (0, ts_ps)):
                    if w == 0 and before:
                        pe.wait_ge(exp_done, HG * (u - 1))
                    for i in range(HG):
                        c = w * half + i * ST
                        ins = nc.tensor.transpose(dst[0:ST, i * T:(i + 1) * T].bitcast(F32R),
                                                  stack[:, c:c + ST], ident_r[:, :])
                ins.then_inc(stack_t, 1)

            def scores(u):
                pe.wait_ge(stack_read, 2 * (u - 1))
                for i in range(HG):
                    ins = nc.tensor.matmul(ts_ps[:, i * T:(i + 1) * T], qs[0:ST, i * T:(i + 1) * T],
                                           ks[0:ST, i * T:(i + 1) * T], start=True, stop=True)
                ins.then_inc(scores_done, 1)

            def probs_transposed(u, before):
                if before:
                    pe.wait_ge(probs_split, u - 2)
                for i in range(HG):
                    pe.wait_ge(exp_done, (u - 2) * HG + i + 1)
                    ins = nc.tensor.transpose(pt_ps[:, i * T:(i + 1) * T], pr[:, i * T:(i + 1) * T], ident[:, :])
                ins.then_inc(probs_t, 1)

            def values(g):
                for i in range(HG):
                    out_ = o_ps[:, i * VW:(i + 1) * VW]
                    nc.tensor.matmul(out_[:, 0:1 + 3 * HD], pt_hi[:, i * T:(i + 1) * T], v[:, g, i, 0:1 + 3 * HD],
                                     start=True, stop=False)
                    ins = nc.tensor.matmul(out_[:, 0:1 + 2 * HD], pt_lo[:, i * T:(i + 1) * T], v[:, g, i, 0:1 + 2 * HD],
                                           start=False, stop=True)
                ins.then_inc(pv_done, 1)

            def o_transposed(b):
                pe.wait_ge(o_dup, b + 1)
                if not isinstance(b, int) or b >= 1:
                    pe.wait_ge(gated_done, b)
                pe.wait_ge(h_made, (b + 3) * KT)
                for k in range(KT):
                    last = nc.tensor.transpose(y_flat[:, k * P:(k + 1) * P], o[:, k * P:(k + 1) * P], ident[:, :])
                last.then_inc(o_t, 1)

            proj_passes = [(ot_hi, wp_hi, k) for k in range(KF)] + [(ot_hi, wp_lo, k) for k in range(KF)]
            proj_passes += [(ot_hi, wp_x, KF)] + [(ot_lo, wp_hi, k) for k in range(KF)] + [(ot_lo, wp_y, KF)]

            def project(b, first, last_):
                if first == 0:
                    pe.wait_ge(ot_split, b + 1)
                for n in range(first, last_):
                    a, w, k = proj_passes[n]
                    for c in range(2):
                        mov = w[:, c * NH:(c + 1) * NH] if k == KF else w[:, k, c * NH:(c + 1) * NH]
                        ins = nc.tensor.matmul(y_ps[:, c, 0:NH], a[:, k * P:(k + 1) * P], mov,
                                               start=(n == 0), stop=(n == 13))
                if last_ == 14:
                    ins.then_inc(proj_done, 1)

            def slot(b, g, early, parity, run=True):
                u = 4 * b + g
                one = (early > 0 or g >= 1) and (run or g == 0)
                two = (early > 0 or g >= 2) and (run or g <= 1)
                three = (early > 0 or g >= 3) and (run or g <= 2)
                if run:
                    if g == 0:
                        pe.wait_ge(h_hi_made, b + 1)
                    if early > 0 or g >= 2:
                        pe.wait_ge(qk_scaled, u - 1)
                        pe.wait_ge(v_left, u - 1)
                    qkv(g, parity, 0, BEFORE_SCORES[g])
                if two:
                    scores(u)
                if early == 1 and g < 2:
                    coef_part(2 + g)
                if run:
                    qkv(g, parity, BEFORE_SCORES[g], 9)
                    if g == 0:
                        pe.wait_ge(h_split, b + 1)
                    qkv(g, parity, 9, 14)
                if three:
                    pe.wait_ge(probs_split, u - 2)
                    pe.wait_ge(v_parts, u - 2)
                    if early > 0:
                        pe.wait_ge(o_normed, u - 3)
                    values((g + 1) % 4)
                if early == 0:
                    if g == 0:
                        ada_part(2, y_ps)
                    if g == 1:
                        pe.wait_ge(tanh_done, 1)
                        ada_part(3, y_ps)
                    if g == 3:
                        pe.wait_ge(h_made, 2 * KT)
                        ada_part(4, y_ps)
                if early == 1 and g == 0:
                    pe.wait_ge(coef_made, 3)
                    ada_part(5, y_ps)
                if g == 0 and early == 2:
                    project(b - 2, 0, 7)
                if g == 1 and early == 2:
                    project(b - 2, 7, 14)
                if g == 2:
                    x_transposed(b + 1)
                if g == 3 and early >= 1:
                    o_transposed(b - 1)
                if g == 3 and early == 1:
                    pe.wait_ge(w_split, len(steps))
                    pe.wait_ge(bias_split, 2)
                if two and g in PROBS_FIRST:
                    probs_transposed(u, early > 0 or g >= 3)
                if one:
                    pe.wait_ge(qk_lo, u)
                    pe.wait_ge(qk_dup, u)
                    stacks_transposed(u, early > 0 or g >= 2)
                if two and g not in PROBS_FIRST:
                    probs_transposed(u, early > 0 or g >= 3)

            def batch(b, early, parity):
                for g in range(G):
                    if early == 0:
                        pe.wait_ge(w_split, g + 1)
                    slot(b, g, early, parity)

            pe.wait_ge(coef_made, 2)
            run_batches(pe, batch)
            slot(B, 0, 2, 0, run=False)
            slot(B, 1, 2, 0, run=False)
            slot(B, 2, 2, 0, run=False)
            o_transposed(B - 1)
            project(B - 1, 0, 14)

        @block.scalar
        def _(act):
            act.wait_ge(cond_in, 32)
            act.wait_ge(cond_padded, 1)
            nc.scalar.activation(sigm[:, 0, :, :], condt[:, :, :], ACT.Exp, scale=-1.0).then_inc(silu_exp, 1)

            def w_hi(n):
                _, c0, cols, (raw, x_raw, y_raw), (hi, _, x_, y_) = steps[n]
                act.wait_ge(w_in[n], 64)
                if n == 0:
                    act.wait_ge(bias_split, 1)
                elif n >= 2:
                    act.wait_ge(w_split, n - 1)
                c = slice(c0, c0 + cols)
                nc.scalar.activation(hi[:, :, c], raw[:, :, c], ACT.Copy)
                nc.scalar.activation(aside[64:128, (n % 2) * GC:(n % 2) * GC + cols], x_raw[64:128, c], ACT.Copy)
                nc.scalar.activation(x_[0:64, c], x_raw[0:64, c], ACT.Copy)
                nc.scalar.activation(y_[0:64, c], y_raw[0:64, c], ACT.Copy).then_inc(w_hi_done, 1)

            def bias_hi(i):
                _, cols, y_raw, y_ = biases[i]
                act.wait_ge(bias_in[i], 32)
                at = slice(2 * GC, 2 * GC + cols) if i else slice(0, cols)
                nc.scalar.activation(aside[96:128, at], y_raw[96:128, :], ACT.Copy)
                nc.scalar.activation(y_[64:96, :], y_raw[64:96, :], ACT.Copy).then_inc(bias_hi_done, 1)

            def tile_hi(m):
                act.wait_ge(tiles_in, 16 * (EARLY_TILES + 3))
                mlp_tile_hi(nc, first_tiles, m, aside[:, m * P:(m + 1) * P], tile_hi_done)

            def tanh_of(n, i):
                act.wait_ge(ada_done, 2 * n + 2)
                nc.scalar.activation(gate_rows[i].rearrange("p (a b) -> p a b", a=2), y_ps[0:B, :, 0:NH],
                                     ACT.Tanh).then_inc(tanh_done, 1)

            def square_x(b):
                act.wait_ge(x_in, 16 * b + 16)
                if not isinstance(b, int) or b >= 1:
                    act.wait_ge(x_guarded, b)
                    act.wait_ge(x_t, b)
                nc.scalar.activation(xn[:, 0:D], xin[:, :], ACT.Square, accum_out=xss[:, :]).then_inc(x_squared, 1)

            def modulate(b, k):
                row, element = (2, b - B) if isinstance(b, int) and b >= B else (0, b)
                nc.scalar.activation(h[:, k * P:(k + 1) * P], x_block(k), ACT.Identity,
                                     bias=coef[:, row, k, bass.ds(element, 1)],
                                     scale=coef[:, row + 1, k, bass.ds(element, 1)]).then_inc(h_made, 1)

            def h_hi_of(b, parity):
                act.wait_ge(h_made, (b + 1) * KT)
                dst = h_hi[:, parity, :].rearrange("p (k t) -> p k t", t=T)
                if isinstance(b, int) and b >= B:
                    dst = h2_hi[:, :, b - B, :]
                elif not isinstance(b, int) or b >= 2:
                    act.wait_ge(qkv_done, 4 * b - 4)
                nc.scalar.activation(dst, h[:, :].rearrange("p (k t) -> p k t", t=T), ACT.Copy).then_inc(h_hi_made, 1)

            square_x(0)
            bias_hi(0)
            w_hi(0)
            act.wait_ge(x_t, 1)
            act.wait_ge(coef_made, 2)
            for k in range(ACT_BLOCKS):
                modulate(0, k)
            h_hi_of(0, 0)
            w_hi(1)

            def exps():
                for i in range(HG):
                    nc.scalar.activation(pr[:, i * T:(i + 1) * T], ts_ps[:, i * T:(i + 1) * T], ACT.Exp,
                                         bias=neg_max[:, i:i + 1]).then_inc(exp_done, 1)

            def probs_hi_of(u, before):
                act.wait_ge(probs_t, u - 1)
                if before:
                    act.wait_ge(pv_done, u - 2)
                nc.scalar.activation(pt_hi[:, :], pt_ps[:, :], ACT.Copy, scale=P_SCALE).then_inc(probs_hi, 1)

            def slot(b, g, early, parity, run=True):
                u = 4 * b + g
                one = (early > 0 or g >= 1) and (run or g == 0)
                two = (early > 0 or g >= 2) and (run or g <= 1)
                if two:
                    if early > 0 or g >= 3:
                        act.wait_ge(probs_t, u - 2)
                    act.wait_ge(max_done, u - 1)
                    exps()
                if one:
                    act.wait_ge(qk_hi, u)
                    nc.scalar.activation(stacked(2), stacked(0), ACT.Copy).then_inc(qk_dup, 1)
                if run:
                    act.wait_ge(qkv_done, u + 1)
                    if early > 0 or g >= 1:
                        act.wait_ge(qk_summed, u)
                    nc.scalar.activation(sq[:, :], q_ps[:, g % 2, 0:QK], ACT.Square).then_inc(qk_squared, 1)
                if run:
                    if early > 0:
                        act.wait_ge(pv_done, u - 3)
                    nc.scalar.activation(v_part(g, 0), q_ps[:, g % 2, QK:GC].rearrange("p (a b) -> p a b", b=HD),
                                         ACT.Copy).then_inc(v_first, 1)
                if early == 0 and g != 2:
                    w_hi((2, 3, None, 4)[g])
                if early == 1 and g == 0:
                    w_hi(5)
                    bias_hi(1)
                if two and g in PROBS_FIRST:
                    probs_hi_of(u, early > 0 or g >= 3)
                if one:
                    act.wait_ge(stack_t, u)
                    if early > 0 or g >= 2:
                        act.wait_ge(scores_done, u - 1)
                    nc.scalar.activation(qs[0:ST, :], ts_ps[0:ST, :], ACT.Copy).then_inc(stack_read, 1)
                    nc.scalar.activation(ks[0:ST, :], tk_ps[0:ST, :], ACT.Copy).then_inc(stack_read, 1)
                if two and g not in PROBS_FIRST:
                    probs_hi_of(u, early > 0 or g >= 3)
                if g == 0:
                    square_x(b + 1)
                if early == 0 and g < 2:
                    tanh_of(2 + g, g)
                if g == 2:
                    act.wait_ge(x_t, b + 2)
                    act.wait_ge(h_split, b + 1)
                    for k in range(ACT_BLOCKS):
                        modulate(b + 1, k)
                    h_hi_of(b + 1, 1 - parity)
                if g == 3 and early >= 1:
                    ot_hi_of(b - 1)

            def ot_hi_of(b):
                act.wait_ge(o_t, b + 1)
                if not isinstance(b, int) or b >= 1:
                    act.wait_ge(proj_done, b)
                nc.scalar.activation(ot_hi[:, :], y_flat[:, 0:DX], ACT.Copy).then_inc(ot_hi_made, 1)

            def batch(b, early, parity):
                for g in range(G):
                    slot(b, g, early, parity)

            run_batches(act, batch)
            slot(B, 0, 2, 0, run=False)
            slot(B, 1, 2, 0, run=False)
            slot(B, 2, 2, 0, run=False)
            ot_hi_of(B - 1)
            for m in range(EARLY_TILES):
                tile_hi(m)

        @block.vector
        def _(dve):
            nc.vector.memset(condt[TAIL:P, KF, :], 0.0).then_inc(cond_padded, 1)
            nc.vector.memset(silut[:, :, :], 1.0).then_inc(const_step, 1)
            for t in (h_lo, ot_lo):
                nc.vector.memset(t[64:128, KF * P:DX].bitcast(F32), 0.0).then_inc(const_step, 1)
            dve.wait_ge(const_step, 3)
            for t in (h_lo, ot_lo):
                for row in (64, 96):
                    nc.vector.memset(t[row:row + 1, KF * P:DX].bitcast(F32), 1.0)
            nc.vector.memset(minus_half[:, :], -0.5)
            nc.vector.memset(zero[:, :], 0.0)
            nc.vector.memset(v[:, :, :, 0:1], 1.0).then_inc(constants, 1)
            dve.wait_ge(silu_exp, 1)
            nc.vector.tensor_scalar(sigm[:, 1, :, :], sigm[:, 0, :, :], 1.0, None, ALU.add).then_inc(silu_step, 1)
            dve.wait_ge(silu_step, 1)
            nc.vector.reciprocal(sigm[:, 0, :, :], sigm[:, 1, :, :]).then_inc(silu_step, 1)
            dve.wait_ge(silu_step, 2)
            nc.vector.tensor_tensor(silut[:, 0:KF, :], condt[:, 0:KF, :], sigm[:, 0, 0:KF, :], ALU.mult)
            nc.vector.tensor_tensor(silut[0:TAIL, KF, :], condt[0:TAIL, KF, :], sigm[0:TAIL, 0, KF, :],
                                    ALU.mult).then_inc(silu_made, 1)
            dve.wait_ge(ident_made, 1)
            nc.vector.tensor_copy(ident_r[:, :], ident[:, :]).then_inc(ident_r_made, 1)
            dve.wait_ge(gains_in, 64)
            nc.vector.tensor_scalar(gscale[:, :], gains[:, 0:2], float(D) ** 0.5, None, ALU.mult).then_inc(gains_made, 1)
            nc.vector.tensor_copy(qk_gain[:, 0, :], gains[:, 2:3].to_broadcast([P, HG]))
            nc.vector.tensor_scalar(qk_gain[:, 1, :], gains[:, 3:4].to_broadcast([P, HG]), float(HD) ** 0.5, None,
                                    ALU.mult).then_inc(gains_made, 1)
            dve.wait_ge(gains_made, 2)

            def w_lo(n):
                _, c0, cols, (raw, x_raw, _), (hi, lo, x_, _) = steps[n]
                dve.wait_ge(w_hi_done, n + 1)
                c = slice(c0, c0 + cols)
                nc.vector.tensor_tensor(lo[:, :, c], raw[:, :, c], hi[:, :, c].bitcast(F32), ALU.subtract)
                nc.vector.tensor_tensor(x_[64:128, c], x_raw[64:128, c],
                                        aside[64:128, (n % 2) * GC:(n % 2) * GC + cols].bitcast(F32), ALU.subtract
                                        ).then_inc(w_split, 1)

            def bias_lo(i):
                _, cols, y_raw, y_ = biases[i]
                dve.wait_ge(bias_hi_done, i + 1)
                at = slice(2 * GC, 2 * GC + cols) if i else slice(0, cols)
                nc.vector.tensor_tensor(y_[96:128, :], y_raw[96:128, :], aside[96:128, at].bitcast(F32),
                                        ALU.subtract).then_inc(bias_split, 1)

            def tile_lo(m):
                dve.wait_ge(tile_hi_done, m + 1)
                mlp_tile_lo(nc, first_tiles, m, aside[:, m * P:(m + 1) * P], tile_split)

            def guard_x(b):
                dve.wait_ge(x_squared, b + 1)
                nc.vector.tensor_scalar(xr[:, 0:1], xss[:, :], EPS2, None, ALU.max).then_inc(x_guarded, 1)

            def scale_x(b):
                dve.wait_ge(x_rnorm, b + 1)
                if not isinstance(b, int) or b >= 1:
                    dve.wait_ge(x_t, b)
                nc.vector.tensor_scalar(xn[:, 0:D], xin[:, :], xr[:, 1:2], None, ALU.mult)
                nc.vector.tensor_scalar(xn[:, D:DX], xin[:, KF * P:D], xr[:, 1:2], None, ALU.mult).then_inc(x_scaled, 1)

            def ada_row(i, n, src_ps):
                dve.wait_ge(ada_done, 2 * n + 2)
                if i >= 2:
                    dve.wait_ge(coef_t, i - 1)
                src = src_ps[0:B, :, :]
                dst = modrow[:, i % 2, :]
                pieces = ((dst[:, 0:D].rearrange("p (a b) -> p a b", a=2), src[:, :, 0:NH]),
                          (dst[:, D:DX], src[:, 1, NH - TAIL:NH]))
                for to, of in pieces:
                    if i % 2 == 0:
                        ins = nc.vector.tensor_copy(to, of)
                    else:
                        ins = nc.vector.tensor_scalar(to, of, 1.0, gscale[0:B, i // 2:i // 2 + 1], ALU.add, ALU.mult)
                ins.then_inc(row_done, 1)

            def coef_out(i):
                dve.wait_ge(coef_t, i + 1)
                nc.vector.tensor_copy(coef[:, i, :, :], coef_ps[i].rearrange("p (k b) -> p k b", k=KT)
                                      ).then_inc(coef_made, 1)

            def modulate(b):
                row, element = (2, b - B) if isinstance(b, int) and b >= B else (0, b)
                dve.wait_ge(x_t, b + 1)
                if isinstance(b, int) and b == 0:
                    dve.wait_ge(coef_made, 2)
                else:
                    dve.wait_ge(h_split, b)
                if isinstance(b, int) and b == B:
                    dve.wait_ge(coef_made, 4)
                for k in range(ACT_BLOCKS, KT):
                    nc.vector.tensor_scalar(h[:, k * P:(k + 1) * P], x_block(k), coef[:, row + 1, k, bass.ds(element, 1)],
                                            coef[:, row, k, bass.ds(element, 1)], ALU.mult, ALU.add).then_inc(h_made, 1)

            def h_lo_of(b, parity):
                hi = h_hi[:, parity, :]
                dve.wait_ge(h_hi_made, b + 1)
                if isinstance(b, int) and b >= B:
                    nc.vector.tensor_tensor(h2_lo[:, :, b - B, :], h[:, :].rearrange("p (k t) -> p k t", t=T),
                                            h2_hi[:, :, b - B, :].bitcast(F32), ALU.subtract).then_inc(h_split, 1)
                    return
                nc.vector.tensor_tensor(h_lo[:, 0:KF * P], h[:, 0:KF * P], hi[:, 0:KF * P].bitcast(F32), ALU.subtract)
                nc.vector.tensor_tensor(h_lo[0:64, KF * P:DX], h[0:64, KF * P:DX], hi[0:64, KF * P:DX].bitcast(F32),
                                        ALU.subtract).then_inc(h_split, 1)

            guard_x(0)
            scale_x(0)
            ada_row(0, 0, q_ps)
            bias_lo(0)
            ada_row(1, 1, y_ps)
            for i in range(2):
                coef_out(i)
            modulate(0)
            w_lo(0)
            h_lo_of(0, 0)
            w_lo(1)

            def slot(b, g, early, parity, run=True):
                u = 4 * b + g
                one = (early > 0 or g >= 1) and (run or g == 0)
                two = (early > 0 or g >= 2) and (run or g <= 1)
                three = (early > 0 or g >= 3) and (run or g <= 2)
                if g == 2 and early == 2:
                    gate_of(b - 2)
                if three:
                    dve.wait_ge(probs_hi, u - 2)
                    nc.vector.scalar_tensor_tensor(out=pt_lo[:, :], in0=pt_ps[:, :], scalar=P_SCALE, in1=pt_hi[:, :],
                                                   op0=ALU.mult, op1=ALU.subtract).then_inc(probs_split, 1)
                if two:
                    dve.wait_ge(scores_done, u - 1)
                    if early > 0 or g >= 3:
                        dve.wait_ge(exp_done, HG * (u - 2))
                    nc.vector.tensor_reduce(neg_max[:, :], ts_ps[:, :].rearrange("p (a b) -> p a b", b=T), AX_X, ALU.max,
                                            negate=True).then_inc(max_done, 1)
                if early == 1 and g < 2:
                    coef_out(2 + g)
                if g == 0 and early == 2:
                    ot_lo_of(b - 2)
                if g == 1:
                    guard_x(b + 1)
                if one:
                    dve.wait_ge(qk_rnorm, u)
                    nc.vector.tensor_tensor(qk[:, :, :, :].rearrange("p a b c -> p (a b) c"),
                                            q_ps[:, (g + 1) % 2, 0:QK].rearrange("p (a c) -> p a c", c=HD),
                                            rqk[:, :].unsqueeze(2).to_broadcast([P, 2 * HG, HD]),
                                            ALU.mult).then_inc(qk_scaled, 1)
                    dve.wait_ge(qk_scaled, u)
                    if early > 0 or g >= 2:
                        dve.wait_ge(stack_t, u - 1)
                    nc.vector.tensor_copy(stacked(0), qk[:, :, :, :]).then_inc(qk_hi, 1)
                    dve.wait_ge(qk_hi, u)
                    nc.vector.tensor_tensor(stacked(1), qk[:, :, :, :], stacked(0).bitcast(F32), ALU.subtract
                                            ).then_inc(qk_lo, 1)
                if three:
                    gg = (g + 1) % 4
                    dve.wait_ge(pv_done, u - 2)
                    oh = o_ps[:, 0:HG * VW].rearrange("p (a b) -> p a b", b=VW)
                    nc.vector.reciprocal(rden[:, :].unsqueeze(2), oh[:, :, 0:1])
                    nc.vector.tensor_reduce(o_sum[:, :, :], oh[:, :, 1:1 + 3 * HD].rearrange("p a (c d) -> p a d c", c=3),
                                            AX_X, ALU.add).then_inc(o_summed, 1)
                if run:
                    dve.wait_ge(qk_squared, u + 1)
                    if early > 0 or g >= 1:
                        dve.wait_ge(qk_pow, u)
                    nc.vector.tensor_reduce(ss[:, :], sq[:, :].rearrange("p (a c) -> p a c", c=HD), AX_X, ALU.add
                                            ).then_inc(qk_summed, 1)
                if three:
                    dve.wait_ge(o_summed, u - 2)
                    if gg == 0 and not (isinstance(b, int) and b == 0):
                        dve.wait_ge(o_t, b)
                    nc.vector.tensor_tensor(o[:, gg * HG * HD:(gg + 1) * HG * HD].rearrange("p (a b) -> p a b", b=HD),
                                            o_sum[:, :, :], rden[:, :].unsqueeze(2).to_broadcast([P, HG, HD]),
                                            ALU.mult).then_inc(o_normed, 1)
                if run:
                    dve.wait_ge(qk_summed, u + 1)
                    nc.vector.tensor_scalar(ssg[:, :], ss[:, :], EPS2, None, ALU.max).then_inc(qk_guarded, 1)
                if three:
                    if gg == 3:
                        dve.wait_ge(o_normed, u - 2)
                        nc.vector.tensor_copy(o[:, D:DX], o[:, KF * P:D]).then_inc(o_dup, 1)
                if g == 3:
                    h_lo_of(b + 1, 1 - parity)
                if run:
                    dve.wait_ge(v_first, u + 1)
                    if early > 0 or g >= 1:
                        dve.wait_ge(v_parts, u)
                    nc.vector.tensor_tensor(v_rest[:, :, :], q_ps[:, g % 2, QK:GC].rearrange("p (a b) -> p a b", b=HD),
                                            v_part(g, 0), ALU.subtract).then_inc(v_left, 1)
                if g == 2:
                    modulate(b + 1)
                if g == 1:
                    scale_x(b + 1)
                if early == 0:
                    if g == 0:
                        w_lo(2)
                    if g == 1:
                        w_lo(3)
                    if g == 2:
                        dve.wait_ge(tanh_done, 2)
                        dve.wait_ge(fc2_b_in, 16)
                        nc.vector.tensor_tensor(gb2_rows, gate_rows[1], fc2_b_rows, ALU.mult).then_inc(gb2_done, 1)
                    if g == 3:
                        ada_row(2, 4, y_ps)
                        w_lo(4)
                if early == 1:
                    if g == 0:
                        ada_row(3, 5, y_ps)
                        w_lo(5)
                        bias_lo(1)

            def ot_lo_of(b):
                dve.wait_ge(ot_hi_made, b + 1)
                if not isinstance(b, int) or b >= 1:
                    dve.wait_ge(proj_done, b)
                nc.vector.tensor_tensor(ot_lo[:, 0:KF * P], y_flat[:, 0:KF * P], ot_hi[:, 0:KF * P].bitcast(F32),
                                        ALU.subtract)
                nc.vector.tensor_tensor(ot_lo[0:64, KF * P:DX], y_flat[0:64, KF * P:DX],
                                        ot_hi[0:64, KF * P:DX].bitcast(F32), ALU.subtract).then_inc(ot_split, 1)

            def last_x1():
                dve.wait_ge(gated_done, B)
                dve.wait_ge(res_in, 16 * B)
                dve.wait_ge(x1_out, 16 * (B - 1))
                nc.vector.tensor_tensor(x1[:, :], gated[:, :], xres[:, :], ALU.add).then_inc(x1_done, 1)
                dve.wait_ge(x1_done, B)
                dve.wait_ge(x1g_out, 16 * (B - 1))
                nc.vector.tensor_tensor(x1g[:, :], x1[:, :], gb2_all[:, :], ALU.add).then_inc(x1g_done, 1)

            def gate_of(b):
                dve.wait_ge(proj_done, b + 1)
                dve.wait_ge(gate_in, 32 * b + 32)
                if not isinstance(b, int) or b >= 1:
                    dve.wait_ge(x1_done, b)
                nc.vector.tensor_tensor(gated[:, :].rearrange("p (a b) -> p a b", a=2), y_half,
                                        gate1[:, :].rearrange("p (a b) -> p a b", a=2), ALU.mult
                                        ).then_inc(gated_done, 1)

            def batch(b, early, parity):
                for g in range(G):
                    slot(b, g, early, parity)

            run_batches(dve, batch)
            slot(B, 0, 2, 0, run=False)
            slot(B, 1, 2, 0, run=False)
            slot(B, 2, 2, 0, run=False)
            ot_lo_of(B - 1)
            h_lo_of(B + 1, 1)
            for m in range(EARLY_TILES):
                tile_lo(m)
            gate_of(B - 1)
            last_x1()

        @block.gpsimd
        def _(pool):
            nc.gpsimd.memset(ident[:, :], 0.0).then_inc(ident_zeroed, 1)
            pool.wait_ge(ident_zeroed, 1)
            nc.gpsimd.affine_select(out=ident[:, :], in_=ident[:, :], compare_op=ALU.not_equal, fill=1.0, base=0,
                                    pattern=[[-1, P]], channel_multiplier=1).then_inc(ident_made, 1)
            pool.wait_ge(ident_made, 1)
            nc.gpsimd.memset(wq_y_raw[64:128, :], 0.0).then_inc(bias_zeroed, 1)
            pool.wait_ge(bias_zeroed, 1)
            nc.gpsimd.memset(wp_y_raw[64:128, :], 0.0).then_inc(bias_zeroed, 1)
            pool.wait_ge(bias_zeroed, 2)

            def x_rnorm_of(b):
                pool.wait_ge(x_guarded, b + 1)
                nc.gpsimd.tensor_tensor(xr[:, 1:2], xr[:, 0:1], minus_half[:, 0:1], ALU.pow).then_inc(x_rnorm, 1)

            def qk_rnorm_of(u):
                pool.wait_ge(qk_guarded, u + 1)
                nc.gpsimd.tensor_tensor(rpow[:, :], ssg[:, :], minus_half[:, :], ALU.pow).then_inc(qk_pow, 1)
                pool.wait_ge(qk_pow, u + 1)
                if not isinstance(u, int) or u >= 1:
                    pool.wait_ge(qk_scaled, u)
                nc.gpsimd.tensor_tensor(rqk[:, :], rpow[:, :], qk_gain[:, :, :].rearrange("p a b -> p (a b)"),
                                        ALU.mult).then_inc(qk_rnorm, 1)

            def v_rest_split(b, g):
                u = 4 * b + g
                pool.wait_ge(v_left, u + 1)
                if not isinstance(b, int) or b >= 1:
                    pool.wait_ge(pv_done, u - 3)
                nc.gpsimd.tensor_tensor(v_part(g, 1), v_rest[:, :, :],
                                        zero[:, :].unsqueeze(2).to_broadcast([P, HG, HD]), ALU.add).then_inc(v_second, 1)
                pool.wait_ge(v_second, u + 1)
                nc.gpsimd.tensor_tensor(v_part(g, 2), v_rest[:, :, :], v_part(g, 1), ALU.subtract
                                        ).then_inc(v_parts, 1)

            def x1_of(b):
                pool.wait_ge(gated_done, b + 1)
                pool.wait_ge(res_in, 16 * b + 16)
                if not isinstance(b, int) or b >= 1:
                    pool.wait_ge(x1_out, 16 * b)
                nc.gpsimd.tensor_tensor(x1[:, :], gated[:, :], xres[:, :], ALU.add).then_inc(x1_done, 1)

            def x1g_of(b):
                pool.wait_ge(x1_done, b + 1)
                pool.wait_ge(gate_in, 32 * b + 32)
                if not isinstance(b, int) or b >= 1:
                    pool.wait_ge(x1g_out, 16 * b)
                nc.gpsimd.tensor_tensor(x1g[:, :], x1[:, :], gb2_all[:, :], ALU.add).then_inc(x1g_done, 1)

            pool.wait_ge(gains_made, 2)
            pool.wait_ge(constants, 1)
            x_rnorm_of(0)

            def batch(b, early, parity):
                for g in range(G):
                    if g == 1:
                        x_rnorm_of(b + 1)
                    qk_rnorm_of(4 * b + g)
                    v_rest_split(b, g)
                    if g == 2 and early >= 2:
                        x1_of(b - 2)
                    if g == 3 and early >= 2:
                        x1g_of(b - 2)

            run_batches(pool, batch)
            x_rnorm_of(B + 1)
            x1_of(B - 2)
            x1g_of(B - 2)


def mlp_stage(nc, fc1_wt, fc1_bt, fc2_wt, gate2_d, x1_d, x1g_d, out, coef, ident, minus_half,
              h_hi, h_lo, first_tiles):
    with ExitStack() as ctx:
        def sb(name, shape, dt):
            return ctx.enter_context(nc.sbuf_tensor(name, shape, dt))

        def ps(name, shape):
            return ctx.enter_context(nc.psum_tensor(name, shape, F32))

        def sem(name):
            return ctx.enter_context(nc.semaphore(name))

        other_tiles = mlp_weights(nc, sb, "other", MT - EARLY_TILES)

        def tile_at(m):
            return (first_tiles, m) if m < EARLY_TILES else (other_tiles, m - EARLY_TILES)

        tail_hi = sb("tail_hi", [P, 2, P], F32R)
        fc1_b = sb("fc1_b", [P, MT], F32)
        xin = sb("x1_in", [P, DX], F32)
        xss = sb("x1_ss", [P, 1], F32)
        xr = sb("x1_r", [P, 2], F32)
        h = sb("h2", [P, KT, 2, T], F32)
        act_f = sb("act_f", [P, 2 * T], F32)
        act_hi = sb("act_hi", [P, 2, 2 * T], F32R)
        act_lo = sb("act_lo", [P, 2, 2 * T], F32R)
        res = sb("res", [P, 2, D], F32)
        gate = sb("gate", [P, 2, D], F32)

        z_ps = ps("z_ps", [P, 2, 2, BANK])
        f_ps = ps("f_ps", [P, 2, BANK])
        x_ps = ps("x_ps", [P, 2, BANK])
        x_flat = x_ps[:, :, :].rearrange("p a b -> p (a b)")

        groups = [(EARLY_TILES, 1), (EARLY_TILES + 1, 1)] + [(m, 2) for m in range(EARLY_TILES + 2, MT, 2)]
        tiles_in = [sem(f"tiles_landed{i}") for i in range(len(groups))]
        group_of = {first + i: n for n, (first, tiles) in enumerate(groups) for i in range(tiles)}
        b1_in = sem("b1_in")
        x_in = sem("x1_landed")
        res_in = sem("res_landed")
        gate_in = sem("gate_landed")
        out_done = sem("out_done")
        w_hi_made = sem("w12_hi_made")
        w_split = sem("w12_split")
        x_squared = sem("x1_squared")
        x_guarded = sem("x1_guarded")
        x_rnorm = sem("x1_rnorm")
        x_dup = sem("x1_dup")
        x_scaled = sem("x1_scaled")
        x_t = sem("x1_t")
        h_made = sem("h2_made")
        h_hi_made = sem("h2_hi_made")
        h_split = sem("h2_split")
        f_done = sem("f_done")
        gelu_done = sem("gelu_done")
        act_hi_made = sem("act_hi_made")
        act_split = sem("act_split")
        z_step = sem("z_step")
        gated = sem("mlp_gated")
        summed = sem("mlp_summed")

        def run_pairs(eng, pair):
            pair(0, True, False)
            with eng.Fori(1, PAIRS - 1) as p:
                pair(p, False, False)
            pair(PAIRS - 1, False, True)

        SQUARE_AT, TRANSPOSE_AT, MODULATE_AT = (2, 9), (5, 12), (6, 13)

        block = ctx.enter_context(nc.Block())

        @block.sync
        def _(sp):
            def load_x(b):
                sp.dma_start(xin[:, 0:D], x1_d[bass.ds(b, 1), :, :].rearrange("a t d -> (a t) d")).then_inc(x_in, 16)

            def load_rows(p):
                if not isinstance(p, int) or p >= 1:
                    sp.wait_ge(out_done, 32 * p)
                for i in range(2):
                    sp.dma_start(res[:, i, :], x1g_d[bass.ds(2 * p + i, 1), :, :].rearrange("a t d -> (a t) d")
                                 ).then_inc(res_in, 16)
                    sp.dma_start(gate[:, i, :], gate2_d[bass.ds(2 * p + i, 1), :].partition_broadcast(P)
                                 ).then_inc(gate_in, 16)

            for n, (m, tiles) in enumerate(groups):
                load_mlp_tiles(sp, other_tiles, m - EARLY_TILES, m, tiles, fc1_wt, fc2_wt, tiles_in[n])
                if n == 0:
                    sp.dma_start(fc1_b[:, :], fc1_bt).then_inc(b1_in, 16)
                if n == 3:
                    load_x(2)
            load_rows(0)

            def pair(p, ahead):
                for i in ahead:
                    sp.wait_ge(x_t, 2 * p + i - 2)
                    load_x(2 * p + i)
                for i in range(2):
                    sp.wait_ge(summed, 2 * p + 1 + i)
                    sp.dma_start(out[bass.ds(2 * p + i, 1), :, :].rearrange("a t d -> (a t) d"), res[:, i, :]
                                 ).then_inc(out_done, 16)
                if ahead:
                    load_rows(p + 1)

            pair(0, (3, 4))
            with sp.Fori(1, PAIRS - 2) as p:
                pair(p, (3, 4))
            pair(PAIRS - 2, (3,))
            pair(PAIRS - 1, ())
            sp.wait_ge(out_done, 32 * PAIRS)

        @block.tensor
        def _(pe):
            def x_transposed(b):
                pe.wait_ge(x_scaled, b - 1)
                if not isinstance(b, int) or b >= 3:
                    pe.wait_ge(h_made, KT * (b - 2))
                for k in range(KT):
                    last = nc.tensor.transpose(x_flat[:, k * P:(k + 1) * P], xin[:, k * P:(k + 1) * P], ident[:, :])
                last.then_inc(x_t, 1)

            hi_passes = [(0, h_hi, k) for k in range(KF)] + [(1, h_hi, k) for k in range(KF)] + [(2, h_hi, KF)]
            lo_passes = [(0, h_lo, k) for k in range(KF)] + [(2, h_lo, KF)]
            passes = hi_passes + lo_passes

            def fc1(p, m):
                weights, at = tile_at(m)
                for n, (w, a, k) in enumerate(passes):
                    if m == 0 and n == len(hi_passes) and not (isinstance(p, int) and p == 0):
                        pe.wait_ge(h_split, p)
                    ins = nc.tensor.matmul(f_ps[:, m % 2, 0:2 * T], weights[w][:, at, :] if k == KF else weights[w][:, at, k, :],
                                           a[:, k, :, :], start=(n == 0), stop=(n == len(passes) - 1))
                ins.then_inc(f_done, 1)

            def fc2(m):
                (_, _, _, w2_hi, w2_lo, *_), at = tile_at(m)
                for i in range(2):
                    tok = slice(i * T, (i + 1) * T)
                    for n, (a, w) in enumerate(((act_hi, w2_hi), (act_hi, w2_lo), (act_lo, w2_hi))):
                        for c in range(2):
                            ins = nc.tensor.matmul(z_ps[:, i, c, 0:NH], a[:, m % 2, tok], w[:, at, c * NH:(c + 1) * NH],
                                                   start=(m == 0 and n == 0), stop=(m == MT - 1 and n == 2))
                ins.then_inc(z_step, 1)

            def pair(p, first, last):
                if not first:
                    pe.wait_ge(h_hi_made, p)
                for m in range(MT + 1):
                    if m < MT:
                        if first and m >= EARLY_TILES:
                            pe.wait_ge(w_split, m - EARLY_TILES + 1)
                        if not (first and m < 2):
                            pe.wait_ge(gelu_done, p * MT + m - 1)
                        fc1(p, m)
                    if m >= 1:
                        if m == 1 and not first:
                            pe.wait_ge(gated, 2 * p)
                        pe.wait_ge(act_split, p * MT + m)
                        fc2(m - 1)
                    if not last:
                        for i in range(2):
                            if m == TRANSPOSE_AT[i]:
                                x_transposed(2 * p + 2 + i)

            run_pairs(pe, pair)

        @block.scalar
        def _(act):
            def square_x(b):
                act.wait_ge(x_in, 16 * (b - 1))
                if not isinstance(b, int) or b >= 3:
                    act.wait_ge(x_guarded, b - 2)
                    act.wait_ge(h_made, KT * (b - 2))
                nc.scalar.activation(x_flat[:, 0:D], xin[:, 0:D], ACT.Square, accum_out=xss[:, :]).then_inc(x_squared, 1)

            def modulate(b, i):
                act.wait_ge(x_t, b - 1)
                for k in range(KT):
                    nc.scalar.activation(h[:, k, i, :], x_flat[:, k * P:(k + 1) * P], ACT.Identity,
                                         bias=coef[:, 2, k, bass.ds(b, 1)], scale=coef[:, 3, k, bass.ds(b, 1)]
                                         ).then_inc(h_made, 1)

            def h_hi_of(p):
                act.wait_ge(h_made, p * (2 * KT))
                act.wait_ge(f_done, p * MT)
                nc.scalar.activation(h_hi[:, :, :, :], h[:, :, :, :], ACT.Copy).then_inc(h_hi_made, 1)

            def w_hi(m):
                act.wait_ge(tiles_in[group_of[m]], 16 * (groups[group_of[m]][1] + 3))
                if m >= EARLY_TILES + 2:
                    act.wait_ge(w_split, m - EARLY_TILES - 1)
                weights, at = tile_at(m)
                mlp_tile_hi(nc, weights, at, tail_hi[:, m % 2, :], w_hi_made)

            act.wait_ge(b1_in, 16)

            def pair(p, first, last):
                for m in range(MT):
                    act.wait_ge(f_done, p * MT + m + 1)
                    if not (first and m == 0):
                        act.wait_ge(act_split, p * MT + m)
                    nc.scalar.activation(act_f[:, :], f_ps[:, m % 2, 0:2 * T], ACT.Gelu_apprx_tanh,
                                         bias=fc1_b[:, m:m + 1]).then_inc(gelu_done, 1)
                    if first and m + EARLY_TILES < MT:
                        w_hi(m + EARLY_TILES)
                    if not last:
                        for i in range(2):
                            if m == SQUARE_AT[i]:
                                square_x(2 * p + 2 + i)
                            if m == MODULATE_AT[i]:
                                modulate(2 * p + 2 + i, i)
                if not last:
                    h_hi_of(p + 1)

            run_pairs(act, pair)

        @block.vector
        def _(dve):
            def guard_x(b):
                dve.wait_ge(x_squared, b - 1)
                nc.vector.tensor_scalar(xr[:, 0:1], xss[:, :], EPS2, None, ALU.max).then_inc(x_guarded, 1)

            def scale_x(b):
                dve.wait_ge(x_rnorm, b - 1)
                nc.vector.tensor_scalar(xin[:, D:DX], xin[:, KF * P:D], xr[:, 1:2], None, ALU.mult).then_inc(x_dup, 1)
                dve.wait_ge(x_dup, b - 1)
                nc.vector.tensor_scalar(xin[:, 0:D], xin[:, 0:D], xr[:, 1:2], None, ALU.mult).then_inc(x_scaled, 1)

            def h_lo_of(p):
                dve.wait_ge(h_hi_made, p)
                nc.vector.tensor_tensor(h_lo[:, :, :, :], h[:, :, :, :], h_hi[:, :, :, :].bitcast(F32), ALU.subtract
                                        ).then_inc(h_split, 1)

            def w_lo(m):
                dve.wait_ge(w_hi_made, m - EARLY_TILES + 1)
                weights, at = tile_at(m)
                mlp_tile_lo(nc, weights, at, tail_hi[:, m % 2, :], w_split)

            def pair(p, first, last):
                for m in range(MT):
                    if not (first and m < 2):
                        dve.wait_ge(z_step, p * MT + m - 1)
                    dve.wait_ge(gelu_done, p * MT + m + 1)
                    nc.vector.tensor_copy(act_hi[:, m % 2, :], act_f[:, :]).then_inc(act_hi_made, 1)
                    dve.wait_ge(act_hi_made, p * MT + m + 1)
                    nc.vector.tensor_tensor(act_lo[:, m % 2, :], act_f[:, :], act_hi[:, m % 2, :].bitcast(F32),
                                            ALU.subtract).then_inc(act_split, 1)
                    if first and m + EARLY_TILES < MT:
                        w_lo(m + EARLY_TILES)
                    if not last:
                        for i in range(2):
                            if m == SQUARE_AT[i]:
                                guard_x(2 * p + 2 + i)
                            if m == SQUARE_AT[i] + 1:
                                scale_x(2 * p + 2 + i)
                if not last:
                    h_lo_of(p + 1)
                dve.wait_ge(z_step, p * MT + MT)
                for i in range(2):
                    dve.wait_ge(gate_in, 32 * p + 32)
                    nc.vector.tensor_tensor(gate[:, i, :].rearrange("p (a b) -> p a b", a=2), z_ps[:, i, :, 0:NH],
                                            gate[:, i, :].rearrange("p (a b) -> p a b", a=2), ALU.mult
                                            ).then_inc(gated, 1)

            run_pairs(dve, pair)

        @block.gpsimd
        def _(pool):
            def x_rnorm_of(b):
                pool.wait_ge(x_guarded, b - 1)
                nc.gpsimd.tensor_tensor(xr[:, 1:2], xr[:, 0:1], minus_half[:, 0:1], ALU.pow).then_inc(x_rnorm, 1)

            def pair(p, first, last):
                if not last:
                    x_rnorm_of(2 * p + 2)
                    x_rnorm_of(2 * p + 3)
                for i in range(2):
                    pool.wait_ge(gated, 2 * p + 1 + i)
                    pool.wait_ge(res_in, 32 * p + 32)
                    nc.gpsimd.tensor_tensor(res[:, i, :], res[:, i, :], gate[:, i, :], ALU.add).then_inc(summed, 1)

            run_pairs(pool, pair)


def kernel(**inputs):
    import numpy as np
    import concourse.bacc as bacc
    from concourse import mybir as mb
    from concourse.bass_utils import run_bass_kernel_spmd

    def rows(name):
        return np.asarray(inputs[name]).reshape(1, -1)

    by_unit = lambda a: np.asarray(a).reshape(3, G, HG * HD, -1).transpose(1, 0, 2, 3).reshape(3 * D, -1)
    arrays = {
        "x": np.asarray(inputs["x"]),
        "cond_t": np.asarray(inputs["cond_1152"]).T,
        "g1": rows("L0_cond_g1"), "g2": rows("L0_cond_g2"),
        "qkv_wt": by_unit(inputs["L0_cond_qkv_w"]).T,
        "qkv_b": by_unit(inputs["L0_cond_qkv_b"]).T,
        "qg": rows("L0_cond_qg"), "kg": rows("L0_cond_kg"),
        "proj_wt": np.asarray(inputs["L0_cond_proj_w"]).T, "proj_b": rows("L0_cond_proj_b"),
        "fc1_wt": np.asarray(inputs["L0_cond_fc1_w"]).T,
        "fc1_bt": np.asarray(inputs["L0_cond_fc1_b"]).reshape(MT, P).T,
        "fc2_wt": np.asarray(inputs["L0_cond_fc2_w"]).T, "fc2_b": rows("L0_cond_fc2_b"),
        "ada_wt": np.asarray(inputs["L0_cond_ada_w"]).T, "ada_b": rows("L0_cond_ada_b"),
    }
    arrays = {name: np.ascontiguousarray(a) for name, a in arrays.items()}
    nc = bacc.Bacc("TRN2", target_bir_lowering=False, num_devices=1)
    args = {name: nc.dram_tensor(name + "_dram", a.shape, mb.dt.from_np(a.dtype), kind="ExternalInput").ap()
            for name, a in arrays.items()}
    out = nc.dram_tensor("out_dram", (B, T, D), mb.dt.float32, kind="ExternalOutput").ap()
    build(nc, out=out, **args)
    ran = run_bass_kernel_spmd(nc, [{name + "_dram": a for name, a in arrays.items()}], core_ids=[0])
    return ran.results[0]["out_dram"]
```
